# Optimizing a Trainium2 kernel written in Bass

```python
import numpy as np
import jax
import jax.numpy as jnp

def _softmax(x, axis=-1):
    return jax.nn.softmax(x, axis=axis)

def _gelu(x):
    return jax.nn.gelu(x, approximate=True)

def _silu(x):
    return jax.nn.silu(x)

def _sigmoid(x):
    return jax.nn.sigmoid(x)

def _layernorm(x, axis=-1, eps=1e-05):
    m = jnp.mean(x, axis=axis, keepdims=True)
    v = jnp.var(x, axis=axis, keepdims=True)
    return (x - m) / jnp.sqrt(v + eps)

def _scatter_add(tgt, idx, src, axis=0):
    return tgt.at[idx].add(src)

def _segment_sum(src, seg, n):
    return jax.ops.segment_sum(src, seg, n)
kernel_name = 'mk_gnn_preln_d4_gnn_r32_6e287a'

def setup_inputs(seed: int=0):
    np.random.seed(seed)
    _w = jnp.asarray

    def _rec_inputs():
        import jax
        import jax.numpy as jnp
        _gk = jax.random.key(seed)
        x = -0.0006008 + 1.001 * jax.random.normal(jax.random.fold_in(_gk, 1), (3125, 256), jnp.float32)
        src = jax.random.randint(jax.random.fold_in(_gk, 2), (50000,), 0, 3125, jnp.int32)
        dst = jnp.minimum((3125 * jax.random.uniform(jax.random.fold_in(_gk, 3), (50000,)) ** 2.0).astype(jnp.int32), 99999)
        _o = jnp.argsort(dst, stable=True)
        src = src[_o]
        dst = dst[_o]
        edge_attr_64 = jax.random.uniform(jax.random.fold_in(_gk, 11), (50000, 64), jnp.float32, 0.0, 1)
        return (x, src, dst, edge_attr_64)
    x, src, dst, edge_attr_64 = _rec_inputs()

    def _L0_gnn_setup():
        import jax, jax.numpy as jnp
        import numpy as np
        N, E, D = (10000, 10000, 256)

        def _add_self_loops(src, dst, n):
            loop = jnp.arange(n, dtype=src.dtype)
            return (jnp.concatenate([src, loop]), jnp.concatenate([dst, loop]))

        def _gcn_conv(x, W, b, src, dst, n):
            xw = x @ W
            deg = jax.ops.segment_sum(jnp.ones(src.shape[0], x.dtype), dst, num_segments=n)
            dinv = jnp.where(deg > 0, jax.lax.rsqrt(deg), 0.0)
            norm = dinv[src] * dinv[dst]
            agg = jax.ops.segment_sum(xw[src] * norm[:, None], dst, num_segments=n)
            return agg + b

        def _gat_conv(x, W, a_src, a_dst, b, src, dst, n):
            xw = x @ W
            e = jax.nn.leaky_relu((xw @ a_src)[src] + (xw @ a_dst)[dst], 0.2)
            m = jax.ops.segment_max(e, dst, num_segments=n)
            ex = jnp.exp(e - m[dst])
            s = jax.ops.segment_sum(ex, dst, num_segments=n)
            alpha = ex / (s[dst] + 1e-16)
            agg = jax.ops.segment_sum(alpha[:, None] * xw[src], dst, num_segments=n)
            return agg + b
        key = jax.random.key(seed)
        ks = jax.random.split(key, 6)
        return {'event_emb': jax.random.normal(ks[0], (N, D), jnp.float32), 'edge_index': jax.random.randint(ks[1], (2, E), 0, N), 'W1': jax.random.normal(ks[2], (D, D), jnp.float32) / np.sqrt(D).astype(np.float32), 'b1': jnp.zeros((D,), jnp.float32), 'W2': jax.random.normal(ks[3], (D, D), jnp.float32) / np.sqrt(D).astype(np.float32), 'att_src': jax.random.normal(ks[4], (D,), jnp.float32) / np.sqrt(D).astype(np.float32), 'att_dst': jax.random.normal(ks[5], (D,), jnp.float32) / np.sqrt(D).astype(np.float32), 'b2': jnp.zeros((D,), jnp.float32)}
    _L0_gnn_all = _L0_gnn_setup()
    _L0_gnn_in = {k: v for k, v in _L0_gnn_all.items() if k in ('W1', 'b1', 'W2', 'att_src', 'att_dst', 'b2')}
    del _L0_gnn_all

    def _L1_gnn_setup():
        import jax, jax.numpy as jnp
        import numpy as np
        N, E, HID, NRBF = (10000, 10000, 256, 64)
        key = jax.random.key(seed)
        ks = jax.random.split(key, 12)

        def lin(k, fin, fout):
            bound = 1.0 / np.sqrt(fin)
            kw, kb = jax.random.split(k)
            W = jax.random.uniform(kw, (fin, fout), jnp.float32, -bound, bound)
            b = jax.random.uniform(kb, (fout,), jnp.float32, -bound, bound)
            return (W, b)
        W1, b1 = lin(ks[0], NRBF, HID)
        W2, b2 = lin(ks[1], HID, HID)
        U1, c1 = lin(ks[2], 2 * HID, HID)
        U2, c2 = lin(ks[3], HID, HID)
        h = jax.random.normal(ks[4], (N, HID), jnp.float32)
        edge_index = jax.random.randint(ks[5], (2, E), 0, N, jnp.int64)
        rbf = jax.random.uniform(ks[6], (E, NRBF), jnp.float32)
        return {'h': h, 'edge_index': edge_index, 'rbf': rbf, 'W1': W1, 'b1': b1, 'W2': W2, 'b2': b2, 'U1': U1, 'c1': c1, 'U2': U2, 'c2': c2}
    _L1_gnn_all = _L1_gnn_setup()
    _L1_gnn_in = {k: v for k, v in _L1_gnn_all.items() if k in ('W1', 'b1', 'W2', 'b2', 'U1', 'c1', 'U2', 'c2')}
    del _L1_gnn_all

    def _L2_gnn_setup():
        import jax, jax.numpy as jnp
        import numpy as np
        N_NODES = 10000
        N_EDGES = 10000
        IN_DIM = 256
        OUT_DIM = 256
        LN_EPS = 1e-05
        key = jax.random.key(seed)
        ks = jax.random.split(key, 4)
        x = jax.random.normal(ks[0], (N_NODES, IN_DIM), dtype=jnp.float32)
        edge_index = jax.random.randint(ks[1], (2, N_EDGES), 0, N_NODES, dtype=jnp.int64)
        W_msg = jax.random.normal(ks[2], (2 * IN_DIM, OUT_DIM), dtype=jnp.float32) / np.sqrt(2 * IN_DIM)
        b_msg = jnp.zeros((OUT_DIM,), dtype=jnp.float32)
        W_upd = jax.random.normal(ks[3], (IN_DIM + OUT_DIM, OUT_DIM), dtype=jnp.float32) / np.sqrt(IN_DIM + OUT_DIM)
        b_upd = jnp.zeros((OUT_DIM,), dtype=jnp.float32)
        gamma = jnp.ones((OUT_DIM,), dtype=jnp.float32)
        beta = jnp.zeros((OUT_DIM,), dtype=jnp.float32)
        return {'x': x, 'edge_index': edge_index, 'W_msg': W_msg, 'b_msg': b_msg, 'W_upd': W_upd, 'b_upd': b_upd, 'gamma': gamma, 'beta': beta}
    _L2_gnn_all = _L2_gnn_setup()
    _L2_gnn_in = {k: v for k, v in _L2_gnn_all.items() if k in ('W_msg', 'b_msg', 'W_upd', 'b_upd', 'gamma', 'beta')}
    del _L2_gnn_all

    def _L3_gnn_setup():
        import jax, jax.numpy as jnp
        import numpy as np
        N, E = (50000, 25000)
        IN_DIM, HEADS, OUT_DIM = (256, 8, 32)
        NEG_SLOPE = 0.2
        LN_EPS = 1e-05
        key = jax.random.key(seed)
        ks = jax.random.split(key, 8)
        HC = HEADS * OUT_DIM
        x = jax.random.normal(ks[0], (N, IN_DIM), dtype=jnp.float32)
        edge_index = jax.random.randint(ks[1], (2, E), 0, N, dtype=jnp.int32)
        W = jax.random.normal(ks[2], (IN_DIM, HC), dtype=jnp.float32) / np.sqrt(IN_DIM)
        att_src = jax.random.normal(ks[3], (HEADS, OUT_DIM), dtype=jnp.float32) / np.sqrt(OUT_DIM)
        att_dst = jax.random.normal(ks[4], (HEADS, OUT_DIM), dtype=jnp.float32) / np.sqrt(OUT_DIM)
        bias = jnp.zeros((HC,), dtype=jnp.float32)
        ln_gamma = jnp.ones((HC,), dtype=jnp.float32)
        ln_beta = jnp.zeros((HC,), dtype=jnp.float32)
        return {'x': x, 'edge_index': edge_index, 'W': W, 'att_src': att_src, 'att_dst': att_dst, 'bias': bias, 'ln_gamma': ln_gamma, 'ln_beta': ln_beta}
    _L3_gnn_all = _L3_gnn_setup()
    _L3_gnn_in = {k: v for k, v in _L3_gnn_all.items() if k in ('W', 'att_src', 'att_dst', 'bias', 'ln_gamma', 'ln_beta')}
    del _L3_gnn_all
    return {'x': x, 'src': src, 'dst': dst, 'edge_attr_64': edge_attr_64, 'L0_gnn_W1': _L0_gnn_in['W1'], 'L0_gnn_b1': _L0_gnn_in['b1'], 'L0_gnn_W2': _L0_gnn_in['W2'], 'L0_gnn_att_src': _L0_gnn_in['att_src'], 'L0_gnn_att_dst': _L0_gnn_in['att_dst'], 'L0_gnn_b2': _L0_gnn_in['b2'], 'L1_gnn_W1': _L1_gnn_in['W1'], 'L1_gnn_b1': _L1_gnn_in['b1'], 'L1_gnn_W2': _L1_gnn_in['W2'], 'L1_gnn_b2': _L1_gnn_in['b2'], 'L1_gnn_U1': _L1_gnn_in['U1'], 'L1_gnn_c1': _L1_gnn_in['c1'], 'L1_gnn_U2': _L1_gnn_in['U2'], 'L1_gnn_c2': _L1_gnn_in['c2'], 'L2_gnn_W_msg': _L2_gnn_in['W_msg'], 'L2_gnn_b_msg': _L2_gnn_in['b_msg'], 'L2_gnn_W_upd': _L2_gnn_in['W_upd'], 'L2_gnn_b_upd': _L2_gnn_in['b_upd'], 'L2_gnn_gamma': _L2_gnn_in['gamma'], 'L2_gnn_beta': _L2_gnn_in['beta'], 'L3_gnn_W': _L3_gnn_in['W'], 'L3_gnn_att_src': _L3_gnn_in['att_src'], 'L3_gnn_att_dst': _L3_gnn_in['att_dst'], 'L3_gnn_bias': _L3_gnn_in['bias'], 'L3_gnn_ln_gamma': _L3_gnn_in['ln_gamma'], 'L3_gnn_ln_beta': _L3_gnn_in['ln_beta']}

def reference(x, src, dst, edge_attr_64, L0_gnn_W1, L0_gnn_b1, L0_gnn_W2, L0_gnn_att_src, L0_gnn_att_dst, L0_gnn_b2, L1_gnn_W1, L1_gnn_b1, L1_gnn_W2, L1_gnn_b2, L1_gnn_U1, L1_gnn_c1, L1_gnn_U2, L1_gnn_c2, L2_gnn_W_msg, L2_gnn_b_msg, L2_gnn_W_upd, L2_gnn_b_upd, L2_gnn_gamma, L2_gnn_beta, L3_gnn_W, L3_gnn_att_src, L3_gnn_att_dst, L3_gnn_bias, L3_gnn_ln_gamma, L3_gnn_ln_beta):
    import jax
    import jax.numpy as jnp

    def _L0_gnn_ref(event_emb, edge_index, W1, b1, W2, att_src, att_dst, b2):
        import jax, jax.numpy as jnp
        import numpy as np
        N, E, D = (10000, 10000, 256)

        def _add_self_loops(src, dst, n):
            loop = jnp.arange(n, dtype=src.dtype)
            return (jnp.concatenate([src, loop]), jnp.concatenate([dst, loop]))

        def _gcn_conv(x, W, b, src, dst, n):
            xw = x @ W
            deg = jax.ops.segment_sum(jnp.ones(src.shape[0], x.dtype), dst, num_segments=n)
            dinv = jnp.where(deg > 0, jax.lax.rsqrt(deg), 0.0)
            norm = dinv[src] * dinv[dst]
            agg = jax.ops.segment_sum(xw[src] * norm[:, None], dst, num_segments=n)
            return agg + b

        def _gat_conv(x, W, a_src, a_dst, b, src, dst, n):
            xw = x @ W
            e = jax.nn.leaky_relu((xw @ a_src)[src] + (xw @ a_dst)[dst], 0.2)
            m = jax.ops.segment_max(e, dst, num_segments=n)
            ex = jnp.exp(e - m[dst])
            s = jax.ops.segment_sum(ex, dst, num_segments=n)
            alpha = ex / (s[dst] + 1e-16)
            agg = jax.ops.segment_sum(alpha[:, None] * xw[src], dst, num_segments=n)
            return agg + b
        n = event_emb.shape[0]
        src, dst = _add_self_loops(edge_index[0], edge_index[1], n)
        x = jax.nn.relu(_gcn_conv(event_emb, W1, b1, src, dst, n))
        x = jax.nn.relu(_gat_conv(x, W2, att_src, att_dst, b2, src, dst, n))
        return x

    def _L1_gnn_ref(h, edge_index, rbf, W1, b1, W2, b2, U1, c1, U2, c2):
        import jax, jax.numpy as jnp
        import numpy as np
        N, E, HID, NRBF = (10000, 10000, 256, 64)
        src, dst = (edge_index[0], edge_index[1])
        gate = jax.nn.sigmoid(jax.nn.silu(rbf @ W1 + b1) @ W2 + b2)
        msg = gate * h[src]
        aggr = jax.ops.segment_sum(msg, dst, num_segments=h.shape[0])
        upd = jax.nn.silu(jnp.concatenate([h, aggr], axis=-1) @ U1 + c1) @ U2 + c2
        return h + upd

    def _L2_gnn_ref(x, edge_index, W_msg, b_msg, W_upd, b_upd, gamma, beta):
        import jax, jax.numpy as jnp
        import numpy as np
        N_NODES = 10000
        N_EDGES = 10000
        IN_DIM = 256
        OUT_DIM = 256
        LN_EPS = 1e-05
        row, col = (edge_index[0], edge_index[1])
        msg_in = jnp.concatenate([x[row], x[col]], axis=-1)
        messages = jax.nn.relu(msg_in @ W_msg + b_msg)
        aggregated = jax.ops.segment_sum(messages, col, num_segments=x.shape[0])
        h = jax.nn.relu(jnp.concatenate([x, aggregated], axis=-1) @ W_upd + b_upd)
        mu = jnp.mean(h, axis=-1, keepdims=True)
        var = jnp.mean(jnp.square(h - mu), axis=-1, keepdims=True)
        return (h - mu) * jax.lax.rsqrt(var + LN_EPS) * gamma + beta

    def _L3_gnn_ref(x, edge_index, W, att_src, att_dst, bias, ln_gamma, ln_beta):
        import jax, jax.numpy as jnp
        import numpy as np
        N, E = (50000, 25000)
        IN_DIM, HEADS, OUT_DIM = (256, 8, 32)
        NEG_SLOPE = 0.2
        LN_EPS = 1e-05
        n = x.shape[0]
        loop = jnp.arange(n, dtype=edge_index.dtype)
        src = jnp.concatenate([edge_index[0], loop])
        dst = jnp.concatenate([edge_index[1], loop])
        h = (x @ W).reshape(n, HEADS, OUT_DIM)
        a_src = jnp.einsum('nhc,hc->nh', h, att_src)
        a_dst = jnp.einsum('nhc,hc->nh', h, att_dst)
        e = jax.nn.leaky_relu(a_src[src] + a_dst[dst], NEG_SLOPE)
        m = jax.ops.segment_max(e, dst, num_segments=n)
        e = jnp.exp(e - m[dst])
        denom = jax.ops.segment_sum(e, dst, num_segments=n)
        alpha = e / (denom[dst] + 1e-16)
        out = jax.ops.segment_sum(h[src] * alpha[:, :, None], dst, num_segments=n)
        out = out.reshape(n, HEADS * OUT_DIM) + bias
        mu = jnp.mean(out, axis=-1, keepdims=True)
        var = jnp.mean(jnp.square(out - mu), axis=-1, keepdims=True)
        return ln_gamma * (out - mu) * jax.lax.rsqrt(var + LN_EPS) + ln_beta
    edge_index = jnp.stack([src, dst])
    h = jnp.maximum(_layernorm(x, axis=-1), 0.0)
    x = x + _L0_gnn_ref(h, edge_index, L0_gnn_W1, L0_gnn_b1, L0_gnn_W2, L0_gnn_att_src, L0_gnn_att_dst, L0_gnn_b2)
    h = jnp.maximum(_layernorm(x, axis=-1), 0.0)
    x = x + _L1_gnn_ref(h, edge_index, edge_attr_64, L1_gnn_W1, L1_gnn_b1, L1_gnn_W2, L1_gnn_b2, L1_gnn_U1, L1_gnn_c1, L1_gnn_U2, L1_gnn_c2)
    h = jnp.maximum(_layernorm(x, axis=-1), 0.0)
    x = x + _L2_gnn_ref(h, edge_index, L2_gnn_W_msg, L2_gnn_b_msg, L2_gnn_W_upd, L2_gnn_b_upd, L2_gnn_gamma, L2_gnn_beta)
    h = jnp.maximum(_layernorm(x, axis=-1), 0.0)
    x = x + _L3_gnn_ref(h, edge_index, L3_gnn_W, L3_gnn_att_src, L3_gnn_att_dst, L3_gnn_bias, L3_gnn_ln_gamma, L3_gnn_ln_beta)
    return x

_drawn_inputs = setup_inputs


def setup_inputs(seed=0):
    import zlib

    import numpy as np

    out = dict(_drawn_inputs(seed))
    spreads = {'L0_gnn_b1': (0.0, 0.1),
     'L0_gnn_b2': (0.0, 0.1),
     'L2_gnn_b_msg': (0.0, 0.1),
     'L2_gnn_b_upd': (0.0, 0.377),
     'L2_gnn_gamma': (1.0, 0.2),
     'L2_gnn_beta': (0.0, 0.1),
     'L3_gnn_bias': (0.0, 0.1),
     'L3_gnn_ln_gamma': (1.0, 0.2),
     'L3_gnn_ln_beta': (0.0, 0.1)}
    factors = {'edge_attr_64': 8.0,
     'L0_gnn_att_src': 6.37,
     'L0_gnn_att_dst': 24.439,
     'L1_gnn_W1': 3.261,
     'L1_gnn_b1': 8.0,
     'L1_gnn_W2': 2.955,
     'L1_gnn_b2': 36.024,
     'L1_gnn_c1': 8.0,
     'L1_gnn_c2': 3.004,
     'L3_gnn_att_dst': 2.676}
    for name, (base, spread) in spreads.items():
        noise = np.random.default_rng([zlib.crc32(name.encode()), seed]).standard_normal(out[name].shape)
        drawn = base * np.exp(spread * noise) if base else spread * noise
        out[name] = jnp.asarray(drawn.astype(out[name].dtype))
    for name, factor in factors.items():
        out[name] = (out[name] * factor).astype(out[name].dtype)
    return out
```

```python
import concourse.bass as bass
from concourse import mybir
from concourse.alu_op_type import AluOpType as ALU
from contextlib import ExitStack, contextmanager

FP32 = mybir.dt.float32
BF16 = mybir.dt.bfloat16
I32 = mybir.dt.int32
ACT = mybir.ActivationFunctionType
X_AXIS = mybir.AxisListType.X

P = 128
N = 3125
E = 50000
D = 256
HEADS = 8
RBF = 64
REAL_TILES = -(-N // P)
NT = REAL_TILES + 1
PAIRS = NT // 2
GROUP = 8
ROUND = 2 * GROUP
STEPS = -(-(E // P + REAL_TILES) // ROUND) * ROUND
ROUNDS = STEPS // ROUND
LIVE = 4
GROUPS = STEPS // GROUP
TURNS = GROUPS // LIVE
QS = 4
ROWS = STEPS // QS
ECOLS = -(-E // P)
EQR = -(-ECOLS // QS)
EC = EQR * QS
EW = EC + ECOLS + 1
HB = 7
HROUNDS = EC // (2 * HB)
PAD_DST = 4000
CODE = 4096
TW = D + HEADS
GW = D + 2 * HEADS
BIG = 3.0e38
LOW = -1.0e30
EPS = 1e-5
SLOPE = 0.2


class Ordered:

    def __init__(self, engine, semaphore):
        self.engine, self.semaphore, self.base, self.n = engine, semaphore, 0, 0

    def done(self, instruction):
        instruction.then_inc(self.semaphore, 1)
        self.n += 1
        self.engine.wait_ge(self.semaphore, self.base + self.n)

    def start(self, instruction):
        instruction.then_inc(self.semaphore, 1)
        self.n += 1

    @contextmanager
    def loop(self, low, high, per):
        start = self.base + self.n
        with self.engine.Fori(low, high) as it:
            self.base, self.n = start + (it - low) * per, 0
            yield it
            assert self.n == per, (self.n, per)
        self.base, self.n = start + (high - low) * per, 0


def gnn_four_layers(nc, x, src, dst, edge_attr, g1_w, g1_b, g2_w, g2_as, g2_ad, g2_b,
                    e_w1, e_b1, e_w2, e_b2, e_u1, e_c1, e_u2, e_c2,
                    m_w, m_b, m_wu, m_bu, m_gamma, m_beta,
                    a_w, a_as, a_ad, a_b, a_gamma, a_beta, out):
    ctx = ExitStack()
    with ctx:
        def sb(name, shape, dt=FP32):
            return ctx.enter_context(nc.sbuf_tensor(name, shape, dt))

        def sem(name):
            return ctx.enter_context(nc.semaphore(name))

        def dram(name, shape, dt=FP32):
            return nc.dram_tensor(name, shape, dt).ap()

        step_table = dram("step_table", (2, STEPS), I32)
        slot_rows = dram("slot_rows", (STEPS * P + 1,))
        reset_rows = dram("reset_rows", (STEPS * P + P,))
        rbf_pad = dram("rbf_pad", (E + P, RBF))
        table_gcn = dram("table_gcn", (NT * P, D))
        table_gat = dram("table_gat", (NT * P, D + 1))
        table_gate = dram("table_gate", (NT * P, D))
        table_msg = dram("table_msg", (NT * P, D))
        table_heads = dram("table_heads", (NT * P, TW))

        X = sb("X", [P, NT, D])
        acc = sb("acc", [P, NT, GW])
        H = sb("H", [P, NT, TW])
        HT = sb("HT", [P, NT, 2, P])
        Q = sb("Q", [P, NT * D])
        G = sb("G", [P, ROUND, GW])
        onehot = sb("onehot", [P, ROUND, P])
        pair_space = sb("pair_space", [P, 4 * D])
        rows = pair_space[:, 0:2 * D].rearrange("p (k d) -> p k d", k=2)
        HTs = pair_space[:, 2 * D:4 * D].rearrange("p (a b n) -> p a b n", a=2, b=2)
        w_a = sb("w_a", [P, 4, D])
        w_b = sb("w_b", [P, 2, D])
        w_c = sb("w_c", [P, 2, D + 2])
        w_heads = sb("w_heads", [P, 2, GW])
        w_msg = sb("w_msg", [P, 2, 2 * D])
        w_rbf = sb("w_rbf", [RBF, D])
        b_gcn = sb("b_gcn", [P, D])
        b_gat = sb("b_gat", [P, D])
        b_msg = sb("b_msg", [P, D])
        b_heads = sb("b_heads", [P, D])
        b_add = sb("b_add", [P, D])
        gam_msg = sb("gam_msg", [P, D])
        gam_heads = sb("gam_heads", [P, D])
        b_rbf = sb("b_rbf", [P, 2])
        b_u1 = sb("b_u1", [P, 2])
        row_upd = sb("row_upd", [1, D])
        part_gate = sb("part_gate", [1, 3, D], BF16)
        parts_gate = sb("parts_gate", [3, D], BF16)
        ones_bf = sb("ones_bf", [3, P], BF16)
        ident = sb("ident", [P, P])
        ones = sb("ones", [P, P])
        iota_row = sb("iota_row", [P, P])
        iota_bf = sb("iota_bf", [P, P], BF16)
        srcI = sb("srcI", [P, STEPS], I32)
        dloc = sb("dloc", [P, STEPS])
        first = sb("first", [P, STEPS])
        step_row = sb("step_row", [1, 2, STEPS], I32)
        idx = sb("idx", [P, LIVE * GROUP], I32)
        tb = sb("tb", [P, 12, NT])
        tile_i = sb("tile_i", [P, 4, NT], I32)
        nd = sb("nd", [P, NT, 2 * HEADS])
        w_self = sb("w_self", [P, NT, HEADS])
        den = sb("den", [P, NT, HEADS])
        dinv = sb("dinv", [P, NT])
        lonely = sb("lonely", [P, NT])
        stats = sb("stats", [P, NT, 6])
        mean2 = sb("mean2", [P, NT])
        gap = sb("gap", [P, NT])
        var = sb("var", [P, NT])
        rstd = sb("rstd", [P, NT])
        nmr = sb("nmr", [P, NT])
        att = sb("att", [P, 640])
        edge_pad = sb("edge_pad", [1, P])
        step_i = sb("step_i", [ROWS, QS], I32)
        step_f = sb("step_f", [ROWS, 4, QS])
        step_out = sb("step_out", [ROWS, 2, QS], I32)

        PS = ctx.enter_context(nc.psum_tensor("psum", [P, 8, 512], FP32))
        banks = [PS[:, i, :] for i in range(8)]

        E_col = Q[:, 0:EW]
        slots = Q[:, 800:800 + EC + STEPS]
        code_rows = Q[0:EQR, 1700:1700 + QS * P].rearrange("p (q e) -> p q e", q=QS)
        dst_f = Q[0:EQR, 2300:2300 + QS * P].rearrange("p (q e) -> p q e", q=QS)
        src_f = Q[0:EQR, 2900:2900 + QS * P].rearrange("p (q e) -> p q e", q=QS)
        lo_f = Q[:, 3500:3500 + EC]
        hi_f = Q[:, 3900:3900 + EC]
        tmp_a = Q[:, 4300:4300 + STEPS]
        tmp_b = Q[:, 4720:4720 + STEPS]
        seg_rows = Q[0:ROWS, 5140:5140 + QS * P].rearrange("p (q e) -> p q e", q=QS)
        prev_rows = Q[0:ROWS, 5660:5660 + QS * P].rearrange("p (q e) -> p q e", q=QS)
        Hf = H[:, :, :].rearrange("p t c -> p (t c)")
        dst_i = Hf[0:EQR, 0:512].bitcast(I32).rearrange("p (q e) -> p q e", q=QS)
        src_i = Hf[0:EQR, 512:1024].bitcast(I32).rearrange("p (q e) -> p q e", q=QS)
        col_i = Hf[:, 1024:1024 + EC].bitcast(I32)
        col_j = Hf[:, 1420:1420 + EC].bitcast(I32)
        slot_i = Hf[:, 1820:1820 + STEPS].bitcast(I32)
        jB = Hf[:, 2240:2240 + STEPS].bitcast(I32)
        oh_lo = Hf[:, 2660:2660 + HB * P].bitcast(BF16).rearrange("p (b c n) -> p b c n", b=2, c=HB)
        oh_hi = Hf[:, 3556:3556 + HB * NT].bitcast(BF16).rearrange("p (b c n) -> p b c n", b=2, c=HB)
        indic = Hf[0:ROWS, 3740:3740 + 2 * QS * NT].rearrange("p (a q n) -> p a q n", a=2, q=QS)
        shift = Hf[:, 3948:3948 + 4 * P].rearrange("p (k a n) -> p k a n", k=2, a=2)
        diff = Hf[:, 4460:4460 + P]
        att_vec = Hf[:, 4588:4588 + 4 * D].rearrange("p (v d) -> p v d", v=4)
        att_tmp = Hf[:, 5612:5612 + D]
        row_gate = Hf[0:1, 5868:5868 + 3 * D].rearrange("p (v d) -> p v d", v=3)

        SG = GROUP * P
        reset_b = [Q[0:HEADS, b * 1028:b * 1028 + SG + 1] for b in range(2)]
        fwd_b = [Q[0:HEADS, 2056 + b * SG:2056 + (b + 1) * SG] for b in range(2)]
        both = Q[0:HEADS, 2056 + 2 * SG:2056 + 3 * SG]
        HTf = HT[:, :, :, :].rearrange("p t b n -> p (t b n)")
        G_more = HTf[:, 0:ROUND * GW].rearrange("p (k c) -> p k c", k=ROUND)
        G_b = [G[:, 0:GROUP, :], G[:, GROUP:ROUND, :], G_more[:, 0:GROUP, :], G_more[:, GROUP:ROUND, :]]
        onehotT_b = [HTf[:, ROUND * GW + b * SG:ROUND * GW + (b + 1) * SG].rearrange("p (k n) -> p k n", k=GROUP)
                     for b in range(2)]
        onehot_b = [onehot[:, 0:GROUP, :], onehot[:, GROUP:ROUND, :],
                    Q[:, 5128:5128 + SG].rearrange("p (k n) -> p k n", k=GROUP),
                    pair_space[:, :].rearrange("p (k n) -> p k n", k=GROUP)]
        rbf_rows = Q[:, 0:ROUND * RBF].rearrange("p (k c) -> p k c", k=ROUND)
        rbf_cols = [Q[0:RBF, 1024 + b * 512:1536 + b * 512] for b in range(2)]
        hidden = [Q[:, 2048 + b * 1024:3072 + b * 1024].rearrange("p (h e) -> p h e", h=2) for b in range(2)]
        gates = [Q[:, 4096 + b * 1024:5120 + b * 1024].rearrange("p (k d) -> p k d", k=4) for b in range(2)]
        onehotT_msg = Hf[:, 0:ROUND * P].rearrange("p (k n) -> p k n", k=ROUND)
        upd_T = Q[:, 0:2 * D].rearrange("p (h n) -> p h n", h=2)

        block = ctx.enter_context(nc.Block())

        pads_set = sem("pads_set")
        consts = sem("consts")
        x_in = sem("x_in")
        edges_in = sem("edges_in")
        weights_in = sem("weights_in")
        rbf_copied = sem("rbf_copied")
        codes = sem("codes")
        codes_T = sem("codes_T")
        hist_oh = sem("hist_oh")
        hist_mm = sem("hist_mm")
        hist_add = sem("hist_add")
        counts = sem("counts")
        totals = sem("totals")
        deg_ready = sem("deg_ready")
        dinv_ready = sem("dinv_ready")
        tiles_known = sem("tiles_known")
        steps_known = sem("steps_known")
        steps_out = sem("steps_out")
        steps_in = sem("steps_in")
        shift_ready = sem("shift_ready")
        shifted = sem("shifted")
        slots_copied = sem("slots_copied")
        slots_ready = sem("slots_ready")
        seg_ready = sem("seg_ready")
        seg_T = sem("seg_T")
        seg_rows_ready = sem("seg_rows_ready")
        seg_stored = sem("seg_stored")
        seg_back = sem("seg_back")
        reset_ready = sem("reset_ready")
        reset_stored = sem("reset_stored")
        first_T = sem("first_T")
        first_ready = sem("first_ready")
        pe_go = sem("pe_go")
        dve_seq = sem("dve_seq")
        pool_seq = sem("pool_seq")
        act_seq = sem("act_seq")
        out_stored = sem("out_stored")

        class Phase:

            def __init__(self, name, after=None, totals=None):
                self.name, self.made, self.totals = name, {}, {}
                if after is not None:
                    self.made = after.made
                    self.totals = {k: totals.get(k, 0) + after.totals.get(k, 0) for k in totals | after.totals}

            def __call__(self, what):
                if what not in self.made:
                    self.made[what] = sem(f"{self.name}_{what}")
                return self.made[what]

            def at(self, what, count):
                return self(what), self.totals.get(what, 0) + count

        norm = {"var": 1, "std": 1, "rstd": 1}
        pair_wise = {"tr": 4 * PAIRS, "ht": PAIRS, "mm": 4 * PAIRS, "row": NT, "stored": 16 * PAIRS}
        n0 = Phase("n0")
        n1 = Phase("n1", n0, norm | {"h": NT, "tr": 4 * PAIRS, "mm": 4 * PAIRS, "out": NT, "stored": 16 * PAIRS})
        n2 = Phase("n2", n1, pair_wise | {"agg": NT, "nd": NT})
        n3 = Phase("n3", n2, norm | {"h": NT, "tr": 4 * PAIRS, "ht": PAIRS, "xrow": NT, "stored": 16 * PAIRS})
        n3b = Phase("n3b", n3, {"agg": PAIRS, "tr": 4 * PAIRS, "ht": PAIRS, "mm": 4 * PAIRS, "out": NT, "w_in": 32})
        n4 = Phase("n4", n3b, norm | pair_wise | {"h": NT, "out": NT})
        n4b = Phase("n4b", n4, norm | {"agg": PAIRS, "tr": 4 * PAIRS, "ht": 2 * PAIRS, "mm": 10 * PAIRS, "row": NT,
                                       "normed": NT, "w_in": 16})
        n5 = Phase("n5", n4b, norm | pair_wise | {"h": NT, "nd": NT})
        g0 = Phase("g0")
        g1 = Phase("g1")
        four = {f"rows{b}": 16 * 4 * ROUNDS for b in range(4)}
        four |= {"idx_ready": 4 * ROUNDS, "onehot": STEPS, "mm": STEPS, "added": STEPS}
        g2 = Phase("g2", g0, four)
        g3 = Phase("g3", g2, four)
        eight = {f"rows{b}": 16 * GROUP * TURNS for b in range(LIVE)} | {f"reset{b}": 16 * ROUNDS for b in range(2)}
        eight |= {k: STEPS for k in ("onehot", "mm", "added", "oh_tr", "ad_mm", "as_tr")}
        eight |= {k: 2 * ROUNDS for k in ("idx_ready", "ad_copy", "small", "rho_in", "rho_ex", "rho", "rho_mm", "rescale")}
        eight |= {k: 4 * ROUNDS for k in ("oh_evac", "scan", "ex")}
        eight |= {"max_tr": (GROUP + 1) * 2 * ROUNDS}
        g4 = Phase("g4", g1, eight)
        REST = 16 * (2 + 1 + 1 + 7 + 1 + 2 + 1 + 3)
        gate = Phase("gate")
        prep = Phase("prep")

        def step_values(engine_type, row, start, count, top):
            return nc.values_load_multi_w_load_instructions(step_row[0:1, row, bass.ds(start, count)],
                                                            engines=[engine_type], min_val=0, max_val=top,
                                                            skip_runtime_bounds_check_because=
                                                            "the step table is worked out on the chip within its bounds")[1]

        def rounds(engine, body, count):
            body(0, True, False)
            with engine.Fori(1, count - 1) as it:
                body(it, False, False)
            body(count - 1, False, True)

        def norm_stats(seq, src_t, ph):
            with seq.loop(0, PAIRS, 2) as it:
                for k in range(2):
                    seq.done(nc.vector.bn_stats(stats[:, bass.ds(2 * it + k, 1), :].rearrange("p a c -> p (a c)"),
                                                src_t[:, bass.ds(2 * it + k, 1), 0:D].rearrange("p a c -> p (a c)")))
            norm_scales(seq, ph)

        def norm_scales(seq, ph):
            seq.done(nc.vector.tensor_tensor(mean2[:, :], stats[:, :, 1], stats[:, :, 4], ALU.add))
            seq.done(nc.vector.tensor_tensor(gap[:, :], stats[:, :, 1], stats[:, :, 4], ALU.subtract))
            seq.done(nc.vector.tensor_tensor(var[:, :], stats[:, :, 2], stats[:, :, 5], ALU.add))
            seq.done(nc.vector.scalar_tensor_tensor(out=gap[:, :], in0=gap[:, :], scalar=0.25, in1=gap[:, :],
                                                    op0=ALU.mult, op1=ALU.mult))
            seq.done(nc.vector.scalar_tensor_tensor(out=var[:, :], in0=var[:, :], scalar=1.0 / D, in1=gap[:, :],
                                                    op0=ALU.mult, op1=ALU.add))
            nc.vector.tensor_scalar(var[:, :], var[:, :], EPS, None, ALU.add).then_inc(ph("var"), 1)
            seq.engine.wait_ge(*ph.at("std", 1))
            seq.done(nc.vector.reciprocal(rstd[:, :], nmr[:, :]))
            nc.vector.scalar_tensor_tensor(out=nmr[:, :], in0=mean2[:, :], scalar=-0.5, in1=rstd[:, :],
                                           op0=ALU.mult, op1=ALU.mult).then_inc(ph("rstd"), 1)

        def norm_sqrt(act, ph):
            act.wait_ge(*ph.at("var", 1))
            nc.scalar.activation(nmr[:, :], var[:, :], ACT.Sqrt).then_inc(ph("std"), 1)

        def norm_relu_rows(act, ph):
            def pair(it, first_pair):
                for k in range(2):
                    if not first_pair:
                        act.wait_ge(*ph.at("tr", 4 * it - 2 + 2 * k))
                    t = 2 * it + k
                    nc.scalar.activation(rows[:, k:k + 1, :], X[:, bass.ds(t, 1), :], ACT.Relu,
                                         bias=nmr[:, bass.ds(t, 1)], scale=rstd[:, bass.ds(t, 1)]).then_inc(ph("h"), 1)
            act.wait_ge(*ph.at("rstd", 1))
            pair(0, True)
            with act.Fori(1, PAIRS) as it:
                pair(it, False)

        @block.sync
        def _(sp):
            sp.wait_ge(pads_set, 4)
            whole = (E // P // EQR) * EQR * P
            for t, a in ((dst_i, dst), (src_i, src)):
                sp.dma_start(t[:, 0:QS - 1, :], a[0:whole].rearrange("(q p e) -> p q e", p=EQR, e=P)).then_inc(edges_in, 16)
                left = (E - whole) // P
                sp.dma_start(t[0:left, QS - 1, :], a[whole:whole + left * P].rearrange("(p e) -> p e", e=P)).then_inc(edges_in, 16)
                tail = E - whole - left * P
                sp.dma_start(t[left:left + 1, QS - 1, 0:tail], a[E - tail:E].rearrange("(o e) -> o e", o=1)).then_inc(edges_in, 16)
            full = (N // P) * P
            sp.dma_start(X[:, 0:N // P, :], x[0:full, :].rearrange("(t p) d -> p t d", p=P)).then_inc(x_in, 16)
            sp.dma_start(X[0:N - full, N // P, :], x[full:N, :]).then_inc(x_in, 16)
            def blocks(w):
                return w.rearrange("(b p) n -> p b n", p=P)

            def everywhere(v):
                return v.rearrange("(o d) -> o d", o=1).broadcast_to([P, D])

            sp.dma_start(w_b[:, :, :], blocks(g1_w)).then_inc(weights_in, 16)
            sp.dma_start(w_c[:, :, 0:D], blocks(g2_w)).then_inc(prep("w_in"), 16)
            sp.dma_start(w_heads[:, :, 0:D], blocks(a_w)).then_inc(prep("w_in"), 16)
            for i, v in enumerate((g2_as, g2_ad, a_as.rearrange("h c -> (h c)"), a_ad.rearrange("h c -> (h c)"))):
                sp.dma_start(att_vec[:, i, :], everywhere(v)).then_inc(prep("w_in"), 16)
            sp.dma_start(row_gate[:, 0, :], e_b2.rearrange("(o d) -> o d", o=1)).then_inc(prep("w_in"), 16)
            rest = prep("rest_in")
            for i in range(2):
                sp.dma_start(w_msg[:, :, i * D:(i + 1) * D], blocks(m_w[i * D:(i + 1) * D, :])).then_inc(rest, 16)
            sp.dma_start(w_a[:, :, :], blocks(e_u1)).then_inc(rest, 16)
            sp.dma_start(w_rbf[:, :], e_w1).then_inc(rest, 16)
            for t, v in ((b_gcn, g1_b), (b_gat, g2_b), (b_msg, m_b), (b_heads, a_b), (b_add, e_c2),
                         (gam_msg, m_gamma), (gam_heads, a_gamma)):
                sp.dma_start(t[:, :], everywhere(v)).then_inc(rest, 16)
            sp.dma_start(row_upd[:, :], m_bu.rearrange("(o d) -> o d", o=1)).then_inc(rest, 16)
            with nc.allow_non_contiguous_dma(reason="two short bias columns"):
                sp.dma_start(b_rbf[:, :], e_b1.rearrange("(b p) -> p b", p=P)).then_inc(rest, 16)
                sp.dma_start(b_u1[:, :], e_c1.rearrange("(b p) -> p b", p=P)).then_inc(rest, 16)
            sp.dma_start(rbf_pad[0:E, :], edge_attr).then_inc(rbf_copied, 16)
            sp.wait_ge(steps_known, 1)
            with nc.allow_non_contiguous_dma(reason="416 step entries"):
                for a in range(2):
                    sp.dma_start(step_table[a, :].rearrange("(q p) -> p q", p=ROWS), step_out[:, a, :]).then_inc(steps_out, 16)
            sp.wait_ge(steps_out, 32)
            sp.dma_start(step_row[:, :, :], step_table.rearrange("(o a) s -> o a s", o=1)).then_inc(steps_in, 16)
            sp.dma_start(jB[:, :], step_table[0:1, :].broadcast_to([P, STEPS])).then_inc(steps_in, 16)
            def store_rows(ph, ready, table, rows_t, width):
                with sp.Fori(0, PAIRS) as it:
                    sp.wait_ge(*ph.at(ready, 2 * it + 2))
                    sp.dma_start(table[bass.ds(it * 2 * P, 2 * P), :].rearrange("(t p) d -> p t d", p=P),
                                 rows_t[:, bass.ds(2 * it, 2), 0:width]).then_inc(ph("stored"), 16)

            store_rows(n0, "out", table_gcn, acc, D)
            sp.wait_ge(*n0.at("mm", 4 * PAIRS))
            sp.dma_start(w_b[:, :, :], blocks(e_u2)).then_inc(rest, 16)
            sp.wait_ge(prep("gate_parts"), 1)
            for i in range(3):
                sp.dma_start(parts_gate[i:i + 1, :], part_gate[:, i, :]).then_inc(rest, 16)
            sp.dma_start(rbf_pad[E:E + P // 2, :], edge_attr[0:P // 2, :]).then_inc(rbf_copied, 16)
            sp.dma_start(rbf_pad[E + P // 2:E + P, :], edge_attr[0:P // 2, :]).then_inc(rbf_copied, 16)
            sp.wait_ge(seg_rows_ready, 1)
            sp.dma_start(slot_rows[1:STEPS * P + 1].rearrange("(q p e) -> p q e", p=ROWS, e=P), seg_rows).then_inc(seg_stored, 16)
            sp.dma_start(slot_rows[0:1].rearrange("(o e) -> o e", o=1), edge_pad[:, 0:1]).then_inc(seg_stored, 16)
            sp.wait_ge(seg_stored, 32)
            sp.dma_start(prev_rows, slot_rows[0:STEPS * P].rearrange("(q p e) -> p q e", p=ROWS, e=P)).then_inc(seg_back, 16)
            sp.wait_ge(reset_ready, 1)
            sp.dma_start(reset_rows[0:STEPS * P].rearrange("(q p e) -> p q e", p=ROWS, e=P), prev_rows).then_inc(reset_stored, 16)
            sp.dma_start(reset_rows[STEPS * P:STEPS * P + P].rearrange("(o e) -> o e", o=1), edge_pad[:, :]).then_inc(reset_stored, 16)
            sp.wait_ge(reset_stored, 32)

            def reset_loads(ph, heads):
                def one(it, b, reused):
                    if reused:
                        sp.wait_ge(*ph.at("scan", 2 * (2 * it + b - 1)))
                    sp.dma_start(reset_b[b][0:heads, :],
                                 reset_rows[bass.ds(it * 2 * SG + b * SG, SG + 1)].rearrange("(o e) -> o e", o=1)
                                 .broadcast_to([heads, SG + 1])).then_inc(ph(f"reset{b}"), 16)
                for b in range(2):
                    one(0, b, False)
                with sp.Fori(1, ROUNDS) as it:
                    for b in range(2):
                        one(it, b, True)

            store_rows(n1, "row", table_gat, H, D + 1)
            reset_loads(g1, 1)
            sp.wait_ge(*n1.at("mm", 4 * PAIRS))
            sp.dma_start(w_c[:, :, 0:D], blocks(e_w2)).then_inc(gate("w_in"), 16)
            store_rows(n2, "xrow", table_gate, H, D)
            sp.wait_ge(rbf_copied, 48)

            def rbf_round(it, first_round):
                e0 = step_values(mybir.EngineType.SP, 1, ROUND * it, ROUND, E)
                for k in range(ROUND):
                    if not first_round:
                        sp.wait_ge(gate("rbf_T"), ROUND * (it - 1) + k + 1)
                    sp.dma_start(rbf_rows[:, k, :], rbf_pad[bass.ds(e0[k], P), :]).then_inc(gate(f"rbf{k // 4}"), 16)
            rbf_round(0, True)
            with sp.Fori(1, ROUNDS) as it:
                rbf_round(it, False)
            sp.wait_ge(gate("added"), 1)
            sp.dma_start(b_add[:, :], everywhere(m_beta)).then_inc(n3("w_in"), 16)
            sp.wait_ge(*n3.at("hid", 8 * PAIRS))
            sp.dma_start(w_a[:, :, :], blocks(m_wu)).then_inc(n3("w_in"), 16)
            store_rows(n3b, "row", table_msg, H, D)
            sp.wait_ge(*n3b.at("added", 1))
            sp.dma_start(b_add[:, :], everywhere(a_beta)).then_inc(n4("w_in"), 16)
            store_rows(n4b, "row", table_heads, H, TW)
            reset_loads(g4, HEADS)
            full = N // P
            with sp.Fori(0, full // 2) as it:
                sp.wait_ge(*n5.at("xrow", 2 * it + 2))
                sp.dma_start(out[bass.ds(it * 2 * P, 2 * P), :].rearrange("(t p) d -> p t d", p=P),
                             X[:, bass.ds(2 * it, 2), :]).then_inc(out_stored, 16)
            sp.wait_ge(*n5.at("xrow", full + 1))
            sp.dma_start(out[full * P:N, :], X[0:N - full * P, full, :]).then_inc(out_stored, 16)
            sp.wait_ge(out_stored, 16 * (full // 2 + 1))

        @block.gpsimd
        def _(pool):
            seq = Ordered(pool, pool_seq)
            pool.memset(dst_i[:, QS - 1:QS, :], PAD_DST).then_inc(pads_set, 1)
            pool.memset(src_i[:, QS - 1:QS, :], 0).then_inc(pads_set, 1)
            pool.memset(X[:, N // P:NT, :], 0.0).then_inc(pads_set, 1)
            pool.memset(edge_pad[:, :], -BIG).then_inc(pads_set, 1)
            pool.memset(E_col[:, EC:EW], float(PAD_DST * CODE)).then_inc(consts, 1)
            pool.memset(ones[:, :], 1.0).then_inc(consts, 1)
            pool.memset(ones_bf[:, :], 1.0).then_inc(consts, 1)
            seq.done(pool.memset(ident[:, :], 0.0))
            pool.affine_select(out=ident[:, :], in_=ident[:, :], compare_op=ALU.not_equal, fill=1.0,
                               base=0, pattern=[[-1, P]], channel_multiplier=1).then_inc(consts, 1)
            pool.iota(iota_row[:, :], pattern=[[1, P]], base=0, channel_multiplier=0,
                      allow_small_or_imprecise_dtypes=True).then_inc(consts, 1)
            pool.iota(iota_bf[:, :], pattern=[[1, P]], base=0, channel_multiplier=0,
                      allow_small_or_imprecise_dtypes=True).then_inc(consts, 1)
            pool.iota(diff[:, :], pattern=[[1, P]], base=0, channel_multiplier=-1,
                      allow_small_or_imprecise_dtypes=True).then_inc(consts, 1)
            pool.iota(step_i[:, :], pattern=[[ROWS, QS]], base=0, channel_multiplier=1).then_inc(consts, 1)

            def gather_rounds(ph, table, width, per, places):
                turns = len(places)

                def turn(it, first_turn):
                    for b, place in enumerate(places):
                        if not first_turn:
                            pool.wait_ge(*ph.at("mm", per * (turns * (it - 1) + b + 1)))
                        pool.tensor_copy(idx[:, b * per:(b + 1) * per],
                                         srcI[:, bass.ds(per * (turns * it + b), per)]).then_inc(ph("idx_ready"), 1)
                        pool.wait_ge(*ph.at("idx_ready", turns * it + b + 1))
                        pool.sem_inc(ph("go"), 1)
                        for k in range(per):
                            pool.indirect_dma_start(
                                out=place[:, k, 0:width], out_offset=None, in_=table,
                                in_offset=bass.IndirectOffsetOnAxis(ap=idx[:, b * per + k:b * per + k + 1], axis=0)
                            ).then_inc(ph(f"rows{b}"), 16)
                turn(0, True)
                with pool.Fori(1, STEPS // (per * turns)) as it:
                    turn(it, False)

            fours = [G[:, 4 * q:4 * q + 4, :] for q in range(4)]

            pool.wait_ge(*n0.at("stored", 16 * PAIRS))
            pool.wait_ge(slots_ready, 1)
            gather_rounds(g0, table_gcn, D, 4, fours)
            pool.wait_ge(*g0.at("mm", STEPS))
            pool.wait_ge(*n1.at("stored", 16 * PAIRS))
            gather_rounds(g1, table_gat, D + 1, GROUP, G_b)
            pool.wait_ge(*g1.at("mm", STEPS))
            pool.wait_ge(*n2.at("stored", 16 * PAIRS))
            gather_rounds(g2, table_gate, D, 4, fours)
            pool.wait_ge(*g2.at("mm", STEPS))
            pool.wait_ge(*n3b.at("stored", 16 * PAIRS))
            gather_rounds(g3, table_msg, D, 4, fours)
            pool.wait_ge(*g3.at("mm", STEPS))
            pool.wait_ge(*n4b.at("stored", 16 * PAIRS))
            gather_rounds(g4, table_heads, TW, GROUP, G_b)

        @block.scalar
        def _(act):
            seq = Ordered(act, act_seq)
            act.wait_ge(deg_ready, 1)
            nc.scalar.activation(dinv[:, :], tb[:, 2, :], ACT.Sqrt).then_inc(dinv_ready, 1)
            norm_sqrt(act, n0)
            norm_relu_rows(act, n0)

            def evac_transposed(ph, func, first_done=0):
                def pair(it, first_pair, last_pair):
                    if not first_pair:
                        act.wait_ge(*ph.at("mm", 4 * it))
                    act.wait_ge(*ph.at("tr", 4 * it + 4))
                    nc.scalar.activation(HTs.rearrange("p a b c -> p (a b c)"), banks[3], func).then_inc(ph("ht"), 1)
                return pair

            def attention_node_rows(ph, func, heads, rows_of):
                evac = evac_transposed(ph, func)

                def pair(it, first_pair, last_pair):
                    if rows_of is not None:
                        rows_of(it, first_pair)
                    evac(it, first_pair, last_pair)
                    for k in range(2):
                        act.wait_ge(*ph.at("mm", 4 * it + 2 * k + 2))
                        nc.scalar.activation(H[:, bass.ds(2 * it + k, 1), 0:D + heads],
                                             banks[4 + k][:, 0:D + heads].unsqueeze(1), ACT.Copy).then_inc(ph("row"), 1)
                rounds(act, pair, PAIRS)

            def attention_phase(ph, heads):
                w = 2 * heads
                ade = att[:, 0:2 * HEADS * GROUP].rearrange("p (k c) -> p k c", k=GROUP)
                expo = att[:, 384:384 + 2 * heads * GROUP].rearrange("p (a k h) -> p a k h", a=2, k=GROUP)
                ex1 = att[:, 512:512 + heads * GROUP].rearrange("p (k h) -> p k h", k=GROUP)

                def evacs(g, b):
                    for h in range(2):
                        act.wait_ge(*ph.at("oh_tr", GROUP * g + 4 * h + 4))
                        nc.scalar.activation(onehotT_b[b % 2][:, 4 * h:4 * h + 4, :],
                                             banks[h].rearrange("p (k n) -> p k n", k=4), ACT.Copy).then_inc(ph("oh_evac"), 1)

                def copy_ad(g):
                    act.wait_ge(*ph.at("ad_mm", GROUP * (g + 1)))
                    nc.scalar.activation(ade[:, :, 0:w], banks[6][:, 0:16 * GROUP].rearrange("p (k c) -> p k c", k=GROUP)[:, :, 0:w],
                                         ACT.Copy).then_inc(ph("ad_copy"), 1)

                def scales(g, b, low, high):
                    for k in range(low, high):
                        nc.scalar.activation(G_b[b][:, k, 0:D], G_b[b][:, k, 0:D], ACT.Identity,
                                             scale=G_b[b][:, k, D:D + 1]).then_inc(ph("act_scaled"), 1)

                evacs(0, 0)
                copy_ad(0)

                def turn(it, first_turn, last_turn):
                    for b in range(LIVE):
                        g = LIVE * it + b
                        act.wait_ge(*ph.at("small", g + 1))
                        nc.scalar.activation(G_b[b][:, :, D:D + heads], expo[:, 0, :, :], ACT.Exp).then_inc(ph("ex"), 1)
                        nc.scalar.activation(ex1, expo[:, 1, :, :], ACT.Exp).then_inc(ph("ex"), 1)
                        act.wait_ge(*ph.at("rho_in", g + 1))
                        nc.scalar.activation(att[0:1, 600:600 + heads], att[0:1, 592:592 + heads], ACT.Exp).then_inc(ph("rho_ex"), 1)
                        if not (last_turn and b == LIVE - 1):
                            evacs(g + 1, b + 1)
                        if heads == 1:
                            act.wait_ge(*ph.at("ex", 2 * g + 2))
                            scales(g, b, 0, GROUP // 2)
                        if not (last_turn and b == LIVE - 1):
                            copy_ad(g + 1)
                        if heads == 1:
                            scales(g, b, GROUP // 2, GROUP)
                rounds(act, turn, TURNS)

            attention_node_rows(n1, ACT.Relu, 1, None)
            attention_phase(g1, 1)

            def rows_pair(ph, consumed):
                def pair(it, first_pair, last_pair):
                    for k in range(2):
                        if not first_pair:
                            act.wait_ge(*ph.at("tr", 4 * it - 2 + 2 * k))
                            if consumed:
                                act.wait_ge(*ph.at("xrow", 2 * it - 1 + k))
                        t = 2 * it + k
                        nc.scalar.activation(rows[:, k:k + 1, :], X[:, bass.ds(t, 1), :], ACT.Relu,
                                             bias=nmr[:, bass.ds(t, 1)], scale=rstd[:, bass.ds(t, 1)]).then_inc(ph("h"), 1)
                return pair

            def keep_pair(ph):
                def pair(it):
                    act.wait_ge(*ph.at("tr", 4 * it + 4))
                    nc.scalar.activation(HT[:, bass.ds(2 * it, 2), :, :].rearrange("p a b c -> p a (b c)"),
                                         banks[3].rearrange("p (a c) -> p a c", a=2), ACT.Copy).then_inc(ph("ht"), 1)
                return pair

            norm_sqrt(act, n2)
            act.wait_ge(*n2.at("rstd", 1))
            n2_rows, n2_keep = rows_pair(n2, True), keep_pair(n2)

            def n2_pair(it, first_pair, last_pair):
                n2_rows(it, first_pair, last_pair)
                n2_keep(it)
            rounds(act, n2_pair, PAIRS)

            act.wait_ge(prep("rest_in"), REST)

            def cols(j, q):
                act.wait_ge(gate("rbf_T"), 4 * j + 4)
                nc.scalar.activation(rbf_cols[q % 2], banks[0][0:RBF, :], ACT.Copy).then_inc(gate("cols"), 1)

            def silus(j, q):
                for h in range(2):
                    act.wait_ge(gate("hid_mm"), 2 * j + h + 1)
                    nc.scalar.activation(hidden[q % 2][:, h, :], banks[2 + h], ACT.Silu,
                                         bias=b_rbf[:, h:h + 1]).then_inc(gate("hid"), 1)

            def tanhs(j, q, reused):
                for k in range(4):
                    if reused and k == 0:
                        act.wait_ge(gate("gated"), 4 * j - 4)
                    act.wait_ge(gate("gate_mm"), 4 * j + k + 1)
                    nc.scalar.activation(gates[q % 2][:, k, :], banks[6 + k % 2][:, 0:D], ACT.Tanh,
                                         scale=0.5).then_inc(gate("gate"), 1)

            cols(0, 0)
            cols(1, 1)
            silus(0, 0)

            def gate_round(it, first_round, last_round):
                for q in range(4):
                    j = 4 * it + q
                    if not (last_round and q >= 2):
                        cols(j + 2, q)
                    if not (last_round and q == 3):
                        silus(j + 1, q + 1)
                    tanhs(j, q, not (first_round and q < 2))
            rounds(act, gate_round, ROUNDS)

            def n3_pair(it, first_pair, last_pair):
                act.wait_ge(*n3.at("tr", 4 * it + 4))
                if not first_pair:
                    act.wait_ge(*n3.at("hid", 8 * it))
                nc.scalar.activation(HTs.rearrange("p a b c -> p (a b c)"), banks[3], ACT.Copy).then_inc(n3("ht"), 1)
                if not first_pair:
                    act.wait_ge(*n3.at("mm", 4 * it))
                for h in range(2):
                    act.wait_ge(*n3.at("hid", 8 * it + 4 * h + 4))
                    nc.scalar.activation(upd_T[:, h, :], banks[1 + h][:, 0:2 * P], ACT.Silu,
                                         bias=b_u1[:, h:h + 1]).then_inc(n3("act"), 1)
            rounds(act, n3_pair, PAIRS)

            norm_sqrt(act, n3b)
            act.wait_ge(*n3b.at("rstd", 1))
            n3b_rows = rows_pair(n3b, False)
            n3b_evac = evac_transposed(n3b, ACT.Copy)

            def n3b_pair(it, first_pair, last_pair):
                n3b_rows(it, first_pair, last_pair)
                if not first_pair:
                    act.wait_ge(*n3b.at("kept", it))
                n3b_evac(it, first_pair, last_pair)
                for k in range(2):
                    act.wait_ge(*n3b.at("mm", 4 * it + 2 * k + 2))
                    nc.scalar.activation(H[:, bass.ds(2 * it + k, 1), 0:D], banks[4 + k][:, 0:D].unsqueeze(1),
                                         ACT.Copy).then_inc(n3b("row"), 1)
            rounds(act, n3b_pair, PAIRS)

            def msg_evac(j, q):
                act.wait_ge(*g3.at("oh_tr", 4 * j + 4))
                nc.scalar.activation(onehotT_msg[:, (4 * q) % ROUND:(4 * q) % ROUND + 4, :],
                                     banks[2].rearrange("p (k n) -> p k n", k=4), ACT.Copy).then_inc(g3("oh_evac"), 1)
            act.wait_ge(*n3b.at("stored", 16 * PAIRS))
            msg_evac(0, 0)

            def msg_round(it, first_round, last_round):
                for q in range(4):
                    j = 4 * it + q
                    if not (last_round and q == 3):
                        msg_evac(j + 1, q + 1)
                    act.wait_ge(*g3.at("sum", 2 * j + 2))
                    nc.scalar.activation(G[:, 4 * q:4 * q + 4, 0:D], G[:, 4 * q:4 * q + 4, 0:D], ACT.Relu).then_inc(g3("relu"), 1)
            rounds(act, msg_round, ROUNDS)

            def n4_pair(it, first_pair, last_pair):
                act.wait_ge(*n4.at("tr", 4 * it + 4))
                if not first_pair:
                    act.wait_ge(*n4.at("mm", 10 * it))
                nc.scalar.activation(HTs.rearrange("p a b c -> p (a b c)"), banks[3], ACT.Copy).then_inc(n4("ht"), 1)
                nc.scalar.activation(rows[:, :, :], HT[:, bass.ds(2 * it, 2), :, :].rearrange("p a b c -> p a (b c)"),
                                     ACT.Copy).then_inc(n4("ht"), 1)
                for k in range(2):
                    act.wait_ge(*n4.at("mm", 10 * it + 5 * k + 5))
                    nc.scalar.activation(H[:, bass.ds(2 * it + k, 1), 0:D], banks[4 + k][:, 0:D].unsqueeze(1),
                                         ACT.Relu).then_inc(n4("row"), 1)
            rounds(act, n4_pair, PAIRS)

            def normalise(ph, t_in, width):
                act.wait_ge(*ph.at("rstd", 1))
                with act.Fori(0, NT) as t:
                    nc.scalar.activation(t_in[:, bass.ds(t, 1), 0:width], t_in[:, bass.ds(t, 1), 0:width], ACT.Identity,
                                         bias=nmr[:, bass.ds(t, 1)], scale=rstd[:, bass.ds(t, 1)]).then_inc(ph("normed"), 1)
            norm_sqrt(act, n4)
            normalise(n4, H, D)

            norm_sqrt(act, n4b)
            act.wait_ge(*n4b.at("rstd", 1))
            n4b_rows = rows_pair(n4b, False)
            attention_node_rows(n4b, ACT.Copy, HEADS, lambda it, first_pair: n4b_rows(it, first_pair, False))
            attention_phase(g4, HEADS)
            norm_sqrt(act, n5)
            normalise(n5, acc, D)

        @block.tensor
        def _(pe):
            pe.wait_ge(consts, 8)
            pe.wait_ge(codes, 1)
            for q in range(QS):
                nc.tensor.transpose(banks[0][:, q * P:q * P + EQR], code_rows[:, q, :], ident[0:EQR, 0:EQR]).then_inc(codes_T, 1)

            def hist(it, first_round):
                for b in range(2):
                    if not first_round:
                        pe.wait_ge(hist_add, 2 * it + b - 1)
                    pe.wait_ge(hist_oh, (2 * it + b + 1) * (HB + 1))
                    for c in range(HB):
                        nc.tensor.matmul(banks[1 + b][:, 0:NT], oh_lo[:, b, c, :], oh_hi[:, b, c, :],
                                         start=c == 0, stop=c == HB - 1).then_inc(hist_mm, 1)
            hist(0, True)
            with pe.Fori(1, HROUNDS) as it:
                hist(it, False)
            pe.wait_ge(counts, 1)
            nc.tensor.matmul(banks[0][:, 0:NT], ones[:, :], tb[:, 0, :], start=True, stop=True).then_inc(totals, 1)

            pe.wait_ge(weights_in, 16)

            def transposes(it, ph, first_round):
                pe.wait_ge(*ph.at("h", 2 * it + 2))
                for k in range(2):
                    for c in range(2):
                        nc.tensor.transpose(banks[3][:, (2 * k + c) * P:(2 * k + c + 1) * P],
                                            rows[:, k, c * P:(c + 1) * P],
                                            ident[:, :]).then_inc(ph("tr"), 1)

            def products(it, ph, w, width, first_round):
                for k in range(2):
                    if not first_round:
                        pe.wait_ge(*ph.at("out", 2 * it - 1 + k))
                    for c in range(2):
                        nc.tensor.matmul(banks[4 + k][:, 0:width],
                                         HTs[:, k, c, :],
                                         w[:, c, 0:width], start=c == 0, stop=c == 1).then_inc(ph("mm"), 1)

            def node_rounds(ph, w, width):
                def one(it, first_round):
                    transposes(it, ph, first_round)
                    pe.wait_ge(*ph.at("ht0", it + 1))
                    products(it, ph, w, width, first_round)
                one(0, True)
                with pe.Fori(1, PAIRS) as it:
                    one(it, False)
            node_rounds(n0, w_b, D)

            pe.wait_ge(tiles_known, 1)

            def shift_round(it, first_round):
                q = [pe.value_load(tile_i[0:1, 0, bass.ds(2 * it + k, 1)], min_val=0, max_val=ECOLS - 1) for k in range(2)]
                for k in range(2):
                    if not first_round:
                        pe.wait_ge(slots_copied, 2 * it + k - 1)
                    pe.wait_ge(shift_ready, 2 * (2 * it + k + 1))
                    for a in range(2):
                        nc.tensor.matmul(banks[6 + k][:, 0:ECOLS], shift[:, k, a, :], E_col[:, bass.ds(q[k] + a, ECOLS)],
                                         start=a == 0, stop=a == 1).then_inc(shifted, 1)
            shift_round(0, True)
            with pe.Fori(1, PAIRS) as it:
                shift_round(it, False)

            pe.wait_ge(seg_ready, 1)
            for q in range(QS):
                nc.tensor.transpose(banks[0][0:ROWS, q * P:(q + 1) * P], tmp_a[:, q * ROWS:(q + 1) * ROWS], ident[:, :]).then_inc(seg_T, 1)
            pe.wait_ge(reset_ready, 1)
            for q in range(QS):
                nc.tensor.transpose(banks[1][:, q * ROWS:(q + 1) * ROWS], seg_rows[:, q, :], ident[0:ROWS, 0:ROWS]).then_inc(first_T, 1)

            def scatter(it, k, ph, first_round):
                if not (first_round and k < 2):
                    pe.wait_ge(*ph.at("added", ROUND * it + k - 1))
                nc.tensor.matmul(banks[4 + k % 2][:, 0:D], onehot[:, k, :], G[:, k, 0:D],
                                 start=True, stop=True).then_inc(ph("mm"), 1)

            def gcn_round(it, first_round, last_round):
                for k in range(ROUND):
                    if k % 4 == 0:
                        pe.wait_ge(*g0.at(f"rows{k // 4}", 64 * it + 64))
                        pe.wait_ge(*g0.at("onehot", ROUND * it + k + 4))
                    scatter(it, k, g0, first_round)
            rounds(pe, gcn_round, ROUNDS)

            def node_products(ph, w, width, ready, source):
                def one(it, first_pair, last_pair):
                    pe.wait_ge(*ph.at(ready, 2 * it + 2))
                    if not first_pair:
                        pe.wait_ge(*ph.at("ht", it))
                    for k in range(2):
                        for c in range(2):
                            nc.tensor.transpose(banks[3][:, (2 * k + c) * P:(2 * k + c + 1) * P],
                                                rows[:, k, c * P:(c + 1) * P], ident[:, :]).then_inc(ph("tr"), 1)
                    pe.wait_ge(*ph.at("ht", it + 1))
                    for k in range(2):
                        if not first_pair:
                            for what in source:
                                pe.wait_ge(*ph.at(what, 2 * it - 1 + k))
                        for c in range(2):
                            nc.tensor.matmul(banks[4 + k][:, 0:width], HTs[:, k, c, :], w[:, c, 0:width],
                                             start=c == 0, stop=c == 1).then_inc(ph("mm"), 1)
                rounds(pe, one, PAIRS)

            def attention_phase(ph, heads, scores):
                w = 2 * heads

                def targets(g, b, reused):
                    pe.wait_ge(*ph.at("onehot", GROUP * (g + 1)))
                    for k in range(GROUP):
                        if reused and k % 4 == 0:
                            pe.wait_ge(*ph.at("oh_evac", 2 * g - 1 + k // 4))
                        nc.tensor.transpose(banks[k // 4][:, (k % 4) * P:(k % 4 + 1) * P], onehot_b[b][:, k, :],
                                            ident[:, :]).then_inc(ph("oh_tr"), 1)
                    tile_of = step_values(mybir.EngineType.PE, 0, GROUP * g, GROUP, NT - 1)
                    if reused:
                        pe.wait_ge(*ph.at("ad_copy", g))
                    for k in range(GROUP):
                        if k % 4 == 0:
                            pe.wait_ge(*ph.at("oh_evac", 2 * g + 1 + k // 4))
                        nc.tensor.matmul(banks[6][:, 16 * k:16 * k + w], onehotT_b[b % 2][:, k, :],
                                         nd[:, bass.ds(tile_of[k], 1), 0:w].rearrange("p a c -> p (a c)"),
                                         start=True, stop=True).then_inc(ph("ad_mm"), 1)

                def sources(turn_of, g, b, reused):
                    pe.wait_ge(*ph.at(f"rows{b}", GROUP * 16 * (turn_of + 1)))
                    if reused:
                        pe.wait_ge(*ph.at("scan", 2 * g))
                    for k in range(GROUP):
                        nc.tensor.transpose(PS[0:heads, 2 + k // 4, (k % 4) * P:(k % 4 + 1) * P], G_b[b][:, k, D:D + heads],
                                            ident[:, :]).then_inc(ph("as_tr"), 1)

                def sums(g, b, first_group):
                    if heads == 1:
                        pe.wait_ge(*ph.at("own_col", g + 1))
                    for k in range(GROUP):
                        pe.wait_ge(*ph.at("act_scaled" if heads == 1 else "scaled", GROUP * g + k + 1))
                        if not (first_group and k < 2):
                            pe.wait_ge(*ph.at("added", GROUP * g + k - 1))
                        nc.tensor.matmul(banks[4 + k % 2][:, 0:D + w], onehot_b[b][:, k, :],
                                         G_b[b][:, k, 0:D + w], start=True, stop=True).then_inc(ph("mm"), 1)

                def maxima(g, b, reused):
                    pe.wait_ge(*ph.at("scan", 2 * (g + 1)))
                    if reused:
                        pe.wait_ge(*ph.at("rho_in", g))
                    pe.sem_inc(pe_go, 1)
                    for k in range(GROUP):
                        nc.tensor.transpose(banks[7][:, 16 * k:16 * k + heads], both[0:heads, k * P:(k + 1) * P],
                                            ident[0:heads, 0:heads]).then_inc(ph("max_tr"), 1)
                    nc.tensor.transpose(banks[7][0:1, 128:128 + heads], fwd_b[1 - b % 2][0:heads, SG - 1:SG],
                                        ident[0:heads, 0:heads]).then_inc(ph("max_tr"), 1)

                def rescale(g, b, last_group):
                    pe.wait_ge(*ph.at("rho", g + 1))
                    if not last_group:
                        pe.wait_ge(*ph.at("ad_copy", g + 2))
                    nc.tensor.matmul(banks[6][:, 160:160 + heads], onehot_b[b][0:1, 0, :], att[0:1, 608:608 + heads],
                                     start=True, stop=True).then_inc(ph("rho_mm"), 1)

                pe.wait_ge(*scores)
                sources(0, 0, 0, False)
                targets(0, 0, False)
                maxima(0, 0, False)
                sources(0, 1, 1, True)

                def turn(it, first_turn, last_turn):
                    for b in range(LIVE):
                        g = LIVE * it + b
                        last_group = last_turn and b == LIVE - 1
                        if not last_group:
                            if not (first_turn and b == 0):
                                pe.wait_ge(*ph.at("rescale", g))
                            targets(g + 1, (b + 1) % LIVE, True)
                            maxima(g + 1, (b + 1) % LIVE, True)
                        rescale(g, b, last_group)
                        sums(g, b, first_turn and b == 0)
                        if not (last_turn and b >= LIVE - 2):
                            sources(it + (b + 2) // LIVE, g + 2, (b + 2) % LIVE, True)
                rounds(pe, turn, TURNS)

            pe.wait_ge(prep("w_ready"), 2)
            node_products(n1, w_c, D + 2, "agg", ("row", "nd"))
            attention_phase(g1, 1, n1.at("nd", NT))

            def n2_pair(it, first_pair, last_pair):
                pe.wait_ge(*n2.at("h", 2 * it + 2))
                if not first_pair:
                    pe.wait_ge(*n2.at("ht", it))
                for k in range(2):
                    for c in range(2):
                        nc.tensor.transpose(banks[3][:, (2 * k + c) * P:(2 * k + c + 1) * P],
                                            rows[:, k, c * P:(c + 1) * P], ident[:, :]).then_inc(n2("tr"), 1)
            rounds(pe, n2_pair, PAIRS)

            pe.wait_ge(prep("rest_in"), REST)
            pe.wait_ge(gate("w_in"), 16)

            def rbf_T(it, q, j, reused):
                pe.wait_ge(gate(f"rbf{q}"), 64 * (it + 1))
                if reused:
                    pe.wait_ge(gate("cols"), j)
                pe.sem_inc(pe_go, 1)
                for k in range(4):
                    nc.tensor.transpose(banks[0][0:RBF, k * P:(k + 1) * P], rbf_rows[:, 4 * q + k, :],
                                        ident[:, :]).then_inc(gate("rbf_T"), 1)

            def hid_mm(j, q, reused):
                pe.wait_ge(gate("cols"), j + 1)
                for h in range(2):
                    if reused:
                        pe.wait_ge(gate("hid"), 2 * j - 1 + h)
                    nc.tensor.matmul(banks[2 + h], w_rbf[:, h * P:(h + 1) * P], rbf_cols[q % 2],
                                     start=True, stop=True).then_inc(gate("hid_mm"), 1)

            def gate_mm(j, q, reused):
                pe.wait_ge(gate("hid"), 2 * j + 2)
                for k in range(4):
                    if reused or k >= 2:
                        pe.wait_ge(gate("gate"), 4 * j + k - 1)
                    for h in range(2):
                        nc.tensor.matmul(banks[6 + k % 2][:, 0:D], hidden[q % 2][:, h, k * P:(k + 1) * P],
                                         w_c[:, h, 0:D], start=h == 0, stop=False)
                    nc.tensor.matmul(banks[6 + k % 2][:, 0:D], ones_bf[:, :], parts_gate[:, :],
                                     start=False, stop=True).then_inc(gate("gate_mm"), 1)

            rbf_T(0, 0, 0, False)
            rbf_T(0, 1, 1, True)
            hid_mm(0, 0, False)

            def gate_round(it, first_round, last_round):
                for q in range(4):
                    j = 4 * it + q
                    if not (last_round and q >= 2):
                        rbf_T(it + (q + 2) // 4, (q + 2) % 4, j + 2, True)
                    if not (last_round and q == 3):
                        hid_mm(j + 1, q + 1, True)
                    gate_mm(j, q, not (first_round and q == 0))
                    if not (first_round and q == 0):
                        back = (q - 1) % 4
                        pe.wait_ge(gate("gated"), 4 * j)
                        for k in range(4):
                            scatter(it if q else it - 1, 4 * back + k, g2, first_round and q == 1)
            rounds(pe, gate_round, ROUNDS)
            pe.wait_ge(gate("gated"), STEPS)
            for k in range(4):
                scatter(ROUNDS - 1, 12 + k, g2, False)

            def n3_pair(it, first_pair, last_pair):
                pe.wait_ge(*n3.at("agg", it + 1))
                if not first_pair:
                    pe.wait_ge(*n3.at("ht", it))
                for k in range(2):
                    for c in range(2):
                        nc.tensor.transpose(banks[3][:, (2 * k + c) * P:(2 * k + c + 1) * P],
                                            rows[:, k, c * P:(c + 1) * P], ident[:, :]).then_inc(n3("tr"), 1)
                pe.wait_ge(*n3.at("ht", it + 1))
                for h in range(2):
                    if not first_pair:
                        pe.wait_ge(*n3.at("act", 2 * it - 1 + h))
                    for c in range(4):
                        moving = (HT[:, bass.ds(2 * it, 2), c, :] if c < 2 else HTs[:, :, c - 2, :])
                        nc.tensor.matmul(banks[1 + h][:, 0:2 * P], w_a[:, c, h * P:(h + 1) * P], moving,
                                         start=c == 0, stop=c == 3).then_inc(n3("hid"), 1)
                pe.wait_ge(*n3.at("act", 2 * it + 2))
                for k in range(2):
                    if not first_pair:
                        pe.wait_ge(*n3.at("out", 2 * it - 1 + k))
                    for h in range(2):
                        nc.tensor.matmul(banks[4 + k][:, 0:D], upd_T[:, h, k * P:(k + 1) * P], w_b[:, h, :],
                                         start=h == 0, stop=h == 1).then_inc(n3("mm"), 1)
            rounds(pe, n3_pair, PAIRS)
            node_products(n3b, w_msg, 2 * D, "h", ("row", "out"))

            def msg_T(j, q, reused):
                pe.wait_ge(*g3.at("onehot", 4 * j + 4))
                if reused:
                    pe.wait_ge(*g3.at("oh_evac", j))
                for k in range(4):
                    nc.tensor.transpose(banks[2][:, k * P:(k + 1) * P], onehot[:, (4 * q + k) % ROUND, :],
                                        ident[:, :]).then_inc(g3("oh_tr"), 1)

            def msg_q(j, q, tile_of, reused):
                pe.wait_ge(*g3.at("oh_evac", j + 1))
                for k in range(4):
                    if reused and k % 2 == 0:
                        pe.wait_ge(*g3.at("sum", 2 * j - 1 + k // 2))
                    nc.tensor.matmul(banks[k // 2][:, (k % 2) * D:(k % 2 + 1) * D], onehotT_msg[:, 4 * q + k, :],
                                     Q[:, bass.ds(tile_of[4 * q + k] * D, D)], start=True, stop=True).then_inc(g3("qmm"), 1)
            msg_T(0, 0, False)

            def msg_round(it, first_round, last_round):
                tile_of = step_values(mybir.EngineType.PE, 0, ROUND * it, ROUND, NT - 1)
                for q in range(4):
                    j = 4 * it + q
                    if not (last_round and q == 3):
                        msg_T(j + 1, q + 1, True)
                    msg_q(j, q, tile_of, not (first_round and q == 0))
                    if not (first_round and q == 0):
                        back = (q - 1) % 4
                        pe.wait_ge(*g3.at("relu", j))
                        for k in range(4):
                            scatter(it if q else it - 1, 4 * back + k, g3, first_round and q == 1)
            rounds(pe, msg_round, ROUNDS)
            pe.wait_ge(*g3.at("relu", STEPS // 4))
            for k in range(4):
                scatter(ROUNDS - 1, 12 + k, g3, False)

            pe.wait_ge(*n3.at("w_in", 32))

            def n4_pair(it, first_pair, last_pair):
                pe.wait_ge(*n4.at("agg", it + 1))
                if not first_pair:
                    pe.wait_ge(*n4.at("ht", 2 * it))
                for k in range(2):
                    for c in range(2):
                        nc.tensor.transpose(banks[3][:, (2 * k + c) * P:(2 * k + c + 1) * P],
                                            G[:, k, c * P:(c + 1) * P], ident[:, :]).then_inc(n4("tr"), 1)
                pe.wait_ge(*n4.at("ht", 2 * it + 2))
                for k in range(2):
                    if not first_pair:
                        pe.wait_ge(*n4.at("row", 2 * it - 1 + k))
                    nc.tensor.matmul(banks[4 + k][:, 0:D], ones[0:1, :], row_upd[:, :], start=True, stop=False).then_inc(n4("mm"), 1)
                    for c in range(4):
                        still = rows[:, k, c * P:(c + 1) * P] if c < 2 else HTs[:, k, c - 2, :]
                        nc.tensor.matmul(banks[4 + k][:, 0:D], still, w_a[:, c, :], start=False, stop=c == 3).then_inc(n4("mm"), 1)
            rounds(pe, n4_pair, PAIRS)
            node_products(n4b, w_heads, GW, "h", ("row", "nd"))
            attention_phase(g4, HEADS, n4b.at("nd", NT))

        @block.vector
        def _(dve):
            seq = Ordered(dve, dve_seq)
            tile_scalar = tb
            CNT, DEG, REC, TOT, INC, BEG, NUM, SIN, STA, CCC, DLT, RMD = range(12)
            dve.wait_ge(edges_in, 16 * 6)
            seq.done(nc.vector.tensor_copy(dst_f, dst_i[:, :, :]))
            seq.done(nc.vector.tensor_copy(src_f, src_i[:, :, :]))
            nc.vector.scalar_tensor_tensor(out=code_rows, in0=dst_f, scalar=float(CODE), in1=src_f,
                                           op0=ALU.mult, op1=ALU.add).then_inc(codes, 1)
            dve.wait_ge(codes_T, QS)
            for q in range(QS):
                seq.done(nc.vector.tensor_copy(E_col[:, q * EQR:(q + 1) * EQR], banks[0][:, q * P:q * P + EQR]))
            seq.done(nc.vector.tensor_copy(col_i[:, :], E_col[:, 0:EC]))
            seq.done(nc.vector.tensor_scalar(col_j[:, :], col_i[:, :], 19, None, ALU.logical_shift_right))
            seq.done(nc.vector.tensor_copy(hi_f, col_j[:, :]))
            seq.done(nc.vector.tensor_scalar(col_j[:, :], col_i[:, :], 12, 127, ALU.logical_shift_right, ALU.bitwise_and))
            seq.done(nc.vector.tensor_copy(lo_f, col_j[:, :]))
            seq.done(nc.vector.memset(tb[:, CNT, :], 0.0))
            dve.wait_ge(consts, 8)

            def hist(it, first_round):
                for b in range(2):
                    c0 = (2 * it + b) * HB
                    if not first_round:
                        dve.wait_ge(hist_mm, HB * (2 * it + b - 1))
                    for c in range(HB):
                        nc.vector.tensor_scalar(oh_lo[:, b, c, :], iota_bf[:, :], lo_f[:, bass.ds(c0 + c, 1)], None,
                                                ALU.is_equal).then_inc(hist_oh, 1)
                    nc.vector.tensor_tensor(oh_hi[:, b, :, :], iota_row[:, 0:NT].unsqueeze(1).broadcast_to([P, HB, NT]),
                                            hi_f[:, bass.ds(c0, HB)].unsqueeze(2).broadcast_to([P, HB, NT]),
                                            ALU.is_equal).then_inc(hist_oh, 1)
                    if not (first_round and b == 0):
                        dve.wait_ge(hist_mm, HB * (2 * it + b))
                        if not (first_round and b < 2):
                            dve.wait_ge(hist_add, 2 * it + b - 1)
                        nc.vector.tensor_tensor(tb[:, CNT, :], tb[:, CNT, :], banks[2 - b][:, 0:NT], ALU.add).then_inc(hist_add, 1)
            hist(0, True)
            with dve.Fori(1, HROUNDS) as it:
                hist(it, False)
            dve.wait_ge(hist_mm, HB * 2 * HROUNDS)
            dve.wait_ge(hist_add, 2 * HROUNDS - 1)
            seq.done(nc.vector.tensor_tensor(tb[:, CNT, :], tb[:, CNT, :], banks[2][:, 0:NT], ALU.add))
            nc.vector.tensor_scalar(lonely[:, :], tb[:, CNT, :], 0.0, None, ALU.is_equal).then_inc(counts, 1)
            seq.done(nc.vector.tensor_scalar(tb[:, DEG, :], tb[:, CNT, :], 1.0, None, ALU.add))
            nc.vector.reciprocal(tb[:, REC, :], tb[:, DEG, :]).then_inc(deg_ready, 1)

            dve.wait_ge(totals, 1)
            seq.done(nc.vector.tensor_copy(tb[:, TOT, :], banks[0][:, 0:NT]))
            seq.done(nc.vector.tensor_tensor_scan(tb[:, INC, :], ones[:, 0:NT], tb[:, TOT, :], 0.0, ALU.mult, ALU.add))
            seq.done(nc.vector.tensor_tensor(tb[:, BEG, :], tb[:, INC, :], tb[:, TOT, :], ALU.subtract))
            seq.done(nc.vector.tensor_scalar(tile_i[:, 3, :], tb[:, TOT, :], float(P - 1), None, ALU.add))
            seq.done(nc.vector.tensor_scalar(tile_i[:, 2, :], tile_i[:, 3, :], 7, None, ALU.logical_shift_right))
            seq.done(nc.vector.tensor_copy(tb[:, NUM, :], tile_i[:, 2, :]))
            seq.done(nc.vector.tensor_tensor_scan(tb[:, SIN, :], ones[:, 0:NT], tb[:, NUM, :], 0.0, ALU.mult, ALU.add))
            seq.done(nc.vector.tensor_tensor(tb[:, STA, :], tb[:, SIN, :], tb[:, NUM, :], ALU.subtract))
            seq.done(nc.vector.scalar_tensor_tensor(out=tb[:, CCC, :], in0=tb[:, STA, :], scalar=-float(P),
                                                    in1=tb[:, BEG, :], op0=ALU.mult, op1=ALU.add))
            seq.done(nc.vector.tensor_copy(tb[:, DLT, 0:1], tb[:, CCC, 0:1]))
            seq.done(nc.vector.tensor_tensor(tb[:, DLT, 1:NT], tb[:, CCC, 1:NT], tb[:, CCC, 0:NT - 1], ALU.subtract))
            seq.done(nc.vector.tensor_copy(tile_i[:, 1, :], tb[:, STA, :]))
            seq.done(nc.vector.tensor_copy(tile_i[:, 2, :], tb[:, BEG, :]))
            seq.done(nc.vector.tensor_scalar(tile_i[:, 3, :], tile_i[:, 2, :], P - 1, None, ALU.bitwise_and))
            seq.done(nc.vector.tensor_copy(tb[:, RMD, :], tile_i[:, 3, :]))
            nc.vector.tensor_scalar(tile_i[:, 0, :], tile_i[:, 2, :], 7, None, ALU.logical_shift_right).then_inc(tiles_known, 1)

            seq.done(nc.vector.tensor_copy(step_f[:, 0, :], step_i[:, :]))
            seq.done(nc.vector.tensor_tensor(indic[:, 0, :, :], step_f[:, 0, :].unsqueeze(2).broadcast_to([ROWS, QS, NT]),
                                             tb[0:ROWS, STA, :].unsqueeze(1).broadcast_to([ROWS, QS, NT]), ALU.is_ge))
            seq.done(nc.vector.tensor_tensor(indic[:, 1, :, :], indic[:, 0, :, :],
                                             tb[0:ROWS, DLT, :].unsqueeze(1).broadcast_to([ROWS, QS, NT]), ALU.mult))
            seq.done(nc.vector.reduce_sum(step_f[:, 1, :], indic[:, 0, :, :], X_AXIS))
            seq.done(nc.vector.reduce_sum(step_f[:, 2, :], indic[:, 1, :, :], X_AXIS))
            seq.done(nc.vector.tensor_scalar(step_out[:, 0, :], step_f[:, 1, :], -1.0, None, ALU.add))
            seq.done(nc.vector.scalar_tensor_tensor(out=step_f[:, 3, :], in0=step_f[:, 0, :], scalar=float(P),
                                                    in1=step_f[:, 2, :], op0=ALU.mult, op1=ALU.add))
            nc.vector.tensor_scalar(step_out[:, 1, :], step_f[:, 3, :], float(E), None, ALU.min).then_inc(steps_known, 1)

            dve.wait_ge(prep("w_in"), 16 * 7)
            for w, heads, v in ((w_c, 1, 0), (w_heads, HEADS, 2)):
                for i in range(2):
                    for c in range(2):
                        seq.done(nc.vector.tensor_tensor(att_tmp, w[:, c, 0:D], att_vec[:, v + i, :], ALU.mult))
                        last = nc.vector.reduce_sum(w[:, c, D + i * heads:D + (i + 1) * heads],
                                                    att_tmp.rearrange("p (h c) -> p h c", h=heads), X_AXIS)
                        seq.done(last)
                dve.sem_inc(prep("w_ready"), 1)
            for i in range(3):
                seq.done(nc.vector.tensor_copy(part_gate[:, i, :], row_gate[:, i, :]))
                if i < 2:
                    seq.done(nc.vector.tensor_tensor(row_gate[:, i + 1, :], row_gate[:, i, :], part_gate[:, i, :], ALU.subtract))
            dve.sem_inc(prep("gate_parts"), 1)

            dve.wait_ge(x_in, 32)
            norm_stats(seq, X, n0)

            dve.wait_ge(dinv_ready, 1)

            def n0_round(it, first_round):
                if not first_round:
                    dve.wait_ge(*n0.at("mm", 4 * it))
                dve.wait_ge(*n0.at("tr", 4 * it + 4))
                nc.vector.tensor_copy(HTs.rearrange("p a b c -> p (a b c)"), banks[3][:, :]).then_inc(n0("ht0"), 1)
                for k in range(2):
                    dve.wait_ge(*n0.at("mm", 4 * it + 2 * k + 2))
                    nc.vector.tensor_scalar(acc[:, bass.ds(2 * it + k, 1), 0:D],
                                            banks[4 + k][:, 0:D].unsqueeze(1), dinv[:, bass.ds(2 * it + k, 1)], None,
                                            ALU.mult).then_inc(n0("out"), 1)
            n0_round(0, True)
            with dve.Fori(1, PAIRS) as it:
                n0_round(it, False)

            def shift_build(it, k):
                for a in range(2):
                    nc.vector.tensor_scalar(shift[:, k, a, :], diff[:, :], tb[:, RMD, bass.ds(2 * it + k, 1)], float(a * P),
                                            ALU.add, ALU.is_equal).then_inc(shift_ready, 1)

            def shift_round(it, first_round):
                s = [dve.value_load(tile_i[0:1, 1, bass.ds(2 * it + k, 1)], min_val=0, max_val=STEPS - 1) for k in range(2)]
                for k in range(2):
                    if not first_round:
                        dve.wait_ge(shifted, 2 * (2 * it + k - 1))
                    shift_build(it, k)
                for k in range(2):
                    dve.wait_ge(shifted, 2 * (2 * it + k + 1))
                    if not (first_round and k == 0):
                        dve.wait_ge(slots_copied, 2 * it + k)
                    nc.vector.tensor_copy(slots[:, bass.ds(s[k], ECOLS)], banks[6 + k][:, 0:ECOLS]).then_inc(slots_copied, 1)
            shift_round(0, True)
            with dve.Fori(1, PAIRS) as it:
                shift_round(it, False)
            dve.wait_ge(slots_copied, NT)

            dve.wait_ge(steps_in, 32)
            seq.done(nc.vector.tensor_copy(slot_i[:, :], slots[:, 0:STEPS]))
            seq.done(nc.vector.tensor_scalar(srcI[:, :], slot_i[:, :], CODE - 1, None, ALU.bitwise_and))
            seq.done(nc.vector.tensor_scalar(slot_i[:, :], slot_i[:, :], 12, None, ALU.logical_shift_right))
            seq.done(nc.vector.tensor_copy(tmp_a, slot_i[:, :]))
            seq.done(nc.vector.tensor_copy(tmp_b, jB[:, :]))
            seq.done(nc.vector.scalar_tensor_tensor(out=dloc[:, :], in0=tmp_b, scalar=-float(P), in1=tmp_a,
                                                    op0=ALU.mult, op1=ALU.add))
            seq.done(nc.vector.scalar_tensor_tensor(out=tmp_a, in0=tmp_b, scalar=float(CODE), in1=tmp_a,
                                                    op0=ALU.mult, op1=ALU.add))
            seq.done(nc.vector.memset(first[:, 0:1], 0.0))
            dve.sem_inc(slots_ready, 1)
            dve.sem_inc(seg_ready, 1)
            dve.wait_ge(seg_T, QS)
            nc.vector.tensor_copy(seg_rows, banks[0][0:ROWS, :].rearrange("p (q e) -> p q e", q=QS)).then_inc(seg_rows_ready, 1)
            dve.wait_ge(seg_rows_ready, 1)
            dve.wait_ge(seg_back, 16)
            seq.done(nc.vector.tensor_tensor(prev_rows, prev_rows, seg_rows, ALU.is_equal))
            seq.done(nc.vector.tensor_scalar(seg_rows, prev_rows, -1.0, 1.0, ALU.mult, ALU.add))
            nc.vector.tensor_scalar(prev_rows, seg_rows, -BIG, None, ALU.mult).then_inc(reset_ready, 1)
            dve.wait_ge(first_T, QS)
            nc.vector.tensor_copy(first[:, :], banks[1][:, 0:STEPS]).then_inc(first_ready, 1)

            def make_onehot(it, k, ph):
                nc.vector.tensor_scalar(onehot[:, k, :], iota_row[:, :], dloc[:, bass.ds(ROUND * it + k, 1)], None,
                                        ALU.is_equal).then_inc(ph("onehot"), 1)

            def tiles_of(step0, count):
                return step_values(mybir.EngineType.DVE, 0, step0, count, NT - 1)

            def add_step(ph, step, k, reg, width, very_first):
                dve.wait_ge(*ph.at("mm", step + 1))
                if not very_first:
                    dve.wait_ge(*ph.at("added", step))
                nc.vector.tensor_tensor(acc[:, bass.ds(reg, 1), 0:width], acc[:, bass.ds(reg, 1), 0:width],
                                        banks[4 + k % 2][:, 0:width].unsqueeze(1), ALU.add).then_inc(ph("added"), 1)

            for k in range(ROUND):
                make_onehot(0, k, g0)

            def gcn_round(it, first_round, last_round):
                regs = tiles_of(ROUND * it, ROUND)
                for k in range(ROUND):
                    add_step(g0, ROUND * it + k, k, regs[k], D, first_round and k == 0)
                    if not last_round:
                        make_onehot(it + 1, k, g0)
            rounds(dve, gcn_round, ROUNDS)
            dve.wait_ge(*g0.at("added", STEPS))

            def score_columns(ph, heads, it, k):
                dve.wait_ge(*ph.at("row", 2 * it + k + 1))
                nc.vector.tensor_copy(nd[:, bass.ds(2 * it + k, 1), 0:2 * heads],
                                      banks[4 + k][:, D:D + 2 * heads].unsqueeze(1)).then_inc(ph("nd"), 1)

            dve.wait_ge(prep("rest_in"), REST)

            def n1_pair(it, first_pair, last_pair):
                for k in range(2):
                    if not first_pair:
                        dve.wait_ge(*n1.at("tr", 4 * it - 2 + 2 * k))
                    t = 2 * it + k
                    nc.vector.scalar_tensor_tensor(out=rows[:, k:k + 1, :], in0=acc[:, bass.ds(t, 1), 0:D],
                                                   scalar=dinv[:, bass.ds(t, 1)], in1=b_gcn[:, :].unsqueeze(1),
                                                   op0=ALU.mult, op1=ALU.add).then_inc(n1("agg"), 1)
                for k in range(2):
                    score_columns(n1, 1, it, k)
            rounds(dve, n1_pair, PAIRS)
            dve.wait_ge(*n1.at("agg", NT))
            dve.wait_ge(*n1.at("nd", NT))
            seq.done(nc.vector.memset(acc[:, :, :], 0.0))

            def attention_phase(ph, heads):
                w = 2 * heads
                n = heads * GROUP
                ade = att[:, 0:16 * GROUP].rearrange("p (k c) -> p k c", k=GROUP)
                asd, add_ = ade[:, :, 0:heads], ade[:, :, heads:w]
                top = att[:, 128:128 + n].rearrange("p (k h) -> p k h", k=GROUP)
                z = att[:, 192:192 + 3 * n].rearrange("p (a k h) -> p a k h", a=3, k=GROUP)
                zf = att[:, 192:192 + 3 * n]
                expo = att[:, 384:384 + 2 * n].rearrange("p (a k h) -> p a k h", a=2, k=GROUP)
                ex1 = att[:, 512:512 + n].rearrange("p (k h) -> p k h", k=GROUP)
                rr = att[:, 616:616 + heads]
                ps_max = banks[7][:, 0:16 * GROUP].rearrange("p (k c) -> p k c", k=GROUP)[:, :, 0:heads]

                def onehot_of(g, b, k):
                    nc.vector.tensor_scalar(onehot_b[b][:, k, :], iota_row[:, :],
                                            dloc[:, bass.ds(GROUP * g + k, 1)], None, ALU.is_equal).then_inc(ph("onehot"), 1)

                def scans(turn_of, g, b, reused):
                    b = b % 2
                    dve.wait_ge(*ph.at(f"reset{b}", 16 * (turn_of + 1)))
                    dve.wait_ge(*ph.at("as_tr", GROUP * (g + 1)))
                    if reused:
                        dve.wait_ge(*ph.at("max_tr", (GROUP + 1) * g))
                        dve.wait_ge(*ph.at("scan", 2 * g))
                    nc.vector.tensor_tensor_scan(fwd_b[b][0:heads, :], reset_b[b][0:heads, 0:SG],
                                                 PS[0:heads, 2:4, :].rearrange("p a e -> p (a e)"),
                                                 fwd_b[1 - b][0:heads, SG - 1:SG], ALU.add, ALU.max).then_inc(ph("scan"), 1)
                    dve.wait_ge(*ph.at("scan", 2 * g + 1))
                    nc.vector.tensor_tensor_scan(both[0:heads, ::-1], reset_b[b][0:heads, SG:0:-1],
                                                 fwd_b[b][0:heads, ::-1], LOW, ALU.add, ALU.max).then_inc(ph("scan"), 1)

                def adds(g, b, regs, first_group, last_groups):
                    for k in range(GROUP):
                        add_step(ph, GROUP * g + k, k, regs[k], D + w, first_group and k == 0)
                        if not last_groups:
                            onehot_of(g + 2, (b + 2) % LIVE, k)

                def exponents(g, b):
                    dve.wait_ge(*ph.at("max_tr", (GROUP + 1) * (g + 1)))
                    dve.wait_ge(*ph.at("ad_copy", g + 1))
                    a0 = att[0:1, 576:576 + heads]
                    a1 = att[0:1, 584:584 + heads]
                    a2 = att[0:1, 592:592 + heads]
                    seq.start(nc.vector.tensor_tensor(z[:, 0, :, :], G_b[b][:, :, D:D + heads], add_, ALU.add))
                    seq.start(nc.vector.tensor_tensor(z[:, 1, :, :], asd, add_, ALU.add))
                    seq.start(nc.vector.tensor_tensor(top, ps_max, asd, ALU.max))
                    seq.done(nc.vector.tensor_tensor(a0, banks[7][0:1, 128:128 + heads], asd[0:1, 0, :], ALU.max))
                    seq.start(nc.vector.tensor_tensor(z[:, 2, :, :], top, add_, ALU.add))
                    seq.done(nc.vector.tensor_tensor(a0, a0, add_[0:1, 0, :], ALU.add))
                    seq.start(nc.vector.scalar_tensor_tensor(out=zf, in0=zf, scalar=SLOPE, in1=zf, op0=ALU.mult, op1=ALU.max))
                    seq.done(nc.vector.scalar_tensor_tensor(out=a1, in0=a0, scalar=SLOPE, in1=a0, op0=ALU.mult, op1=ALU.max))
                    nc.vector.tensor_tensor(expo, z[:, 0:2, :, :], z[:, 2:3, :, :].broadcast_to([P, 2, GROUP, heads]),
                                            ALU.subtract).then_inc(ph("small"), 1)
                    seq.done(nc.vector.tensor_tensor(a1, a1, z[0:1, 2, 0, :], ALU.subtract))
                    nc.vector.tensor_scalar(a2, a1, 0.0, None, ALU.min).then_inc(ph("rho_in"), 1)

                def scales(g, b):
                    dve.wait_ge(*ph.at("ex", 2 * (g + 1)))
                    own = nc.vector.tensor_tensor(G_b[b][:, :, D + heads:D + w], ex1,
                                                  first[:, bass.ds(GROUP * g, GROUP)].unsqueeze(2)
                                                  .broadcast_to([P, GROUP, heads]), ALU.mult)
                    if heads == 1:
                        own.then_inc(ph("own_col"), 1)
                        return
                    for k in range(GROUP):
                        rh = G_b[b][:, k, 0:D].rearrange("p (h c) -> p h c", h=heads)
                        nc.vector.tensor_tensor(rh, rh, G_b[b][:, k, D:D + heads].unsqueeze(2)
                                                .broadcast_to([P, heads, D // heads]), ALU.mult).then_inc(ph("scaled"), 1)

                def rho(g):
                    dve.wait_ge(*ph.at("rho_ex", g + 1))
                    nc.vector.tensor_scalar(att[0:1, 608:608 + heads], att[0:1, 600:600 + heads], -1.0, None,
                                            ALU.add).then_inc(ph("rho"), 1)

                def rescale(g, reg, first_group):
                    if not first_group:
                        dve.wait_ge(*ph.at("added", GROUP * g))
                    dve.wait_ge(*ph.at("rho_mm", g + 1))
                    nc.vector.tensor_scalar(rr, banks[6][:, 160:160 + heads], 1.0, None, ALU.add).then_inc(ph("rescale"), 1)
                    dve.wait_ge(*ph.at("rescale", g + 1))
                    av = acc[:, bass.ds(reg, 1), 0:D].rearrange("p a (h c) -> p (a h) c", h=heads)
                    seq.start(nc.vector.tensor_tensor(av, av, rr.unsqueeze(2).broadcast_to([P, heads, D // heads]), ALU.mult))
                    aw = acc[:, bass.ds(reg, 1), D:D + w].rearrange("p a (v h) -> p (a v) h", v=2)
                    seq.done(nc.vector.tensor_tensor(aw, aw, rr.unsqueeze(1).broadcast_to([P, 2, heads]), ALU.mult))

                seq.done(nc.vector.memset(fwd_b[1][0:heads, SG - 1:SG], LOW))
                scans(0, 0, 0, False)
                for g in range(2):
                    for k in range(GROUP):
                        onehot_of(g, g, k)

                def turn(it, first_turn, last_turn):
                    for b in range(LIVE):
                        g = LIVE * it + b
                        first_group = first_turn and b == 0
                        exponents(g, b)
                        if not (last_turn and b == LIVE - 1):
                            scans(2 * it + (b + 1) // 2, g + 1, b + 1, True)
                        rho(g)
                        regs = tiles_of(GROUP * g, GROUP)
                        scales(g, b)
                        rescale(g, regs[0], first_group)
                        adds(g, b, regs, first_group, last_turn and b >= LIVE - 2)
                turn(0, True, False)
                with seq.loop(1, TURNS - 1, LIVE * (9 + 2)) as it:
                    turn(it, False, False)
                turn(TURNS - 1, False, True)
                dve.wait_ge(*ph.at("added", STEPS))

            def attention_end(heads):
                num = acc[:, :, 0:D].rearrange("p t (h c) -> p t h c", h=heads)
                own = H[:, :, 0:D].rearrange("p t (h c) -> p t h c", h=heads)
                ws, dn = w_self[:, :, 0:heads], den[:, :, 0:heads]
                seq.done(nc.vector.tensor_tensor(ws, acc[:, :, D + heads:D + 2 * heads],
                                                 lonely[:, :].unsqueeze(2).broadcast_to([P, NT, heads]), ALU.add))
                seq.done(nc.vector.scalar_tensor_tensor(out=dn, in0=acc[:, :, D:D + heads], scalar=1e-16, in1=ws,
                                                        op0=ALU.add, op1=ALU.add))
                seq.done(nc.vector.reciprocal(dn, dn))
                seq.done(nc.vector.tensor_tensor(ws, ws, dn, ALU.mult))
                wide = [P, NT, heads, D // heads]
                seq.done(nc.vector.tensor_tensor(num, num, dn.unsqueeze(3).broadcast_to(wide), ALU.mult))
                seq.done(nc.vector.tensor_tensor(own, own, ws.unsqueeze(3).broadcast_to(wide), ALU.mult))
                seq.done(nc.vector.tensor_tensor(num, num, own, ALU.add))

            def on_tiles(row):
                return row[:, :].unsqueeze(1).broadcast_to([P, NT, D])

            attention_phase(g1, 1)

            attention_end(1)
            seq.done(nc.vector.tensor_tensor(acc[:, :, 0:D], acc[:, :, 0:D], on_tiles(b_gat), ALU.add))
            seq.done(nc.vector.scalar_tensor_tensor(out=X[:, :, :], in0=acc[:, :, 0:D], scalar=0.0, in1=X[:, :, :],
                                                    op0=ALU.max, op1=ALU.add))
            norm_stats(seq, X, n2)

            def n2_pair(it, first_pair, last_pair):
                for k in range(2):
                    t = 2 * it + k
                    dve.wait_ge(*n2.at("h", t + 1))
                    nc.vector.tensor_scalar(H[:, bass.ds(t, 1), 0:D], rows[:, k:k + 1, :], 0.5, None, ALU.mult).then_inc(n2("half"), 1)
                    nc.vector.tensor_tensor(X[:, bass.ds(t, 1), :], X[:, bass.ds(t, 1), :], rows[:, k:k + 1, :],
                                            ALU.add).then_inc(n2("xrow"), 1)
            rounds(dve, n2_pair, PAIRS)
            dve.wait_ge(*n2.at("xrow", NT))
            nc.vector.tensor_tensor(X[:, :, :], X[:, :, :], on_tiles(b_add), ALU.add).then_inc(gate("added"), 1)
            seq.done(nc.vector.memset(acc[:, :, 0:D], 0.0))

            def four_onehots(ph, j, q):
                for k in range(4):
                    kk = (4 * q + k) % ROUND
                    nc.vector.tensor_scalar(onehot[:, kk, :], iota_row[:, :], dloc[:, bass.ds(4 * j + k, 1)], None,
                                            ALU.is_equal).then_inc(ph("onehot"), 1)

            def four_adds(ph, j, back, regs, very_first):
                for k in range(4):
                    add_step(ph, 4 * j + k, k, regs[k], D, very_first and k == 0)

            four_onehots(g2, 0, 0)
            four_onehots(g2, 1, 1)

            def gate_round(it, first_round, last_round):
                for q in range(4):
                    j = 4 * it + q
                    if not (last_round and q >= 2):
                        four_onehots(g2, j + 2, q + 2)
                    dve.wait_ge(*g2.at(f"rows{q}", 64 * (it + 1)))
                    for k in range(4):
                        dve.wait_ge(gate("gate"), 4 * j + k + 1)
                        r = G[:, 4 * q + k, 0:D]
                        nc.vector.scalar_tensor_tensor(out=r, in0=gates[q % 2][:, k, :], scalar=1.0, in1=r,
                                                       op0=ALU.add, op1=ALU.mult).then_inc(gate("gated"), 1)
                    if not (first_round and q == 0):
                        regs = tiles_of(4 * j - 4, 4)
                        four_adds(g2, j - 1, 0, regs, first_round and q == 1)
            rounds(dve, gate_round, ROUNDS)
            four_adds(g2, STEPS // 4 - 1, 0, tiles_of(STEPS - 4, 4), False)
            dve.wait_ge(*g2.at("added", STEPS))

            def n3_copy(it, first_pair):
                if not first_pair:
                    dve.wait_ge(*n3.at("tr", 4 * it))
                nc.vector.tensor_copy(rows[:, :, :], acc[:, bass.ds(2 * it, 2), 0:D]).then_inc(n3("agg"), 1)
            dve.wait_ge(gate("added"), 1)
            n3_copy(0, True)

            def n3_pair(it, first_pair, last_pair):
                if not last_pair:
                    n3_copy(it + 1, False)
                for k in range(2):
                    t = 2 * it + k
                    dve.wait_ge(*n3.at("mm", 4 * it + 2 * k + 2))
                    nc.vector.tensor_tensor(X[:, bass.ds(t, 1), :], X[:, bass.ds(t, 1), :],
                                            banks[4 + k][:, 0:D].unsqueeze(1), ALU.add).then_inc(n3("out"), 1)
            rounds(dve, n3_pair, PAIRS)
            dve.wait_ge(*n3.at("out", NT))
            norm_stats(seq, X, n3b)

            def n3b_pair(it, first_pair, last_pair):
                for k in range(2):
                    t = 2 * it + k
                    dve.wait_ge(*n3b.at("row", t + 1))
                    nc.vector.tensor_tensor(Q[:, bass.ds(t * D, D)], banks[4 + k][:, D:2 * D], b_msg[:, :],
                                            ALU.add).then_inc(n3b("out"), 1)
                dve.wait_ge(*n3b.at("ht", it + 1))
                nc.vector.tensor_copy(HT[:, bass.ds(2 * it, 2), :, :].rearrange("p a b c -> p a (b c)"),
                                      HTs.rearrange("p a b c -> p a (b c)")).then_inc(n3b("kept"), 1)
            rounds(dve, n3b_pair, PAIRS)
            dve.wait_ge(*n3b.at("out", NT))
            dve.wait_ge(*n3b.at("kept", PAIRS))
            dve.wait_ge(*n3.at("w_in", 32))
            nc.vector.tensor_tensor(X[:, :, :], X[:, :, :], on_tiles(b_add), ALU.add).then_inc(n3b("added"), 1)
            seq.done(nc.vector.memset(acc[:, :, 0:D], 0.0))

            four_onehots(g3, 0, 0)
            four_onehots(g3, 1, 1)

            def msg_round(it, first_round, last_round):
                for q in range(4):
                    j = 4 * it + q
                    if not (last_round and q >= 2):
                        four_onehots(g3, j + 2, q + 2)
                    dve.wait_ge(*g3.at(f"rows{q}", 64 * (it + 1)))
                    for k in (0, 2):
                        dve.wait_ge(*g3.at("qmm", 4 * j + k + 2))
                        r = G[:, 4 * q + k:4 * q + k + 2, 0:D]
                        nc.vector.tensor_tensor(r, r, banks[k // 2].rearrange("p (k d) -> p k d", k=2),
                                                ALU.add).then_inc(g3("sum"), 1)
                    if not (first_round and q == 0):
                        regs = tiles_of(4 * j - 4, 4)
                        four_adds(g3, j - 1, 0, regs, first_round and q == 1)
            rounds(dve, msg_round, ROUNDS)
            four_adds(g3, STEPS // 4 - 1, 0, tiles_of(STEPS - 4, 4), False)
            dve.wait_ge(*g3.at("added", STEPS))

            dve.wait_ge(*n3b.at("added", 1))
            dve.wait_ge(*g3.at("mm", STEPS))

            def n4_copy(it, first_pair):
                if not first_pair:
                    dve.wait_ge(*n4.at("tr", 4 * it))
                nc.vector.tensor_copy(G[:, 0:2, 0:D], acc[:, bass.ds(2 * it, 2), 0:D]).then_inc(n4("agg"), 1)
            n4_copy(0, True)

            def n4_pair(it, first_pair, last_pair):
                if not last_pair:
                    n4_copy(it + 1, False)
                for k in range(2):
                    t = 2 * it + k
                    dve.wait_ge(*n4.at("row", t + 1))
                    nc.vector.bn_stats(stats[:, bass.ds(t, 1), :].rearrange("p a c -> p (a c)"),
                                       H[:, bass.ds(t, 1), 0:D].rearrange("p a c -> p (a c)")).then_inc(n4("stats"), 1)
            rounds(dve, n4_pair, PAIRS)
            dve.wait_ge(*n4.at("stats", NT))
            norm_scales(seq, n4)

            def scaled_add(ph, t_in):
                with seq.loop(0, PAIRS, 4) as it:
                    for k in range(2):
                        t = 2 * it + k
                        dve.wait_ge(*ph.at("normed", t + 1))
                        seq.done(nc.vector.tensor_tensor(t_in[:, bass.ds(t, 1), 0:D], t_in[:, bass.ds(t, 1), 0:D],
                                                         (gam_msg if ph is n4 else gam_heads)[:, :].unsqueeze(1), ALU.mult))
                        if ph is n4:
                            seq.done(nc.vector.tensor_tensor(X[:, bass.ds(t, 1), :], X[:, bass.ds(t, 1), :],
                                                             t_in[:, bass.ds(t, 1), 0:D], ALU.add))
                        else:
                            ins = nc.vector.tensor_tensor(X[:, bass.ds(t, 1), :], X[:, bass.ds(t, 1), :],
                                                          t_in[:, bass.ds(t, 1), 0:D], ALU.add)
                            seq.done(ins)
                            dve.sem_inc(ph("xrow"), 1)
            scaled_add(n4, H)
            norm_stats(seq, X, n4b)

            def n4b_pair(it, first_pair, last_pair):
                for k in range(2):
                    score_columns(n4b, HEADS, it, k)
            rounds(dve, n4b_pair, PAIRS)
            dve.wait_ge(*n4b.at("nd", NT))
            dve.wait_ge(*n4.at("w_in", 16))
            seq.done(nc.vector.tensor_tensor(X[:, :, :], X[:, :, :], on_tiles(b_add), ALU.add))
            seq.done(nc.vector.memset(acc[:, :, :], 0.0))
            attention_phase(g4, HEADS)
            attention_end(HEADS)
            seq.done(nc.vector.tensor_tensor(acc[:, :, 0:D], acc[:, :, 0:D], on_tiles(b_heads), ALU.add))
            norm_stats(seq, acc, n5)
            scaled_add(n5, acc)


_INS = ['x', 'src', 'dst', 'edge_attr_64', 'L0_gnn_W1', 'L0_gnn_b1', 'L0_gnn_W2', 'L0_gnn_att_src', 'L0_gnn_att_dst',
        'L0_gnn_b2', 'L1_gnn_W1', 'L1_gnn_b1', 'L1_gnn_W2', 'L1_gnn_b2', 'L1_gnn_U1', 'L1_gnn_c1', 'L1_gnn_U2',
        'L1_gnn_c2', 'L2_gnn_W_msg', 'L2_gnn_b_msg', 'L2_gnn_W_upd', 'L2_gnn_b_upd', 'L2_gnn_gamma', 'L2_gnn_beta',
        'L3_gnn_W', 'L3_gnn_att_src', 'L3_gnn_att_dst', 'L3_gnn_bias', 'L3_gnn_ln_gamma', 'L3_gnn_ln_beta']


def kernel(**inputs):
    import numpy as _np
    import concourse.bacc as _bacc
    from concourse import mybir as _mybir
    from concourse.bass_utils import run_bass_kernel_spmd as _run

    nc = _bacc.Bacc("TRN2", target_bir_lowering=False, num_devices=1)
    arrays, args = {}, []
    for name in _INS:
        a = _np.ascontiguousarray(inputs[name])
        arrays[f"in_{name}"] = a
        args.append(nc.dram_tensor(f"in_{name}", a.shape, _mybir.dt.from_np(a.dtype), kind="ExternalInput").ap())
    args.append(nc.dram_tensor("out_x", (N, D), _mybir.dt.float32, kind="ExternalOutput").ap())
    gnn_four_layers(nc, *args)
    r = _run(nc, [arrays], core_ids=[0])
    return r.results[0]["out_x"]
```

```python
import concourse.bass as bass
from concourse import mybir
from concourse.alu_op_type import AluOpType as ALU
from contextlib import ExitStack, contextmanager

FP32 = mybir.dt.float32
BF16 = mybir.dt.bfloat16
I32 = mybir.dt.int32
ACT = mybir.ActivationFunctionType
X_AXIS = mybir.AxisListType.X

P = 128
N = 3125
E = 50000
D = 256
HEADS = 8
RBF = 64
REAL_TILES = -(-N // P)
NT = REAL_TILES + 1
PAIRS = NT // 2
GROUP = 8
ROUND = 2 * GROUP
STEPS = -(-(E // P + REAL_TILES) // ROUND) * ROUND
ROUNDS = STEPS // ROUND
SUM_BANKS = (0, 1, 4, 5)
LIVE = 4
GROUPS = STEPS // GROUP
TURNS = GROUPS // LIVE
QS = 4
ROWS = STEPS // QS
ECOLS = -(-E // P)
EQR = -(-ECOLS // QS)
EC = EQR * QS
EW = EC + ECOLS + 1
HB = 7
HROUNDS = EC // (2 * HB)
PAD_DST = 4000
CODE = 4096
TW = D + HEADS
GW = D + 2 * HEADS
BIG = 3.0e38
LOW = -1.0e30
EPS = 1e-5
SLOPE = 0.2


class Ordered:

    def __init__(self, engine, semaphore):
        self.engine, self.semaphore, self.base, self.n = engine, semaphore, 0, 0

    def done(self, instruction):
        instruction.then_inc(self.semaphore, 1)
        self.n += 1
        self.engine.wait_ge(self.semaphore, self.base + self.n)

    def start(self, instruction):
        instruction.then_inc(self.semaphore, 1)
        self.n += 1

    @contextmanager
    def loop(self, low, high, per):
        start = self.base + self.n
        with self.engine.Fori(low, high) as it:
            self.base, self.n = start + (it - low) * per, 0
            yield it
            assert self.n == per, (self.n, per)
        self.base, self.n = start + (high - low) * per, 0


def gnn_four_layers(nc, x, src, dst, edge_attr, g1_w, g1_b, g2_w, g2_as, g2_ad, g2_b,
                    e_w1, e_b1, e_w2, e_b2, e_u1, e_c1, e_u2, e_c2,
                    m_w, m_b, m_wu, m_bu, m_gamma, m_beta,
                    a_w, a_as, a_ad, a_b, a_gamma, a_beta, out):
    ctx = ExitStack()
    with ctx:
        def sb(name, shape, dt=FP32):
            return ctx.enter_context(nc.sbuf_tensor(name, shape, dt))

        def sem(name):
            return ctx.enter_context(nc.semaphore(name))

        def dram(name, shape, dt=FP32):
            return nc.dram_tensor(name, shape, dt).ap()

        step_table = dram("step_table", (2, STEPS), I32)
        slot_rows = dram("slot_rows", (STEPS * P + 1,))
        reset_rows = dram("reset_rows", (STEPS * P + P,))
        rbf_pad = dram("rbf_pad", (E + P, RBF))
        table_gcn = dram("table_gcn", (NT * P, D))
        table_gat = dram("table_gat", (NT * P, D + 1))
        table_gate = dram("table_gate", (NT * P, D))
        table_msg = dram("table_msg", (NT * P, D))
        table_heads = dram("table_heads", (NT * P, TW))

        X = sb("X", [P, NT, D])
        acc = sb("acc", [P, NT, GW])
        H = sb("H", [P, NT, TW])
        HT = sb("HT", [P, NT, 2, P])
        Q = sb("Q", [P, NT * D])
        G = sb("G", [P, ROUND, GW])
        onehot = sb("onehot", [P, ROUND, P])
        pair_space = sb("pair_space", [P, 4 * D])
        rows = pair_space[:, 0:2 * D].rearrange("p (k d) -> p k d", k=2)
        HTs = pair_space[:, 2 * D:4 * D].rearrange("p (a b n) -> p a b n", a=2, b=2)
        w_a = sb("w_a", [P, 4, D])
        w_b = sb("w_b", [P, 2, D])
        w_c = sb("w_c", [P, 2, D + 2])
        w_heads = sb("w_heads", [P, 2, GW])
        w_msg = sb("w_msg", [P, 2, 2 * D])
        w_rbf = sb("w_rbf", [RBF, D])
        b_gcn = sb("b_gcn", [P, D])
        b_gat = sb("b_gat", [P, D])
        b_msg = sb("b_msg", [P, D])
        b_heads = sb("b_heads", [P, D])
        b_add = sb("b_add", [P, D])
        gam_msg = sb("gam_msg", [P, D])
        gam_heads = sb("gam_heads", [P, D])
        b_rbf = sb("b_rbf", [P, 2])
        b_u1 = sb("b_u1", [P, 2])
        row_upd = sb("row_upd", [1, D])
        part_gate = sb("part_gate", [1, 3, D], BF16)
        parts_gate = sb("parts_gate", [3, D], BF16)
        ones_bf = sb("ones_bf", [3, P], BF16)
        ident = sb("ident", [P, P])
        ones = sb("ones", [P, P])
        iota_row = sb("iota_row", [P, P])
        iota_bf = sb("iota_bf", [P, P], BF16)
        srcI = sb("srcI", [P, STEPS], I32)
        dloc = sb("dloc", [P, STEPS])
        first = sb("first", [P, STEPS])
        step_row = sb("step_row", [1, 2, STEPS], I32)
        idx = sb("idx", [P, LIVE * GROUP], I32)
        tb = sb("tb", [P, 12, NT])
        tile_i = sb("tile_i", [P, 4, NT], I32)
        nd = sb("nd", [P, NT, 2 * HEADS])
        w_self = sb("w_self", [P, NT, HEADS])
        den = sb("den", [P, NT, HEADS])
        dinv = sb("dinv", [P, NT])
        lonely = sb("lonely", [P, NT])
        stats = sb("stats", [P, NT, 6])
        mean2 = sb("mean2", [P, NT])
        gap = sb("gap", [P, NT])
        var = sb("var", [P, NT])
        rstd = sb("rstd", [P, NT])
        nmr = sb("nmr", [P, NT])
        att = sb("att", [P, 640])
        edge_pad = sb("edge_pad", [1, P])
        step_i = sb("step_i", [ROWS, QS], I32)
        step_f = sb("step_f", [ROWS, 4, QS])
        step_out = sb("step_out", [ROWS, 2, QS], I32)

        PS = ctx.enter_context(nc.psum_tensor("psum", [P, 8, 512], FP32))
        banks = [PS[:, i, :] for i in range(8)]

        E_col = Q[:, 0:EW]
        slots = Q[:, 800:800 + EC + STEPS]
        code_rows = Q[0:EQR, 1700:1700 + QS * P].rearrange("p (q e) -> p q e", q=QS)
        dst_f = Q[0:EQR, 2300:2300 + QS * P].rearrange("p (q e) -> p q e", q=QS)
        src_f = Q[0:EQR, 2900:2900 + QS * P].rearrange("p (q e) -> p q e", q=QS)
        lo_f = Q[:, 3500:3500 + EC]
        hi_f = Q[:, 3900:3900 + EC]
        tmp_a = Q[:, 4300:4300 + STEPS]
        tmp_b = Q[:, 4720:4720 + STEPS]
        seg_rows = Q[0:ROWS, 5140:5140 + QS * P].rearrange("p (q e) -> p q e", q=QS)
        prev_rows = Q[0:ROWS, 5660:5660 + QS * P].rearrange("p (q e) -> p q e", q=QS)
        Hf = H[:, :, :].rearrange("p t c -> p (t c)")
        dst_i = Hf[0:EQR, 0:512].bitcast(I32).rearrange("p (q e) -> p q e", q=QS)
        src_i = Hf[0:EQR, 512:1024].bitcast(I32).rearrange("p (q e) -> p q e", q=QS)
        col_i = Hf[:, 1024:1024 + EC].bitcast(I32)
        col_j = Hf[:, 1420:1420 + EC].bitcast(I32)
        slot_i = Hf[:, 1820:1820 + STEPS].bitcast(I32)
        jB = Hf[:, 2240:2240 + STEPS].bitcast(I32)
        oh_lo = Hf[:, 2660:2660 + HB * P].bitcast(BF16).rearrange("p (b c n) -> p b c n", b=2, c=HB)
        oh_hi = Hf[:, 3556:3556 + HB * NT].bitcast(BF16).rearrange("p (b c n) -> p b c n", b=2, c=HB)
        indic = Hf[0:ROWS, 3740:3740 + 2 * QS * NT].rearrange("p (a q n) -> p a q n", a=2, q=QS)
        shift = Hf[:, 3948:3948 + 4 * P].rearrange("p (k a n) -> p k a n", k=2, a=2)
        diff = Hf[:, 4460:4460 + P]
        att_vec = Hf[:, 4588:4588 + 4 * D].rearrange("p (v d) -> p v d", v=4)
        att_tmp = Hf[:, 5612:5612 + D]
        row_gate = Hf[0:1, 5868:5868 + 3 * D].rearrange("p (v d) -> p v d", v=3)

        SG = GROUP * P
        reset_b = [Q[0:HEADS, b * 1028:b * 1028 + SG + 1] for b in range(2)]
        fwd_b = [Q[0:HEADS, 2056 + b * SG:2056 + (b + 1) * SG] for b in range(2)]
        both = Q[0:HEADS, 2056 + 2 * SG:2056 + 3 * SG]
        HTf = HT[:, :, :, :].rearrange("p t b n -> p (t b n)")
        G_more = HTf[:, 0:ROUND * GW].rearrange("p (k c) -> p k c", k=ROUND)
        G_b = [G[:, 0:GROUP, :], G[:, GROUP:ROUND, :], G_more[:, 0:GROUP, :], G_more[:, GROUP:ROUND, :]]
        onehotT_b = [HTf[:, ROUND * GW + b * SG:ROUND * GW + (b + 1) * SG].rearrange("p (k n) -> p k n", k=GROUP)
                     for b in range(2)]
        onehot_b = [onehot[:, 0:GROUP, :], onehot[:, GROUP:ROUND, :],
                    Q[:, 5128:5128 + SG].rearrange("p (k n) -> p k n", k=GROUP),
                    pair_space[:, :].rearrange("p (k n) -> p k n", k=GROUP)]
        rbf_rows = Q[:, 0:ROUND * RBF].rearrange("p (k c) -> p k c", k=ROUND)
        rbf_cols = [Q[0:RBF, 1024 + b * 512:1536 + b * 512] for b in range(2)]
        hidden = [Q[:, 2048 + b * 1024:3072 + b * 1024].rearrange("p (h e) -> p h e", h=2) for b in range(2)]
        gates = [Q[:, 4096 + b * 1024:5120 + b * 1024].rearrange("p (k d) -> p k d", k=4) for b in range(2)]
        onehotT_msg = Hf[:, 0:ROUND * P].rearrange("p (k n) -> p k n", k=ROUND)
        upd_T = Q[:, 0:2 * D].rearrange("p (h n) -> p h n", h=2)

        block = ctx.enter_context(nc.Block())

        pads_set = sem("pads_set")
        consts = sem("consts")
        x_in = sem("x_in")
        edges_in = sem("edges_in")
        weights_in = sem("weights_in")
        rbf_copied = sem("rbf_copied")
        codes = sem("codes")
        codes_T = sem("codes_T")
        hist_oh = sem("hist_oh")
        hist_mm = sem("hist_mm")
        hist_add = sem("hist_add")
        counts = sem("counts")
        totals = sem("totals")
        deg_ready = sem("deg_ready")
        dinv_ready = sem("dinv_ready")
        tiles_known = sem("tiles_known")
        steps_known = sem("steps_known")
        steps_out = sem("steps_out")
        steps_in = sem("steps_in")
        shift_ready = sem("shift_ready")
        shifted = sem("shifted")
        slots_copied = sem("slots_copied")
        slots_ready = sem("slots_ready")
        seg_ready = sem("seg_ready")
        seg_T = sem("seg_T")
        seg_rows_ready = sem("seg_rows_ready")
        seg_stored = sem("seg_stored")
        seg_back = sem("seg_back")
        reset_ready = sem("reset_ready")
        reset_stored = sem("reset_stored")
        first_T = sem("first_T")
        first_ready = sem("first_ready")
        pe_go = sem("pe_go")
        dve_seq = sem("dve_seq")
        pool_seq = sem("pool_seq")
        act_seq = sem("act_seq")
        out_stored = sem("out_stored")
        acc_cleared = sem("acc_cleared")
        bias_added = sem("bias_added")

        class Phase:

            def __init__(self, name, after=None, totals=None):
                self.name, self.made, self.totals = name, {}, {}
                if after is not None:
                    self.made = after.made
                    self.totals = {k: totals.get(k, 0) + after.totals.get(k, 0) for k in totals | after.totals}

            def __call__(self, what):
                if what not in self.made:
                    self.made[what] = sem(f"{self.name}_{what}")
                return self.made[what]

            def at(self, what, count):
                return self(what), self.totals.get(what, 0) + count

        norm = {"var": 1, "std": 1, "rstd": 1}
        pair_wise = {"tr": 4 * PAIRS, "ht": NT, "mm": 4 * PAIRS, "row": NT, "stored": 16 * PAIRS}
        n0 = Phase("n0")
        n1 = Phase("n1", n0, norm | {"h": NT, "ht": NT, "row": NT, "tr": 4 * PAIRS, "mm": 4 * PAIRS, "out": NT, "stored": 16 * PAIRS})
        n2 = Phase("n2", n1, pair_wise | {"agg": NT, "nd": NT})
        n3 = Phase("n3", n2, norm | {"h": NT, "tr": 4 * PAIRS, "ht": NT, "xrow": NT, "stored": 16 * PAIRS})
        n3b = Phase("n3b", n3, {"agg": PAIRS, "tr": 4 * PAIRS, "ht": PAIRS, "mm": 4 * PAIRS, "out": NT, "w_in": 32})
        n4 = Phase("n4", n3b, norm | pair_wise | {"h": NT, "out": NT})
        n4b = Phase("n4b", n4, norm | {"agg": NT, "tr": 4 * PAIRS, "ht": 2 * NT, "mm": 10 * PAIRS, "row": NT,
                                       "normed": NT, "w_in": 16, "xrow": NT, "gamma": NT})
        n5 = Phase("n5", n4b, norm | pair_wise | {"h": NT, "nd": NT})
        g0 = Phase("g0")
        g1 = Phase("g1")
        four = {f"rows{b}": 16 * 4 * ROUNDS for b in range(4)}
        four |= {"idx_ready": 4 * ROUNDS, "onehot": STEPS, "mm": STEPS, "added": STEPS}
        g2 = Phase("g2", g0, four)
        g3 = Phase("g3", g2, four)
        eight = {f"rows{b}": 16 * GROUP * TURNS for b in range(LIVE)} | {f"reset{b}": 16 * ROUNDS for b in range(2)}
        eight |= {k: STEPS for k in ("onehot", "mm", "added", "oh_tr", "ad_mm", "as_tr")}
        eight |= {k: 2 * ROUNDS for k in ("idx_ready", "ad_copy", "small", "rho_in", "rho_ex", "rho", "rho_mm", "rescale")}
        eight |= {k: 4 * ROUNDS for k in ("oh_evac", "scan", "ex")}
        eight |= {"max_tr": (GROUP + 1) * 2 * ROUNDS}
        g4 = Phase("g4", g1, eight)
        REST = 16 * (2 + 1 + 1 + 7 + 1 + 2 + 1 + 3)
        gate = Phase("gate")
        prep = Phase("prep")

        def step_values(engine_type, row, start, count, top):
            return nc.values_load_multi_w_load_instructions(step_row[0:1, row, bass.ds(start, count)],
                                                            engines=[engine_type], min_val=0, max_val=top,
                                                            skip_runtime_bounds_check_because=
                                                            "the step table is worked out on the chip within its bounds")[1]

        def rounds(engine, body, count):
            body(0, True, False)
            with engine.Fori(1, count - 1) as it:
                body(it, False, False)
            body(count - 1, False, True)

        def norm_stats(seq, src_t, ph):
            with seq.loop(0, PAIRS, 2) as it:
                for k in range(2):
                    seq.start(nc.vector.bn_stats(stats[:, bass.ds(2 * it + k, 1), :].rearrange("p a c -> p (a c)"),
                                                 src_t[:, bass.ds(2 * it + k, 1), 0:D].rearrange("p a c -> p (a c)")))
            seq.engine.wait_ge(seq.semaphore, seq.base + seq.n)
            norm_scales(seq, ph)

        def norm_scales(seq, ph):
            seq.start(nc.vector.tensor_tensor(mean2[:, :], stats[:, :, 1], stats[:, :, 4], ALU.add))
            seq.start(nc.vector.tensor_tensor(gap[:, :], stats[:, :, 1], stats[:, :, 4], ALU.subtract))
            seq.done(nc.vector.tensor_tensor(var[:, :], stats[:, :, 2], stats[:, :, 5], ALU.add))
            seq.done(nc.vector.scalar_tensor_tensor(out=gap[:, :], in0=gap[:, :], scalar=0.25, in1=gap[:, :],
                                                    op0=ALU.mult, op1=ALU.mult))
            seq.done(nc.vector.scalar_tensor_tensor(out=var[:, :], in0=var[:, :], scalar=1.0 / D, in1=gap[:, :],
                                                    op0=ALU.mult, op1=ALU.add))
            nc.vector.tensor_scalar(var[:, :], var[:, :], EPS, None, ALU.add).then_inc(ph("var"), 1)
            seq.engine.wait_ge(*ph.at("std", 1))
            seq.done(nc.vector.reciprocal(rstd[:, :], nmr[:, :]))
            nc.vector.scalar_tensor_tensor(out=nmr[:, :], in0=mean2[:, :], scalar=-0.5, in1=rstd[:, :],
                                           op0=ALU.mult, op1=ALU.mult).then_inc(ph("rstd"), 1)

        def norm_sqrt(act, ph):
            act.wait_ge(*ph.at("var", 1))
            nc.scalar.activation(nmr[:, :], var[:, :], ACT.Sqrt).then_inc(ph("std"), 1)

        def tile_rounds(engine, body):
            rounds(engine, lambda it, first_pair, last_pair:
                   [body(2 * it + k, k, first_pair, last_pair) for k in range(2)], PAIRS)

        @block.sync
        def _(sp):
            sp.wait_ge(pads_set, 4)
            whole = (E // P // EQR) * EQR * P
            for t, a in ((dst_i, dst), (src_i, src)):
                sp.dma_start(t[:, 0:QS - 1, :], a[0:whole].rearrange("(q p e) -> p q e", p=EQR, e=P)).then_inc(edges_in, 16)
                left = (E - whole) // P
                sp.dma_start(t[0:left, QS - 1, :], a[whole:whole + left * P].rearrange("(p e) -> p e", e=P)).then_inc(edges_in, 16)
                tail = E - whole - left * P
                sp.dma_start(t[left:left + 1, QS - 1, 0:tail], a[E - tail:E].rearrange("(o e) -> o e", o=1)).then_inc(edges_in, 16)
            full = (N // P) * P
            sp.dma_start(X[:, 0:N // P, :], x[0:full, :].rearrange("(t p) d -> p t d", p=P)).then_inc(x_in, 16)
            sp.dma_start(X[0:N - full, N // P, :], x[full:N, :]).then_inc(x_in, 16)
            def blocks(w):
                return w.rearrange("(b p) n -> p b n", p=P)

            def everywhere(v):
                return v.rearrange("(o d) -> o d", o=1).broadcast_to([P, D])

            sp.dma_start(w_b[:, :, :], blocks(g1_w)).then_inc(weights_in, 16)
            sp.dma_start(w_c[:, :, 0:D], blocks(g2_w)).then_inc(prep("w_in"), 16)
            sp.dma_start(w_heads[:, :, 0:D], blocks(a_w)).then_inc(prep("w_in"), 16)
            for i, v in enumerate((g2_as, g2_ad, a_as.rearrange("h c -> (h c)"), a_ad.rearrange("h c -> (h c)"))):
                sp.dma_start(att_vec[:, i, :], everywhere(v)).then_inc(prep("w_in"), 16)
            sp.dma_start(row_gate[:, 0, :], e_b2.rearrange("(o d) -> o d", o=1)).then_inc(prep("w_in"), 16)
            rest = prep("rest_in")
            for i in range(2):
                sp.dma_start(w_msg[:, :, i * D:(i + 1) * D], blocks(m_w[i * D:(i + 1) * D, :])).then_inc(rest, 16)
            sp.dma_start(w_a[:, :, :], blocks(e_u1)).then_inc(rest, 16)
            sp.dma_start(w_rbf[:, :], e_w1).then_inc(rest, 16)
            for t, v in ((b_gcn, g1_b), (b_gat, g2_b), (b_msg, m_b), (b_heads, a_b), (b_add, e_c2),
                         (gam_msg, m_gamma), (gam_heads, a_gamma)):
                sp.dma_start(t[:, :], everywhere(v)).then_inc(rest, 16)
            sp.dma_start(row_upd[:, :], m_bu.rearrange("(o d) -> o d", o=1)).then_inc(rest, 16)
            with nc.allow_non_contiguous_dma(reason="two short bias columns"):
                sp.dma_start(b_rbf[:, :], e_b1.rearrange("(b p) -> p b", p=P)).then_inc(rest, 16)
                sp.dma_start(b_u1[:, :], e_c1.rearrange("(b p) -> p b", p=P)).then_inc(rest, 16)
            sp.dma_start(rbf_pad[0:E, :], edge_attr).then_inc(rbf_copied, 16)
            sp.wait_ge(steps_known, 1)
            with nc.allow_non_contiguous_dma(reason="416 step entries"):
                for a in range(2):
                    sp.dma_start(step_table[a, :].rearrange("(q p) -> p q", p=ROWS), step_out[:, a, :]).then_inc(steps_out, 16)
            sp.wait_ge(steps_out, 32)
            sp.dma_start(step_row[:, :, :], step_table.rearrange("(o a) s -> o a s", o=1)).then_inc(steps_in, 16)
            sp.dma_start(jB[:, :], step_table[0:1, :].broadcast_to([P, STEPS])).then_inc(steps_in, 16)
            def store_rows(ph, ready, table, rows_t, width):
                with sp.Fori(0, PAIRS) as it:
                    sp.wait_ge(*ph.at(ready, 2 * it + 2))
                    sp.dma_start(table[bass.ds(it * 2 * P, 2 * P), :].rearrange("(t p) d -> p t d", p=P),
                                 rows_t[:, bass.ds(2 * it, 2), 0:width]).then_inc(ph("stored"), 16)

            store_rows(n0, "out", table_gcn, acc, D)
            sp.wait_ge(*n0.at("mm", 4 * PAIRS))
            sp.dma_start(w_b[:, :, :], blocks(e_u2)).then_inc(rest, 16)
            sp.wait_ge(prep("gate_parts"), 1)
            for i in range(3):
                sp.dma_start(parts_gate[i:i + 1, :], part_gate[:, i, :]).then_inc(rest, 16)
            sp.dma_start(rbf_pad[E:E + P // 2, :], edge_attr[0:P // 2, :]).then_inc(rbf_copied, 16)
            sp.dma_start(rbf_pad[E + P // 2:E + P, :], edge_attr[0:P // 2, :]).then_inc(rbf_copied, 16)
            sp.wait_ge(seg_rows_ready, 1)
            sp.dma_start(slot_rows[1:STEPS * P + 1].rearrange("(q p e) -> p q e", p=ROWS, e=P), seg_rows).then_inc(seg_stored, 16)
            sp.dma_start(slot_rows[0:1].rearrange("(o e) -> o e", o=1), edge_pad[:, 0:1]).then_inc(seg_stored, 16)
            sp.wait_ge(seg_stored, 32)
            sp.dma_start(prev_rows, slot_rows[0:STEPS * P].rearrange("(q p e) -> p q e", p=ROWS, e=P)).then_inc(seg_back, 16)
            sp.wait_ge(reset_ready, 1)
            sp.dma_start(reset_rows[0:STEPS * P].rearrange("(q p e) -> p q e", p=ROWS, e=P), prev_rows).then_inc(reset_stored, 16)
            sp.dma_start(reset_rows[STEPS * P:STEPS * P + P].rearrange("(o e) -> o e", o=1), edge_pad[:, :]).then_inc(reset_stored, 16)
            sp.wait_ge(reset_stored, 32)

            def reset_loads(ph, heads):
                def one(it, b, reused):
                    if reused:
                        sp.wait_ge(*ph.at("scan", 2 * (2 * it + b - 1)))
                    sp.dma_start(reset_b[b][0:heads, :],
                                 reset_rows[bass.ds(it * 2 * SG + b * SG, SG + 1)].rearrange("(o e) -> o e", o=1)
                                 .broadcast_to([heads, SG + 1])).then_inc(ph(f"reset{b}"), 16)
                for b in range(2):
                    one(0, b, False)
                with sp.Fori(1, ROUNDS) as it:
                    for b in range(2):
                        one(it, b, True)

            store_rows(n1, "row", table_gat, H, D + 1)
            reset_loads(g1, 1)
            sp.wait_ge(*n1.at("mm", 4 * PAIRS))
            sp.dma_start(w_c[:, :, 0:D], blocks(e_w2)).then_inc(gate("w_in"), 16)
            store_rows(n2, "xrow", table_gate, H, D)
            sp.wait_ge(rbf_copied, 48)

            def rbf_round(it, first_round):
                e0 = step_values(mybir.EngineType.SP, 1, ROUND * it, ROUND, E)
                for k in range(ROUND):
                    if not first_round:
                        sp.wait_ge(gate("rbf_T"), ROUND * (it - 1) + k + 1)
                    sp.dma_start(rbf_rows[:, k, :], rbf_pad[bass.ds(e0[k], P), :]).then_inc(gate(f"rbf{k // 4}"), 16)
            rbf_round(0, True)
            with sp.Fori(1, ROUNDS) as it:
                rbf_round(it, False)
            sp.wait_ge(bias_added, NT)
            sp.dma_start(b_add[:, :], everywhere(m_beta)).then_inc(n3("w_in"), 16)
            sp.wait_ge(*n3.at("hid", 8 * PAIRS))
            sp.dma_start(w_a[:, :, :], blocks(m_wu)).then_inc(n3("w_in"), 16)
            store_rows(n3b, "row", table_msg, H, D)
            sp.wait_ge(bias_added, 2 * NT)
            sp.dma_start(b_add[:, :], everywhere(a_beta)).then_inc(n4("w_in"), 16)
            store_rows(n4b, "row", table_heads, H, TW)
            reset_loads(g4, HEADS)
            full = N // P
            with sp.Fori(0, full // 2) as it:
                sp.wait_ge(*n5.at("xrow", 2 * it + 2))
                sp.dma_start(out[bass.ds(it * 2 * P, 2 * P), :].rearrange("(t p) d -> p t d", p=P),
                             X[:, bass.ds(2 * it, 2), :]).then_inc(out_stored, 16)
            sp.wait_ge(*n5.at("xrow", full + 1))
            sp.dma_start(out[full * P:N, :], X[0:N - full * P, full, :]).then_inc(out_stored, 16)
            sp.wait_ge(out_stored, 16 * (full // 2 + 1))

        @block.gpsimd
        def _(pool):
            seq = Ordered(pool, pool_seq)
            pool.memset(dst_i[:, QS - 1:QS, :], PAD_DST).then_inc(pads_set, 1)
            pool.memset(src_i[:, QS - 1:QS, :], 0).then_inc(pads_set, 1)
            pool.memset(X[:, N // P:NT, :], 0.0).then_inc(pads_set, 1)
            pool.memset(edge_pad[:, :], -BIG).then_inc(pads_set, 1)
            pool.memset(E_col[:, EC:EW], float(PAD_DST * CODE)).then_inc(consts, 1)
            pool.memset(ones[:, :], 1.0).then_inc(consts, 1)
            pool.memset(ones_bf[:, :], 1.0).then_inc(consts, 1)
            seq.done(pool.memset(ident[:, :], 0.0))
            pool.affine_select(out=ident[:, :], in_=ident[:, :], compare_op=ALU.not_equal, fill=1.0,
                               base=0, pattern=[[-1, P]], channel_multiplier=1).then_inc(consts, 1)
            pool.iota(iota_row[:, :], pattern=[[1, P]], base=0, channel_multiplier=0,
                      allow_small_or_imprecise_dtypes=True).then_inc(consts, 1)
            pool.iota(iota_bf[:, :], pattern=[[1, P]], base=0, channel_multiplier=0,
                      allow_small_or_imprecise_dtypes=True).then_inc(consts, 1)
            pool.iota(diff[:, :], pattern=[[1, P]], base=0, channel_multiplier=-1,
                      allow_small_or_imprecise_dtypes=True).then_inc(consts, 1)
            pool.iota(step_i[:, :], pattern=[[ROWS, QS]], base=0, channel_multiplier=1).then_inc(consts, 1)

            def times_gamma(ph, t_in, gamma):
                with pool.Fori(0, NT) as t:
                    pool.wait_ge(*ph.at("normed", t + 1))
                    pool.tensor_tensor(t_in[:, bass.ds(t, 1), 0:D], t_in[:, bass.ds(t, 1), 0:D],
                                       gamma[:, :].unsqueeze(1), ALU.mult).then_inc(ph("gamma"), 1)

            def gather_rounds(ph, table, width, per, places, biased=False):
                turns = len(places)
                tiles = NT * per * turns // STEPS

                def turn(it, first_turn):
                    for b, place in enumerate(places):
                        if not first_turn:
                            pool.wait_ge(*ph.at("mm", per * (turns * (it - 1) + b + 1)))
                        pool.tensor_copy(idx[:, b * per:(b + 1) * per],
                                         srcI[:, bass.ds(per * (turns * it + b), per)]).then_inc(ph("idx_ready"), 1)
                        pool.wait_ge(*ph.at("idx_ready", turns * it + b + 1))
                        pool.sem_inc(ph("go"), 1)
                        for k in range(per):
                            pool.indirect_dma_start(
                                out=place[:, k, 0:width], out_offset=None, in_=table,
                                in_offset=bass.IndirectOffsetOnAxis(ap=idx[:, b * per + k:b * per + k + 1], axis=0)
                            ).then_inc(ph(f"rows{b}"), 16)
                    if biased:
                        for k in range(tiles):
                            pool.tensor_tensor(X[:, bass.ds(tiles * it + k, 1), :], X[:, bass.ds(tiles * it + k, 1), :],
                                               b_add[:, :].unsqueeze(1), ALU.add).then_inc(bias_added, 1)
                turn(0, True)
                with pool.Fori(1, STEPS // (per * turns)) as it:
                    turn(it, False)

            fours = [G[:, 4 * q:4 * q + 4, :] for q in range(4)]

            pool.wait_ge(*n0.at("stored", 16 * PAIRS))
            pool.wait_ge(slots_ready, 1)
            gather_rounds(g0, table_gcn, D, 4, fours)
            pool.wait_ge(*n1.at("agg", NT))
            pool.memset(acc[:, :, :], 0.0).then_inc(acc_cleared, 1)
            pool.wait_ge(*g0.at("mm", STEPS))
            pool.wait_ge(*n1.at("stored", 16 * PAIRS))
            gather_rounds(g1, table_gat, D + 1, GROUP, G_b)
            with pool.Fori(0, NT) as t:
                pool.wait_ge(*n2.at("own", t + 1))
                pool.tensor_tensor(H[:, bass.ds(t, 1), 0:D], H[:, bass.ds(t, 1), 0:D], b_gat[:, :].unsqueeze(1),
                                   ALU.add).then_inc(n2("own_biased"), 1)
            pool.wait_ge(*n2.at("var", 1))
            pool.memset(acc[:, :, 0:D], 0.0).then_inc(acc_cleared, 1)
            pool.wait_ge(*g1.at("mm", STEPS))
            pool.wait_ge(*n2.at("xrow", NT))
            pool.wait_ge(*n2.at("stored", 16 * PAIRS))
            pool.wait_ge(prep("rest_in"), REST)
            gather_rounds(g2, table_gate, D, 4, fours, True)
            pool.wait_ge(*n3.at("agg", PAIRS))
            pool.memset(acc[:, :, 0:D], 0.0).then_inc(acc_cleared, 1)
            pool.wait_ge(*g2.at("mm", STEPS))
            pool.wait_ge(*n3.at("w_in", 32))
            pool.wait_ge(*n3b.at("h", NT))
            pool.wait_ge(*n3b.at("stored", 16 * PAIRS))
            gather_rounds(g3, table_msg, D, 4, fours, True)
            pool.wait_ge(*n4.at("agg", NT))
            pool.memset(acc[:, :, :], 0.0).then_inc(acc_cleared, 1)
            times_gamma(n4, H, gam_msg)
            pool.wait_ge(*g3.at("mm", STEPS))
            pool.wait_ge(*n4.at("w_in", 16))
            pool.wait_ge(*n4b.at("h", NT))
            pool.wait_ge(*n4b.at("stored", 16 * PAIRS))
            gather_rounds(g4, table_heads, TW, GROUP, G_b, True)
            times_gamma(n5, acc, gam_heads)

        @block.scalar
        def _(act):
            seq = Ordered(act, act_seq)
            def evac_tile(ph, t, k, func, reused, also=None):
                act.wait_ge(*ph.at("tr", 2 * t + 2))
                if reused:
                    act.wait_ge(*ph.at("mm", 2 * t - 2))
                    if also is not None:
                        act.wait_ge(*ph.at(also, t - 1))
                nc.scalar.activation(HTs[:, k, :, :].rearrange("p b c -> p (b c)"), banks[2 + k][:, 0:D],
                                     func).then_inc(ph("ht"), 1)

            def norm_row(ph, t, k, reused, also=None):
                if reused:
                    act.wait_ge(*ph.at("tr", 2 * t - 2))
                    if also is not None:
                        act.wait_ge(*ph.at(also, t - 1))
                nc.scalar.activation(rows[:, k:k + 1, :], X[:, bass.ds(t, 1), :], ACT.Relu,
                                     bias=nmr[:, bass.ds(t, 1)], scale=rstd[:, bass.ds(t, 1)]).then_inc(ph("h"), 1)

            def product_rows(ph, func, width, own_rows, also=None, to=H):
                if own_rows:
                    for k in range(2):
                        norm_row(ph, k, k, False)
                evac_tile(ph, 0, 0, func, False)

                def tile(t, k, first_pair, last_pair):
                    if not (last_pair and k == 1):
                        evac_tile(ph, t + 1, 1 - k, func, not (first_pair and k == 0), also)
                    if own_rows and not last_pair:
                        norm_row(ph, t + 2, k, True)
                    act.wait_ge(*ph.at("mm", 2 * t + 2))
                    nc.scalar.activation(to[:, bass.ds(t, 1), 0:width], banks[4 + k][:, 0:width].unsqueeze(1),
                                         ACT.Copy).then_inc(ph("row"), 1)
                tile_rounds(act, tile)

            def attention_phase(ph, heads, scores=None):
                w = 2 * heads
                ade = att[:, 0:2 * HEADS * GROUP].rearrange("p (k c) -> p k c", k=GROUP)
                expo = att[:, 384:384 + 2 * heads * GROUP].rearrange("p (a k h) -> p a k h", a=2, k=GROUP)
                ex1 = att[:, 512:512 + heads * GROUP].rearrange("p (k h) -> p k h", k=GROUP)

                def evacs(g, b):
                    for h in range(2):
                        act.wait_ge(*ph.at("oh_tr", GROUP * g + 4 * h + 4))
                        nc.scalar.activation(onehotT_b[b % 2][:, 4 * h:4 * h + 4, :],
                                             banks[h].rearrange("p (k n) -> p k n", k=4), ACT.Copy).then_inc(ph("oh_evac"), 1)

                def copy_ad(g):
                    act.wait_ge(*ph.at("ad_mm", GROUP * (g + 1)))
                    nc.scalar.activation(ade[:, :, 0:w], banks[6][:, 0:16 * GROUP].rearrange("p (k c) -> p k c", k=GROUP)[:, :, 0:w],
                                         ACT.Copy).then_inc(ph("ad_copy"), 1)

                def scales(g, b, low, high):
                    for k in range(low, high):
                        nc.scalar.activation(G_b[b][:, k, 0:D], G_b[b][:, k, 0:D], ACT.Identity,
                                             scale=G_b[b][:, k, D:D + 1]).then_inc(ph("act_scaled"), 1)

                def onehots(g, b):
                    for k in range(GROUP):
                        nc.scalar.activation(onehot_b[b][:, k, :], iota_row[:, :], ACT.Abs,
                                             bias=dloc[:, bass.ds(GROUP * g + k, 1)], scale=-1.0).then_inc(ph("away"), 1)
                    act.wait_ge(*ph.at("away", GROUP * (g + 1)))
                    nc.scalar.activation(onehot_b[b], onehot_b[b], ACT.Relu, bias=ones[:, 0:1],
                                         scale=-1.0).then_inc(ph("act_onehot"), 1)

                if heads > 1:
                    act.wait_ge(*scores)
                    for g in range(2):
                        onehots(g, g)
                evacs(0, 0)
                copy_ad(0)

                def turn(it, first_turn, last_turn):
                    for b in range(LIVE):
                        g = LIVE * it + b
                        act.wait_ge(*ph.at("small", g + 1))
                        nc.scalar.activation(G_b[b][:, :, D:D + heads], expo[:, 0, :, :], ACT.Exp).then_inc(ph("ex"), 1)
                        nc.scalar.activation(ex1, expo[:, 1, :, :], ACT.Exp).then_inc(ph("ex"), 1)
                        act.wait_ge(*ph.at("rho_in", g + 1))
                        nc.scalar.activation(att[0:1, 600:600 + heads], att[0:1, 592:592 + heads], ACT.Exp).then_inc(ph("rho_ex"), 1)
                        if not (last_turn and b == LIVE - 1):
                            evacs(g + 1, b + 1)
                        if heads == 1:
                            act.wait_ge(*ph.at("ex", 2 * g + 2))
                            scales(g, b, 0, GROUP // 2)
                        if not (last_turn and b == LIVE - 1):
                            copy_ad(g + 1)
                        if heads == 1:
                            scales(g, b, GROUP // 2, GROUP)
                        elif not (last_turn and b >= LIVE - 2):
                            if not first_turn:
                                act.wait_ge(*ph.at("mm", GROUP * (g - 1)))
                            onehots(g + 2, (b + 2) % LIVE)
                rounds(act, turn, TURNS)

            norm_sqrt(act, n0)
            act.wait_ge(*n0.at("rstd", 1))
            product_rows(n0, ACT.Copy, D, True, to=acc)
            act.wait_ge(deg_ready, 1)
            nc.scalar.activation(dinv[:, :], tb[:, 2, :], ACT.Sqrt).then_inc(dinv_ready, 1)

            product_rows(n1, ACT.Relu, D + 1, False)
            attention_phase(g1, 1)

            act.wait_ge(*n2.at("shares", 1))
            with act.Fori(0, NT) as t:
                nc.scalar.activation(H[:, bass.ds(t, 1), 0:D], H[:, bass.ds(t, 1), 0:D], ACT.Identity,
                                     scale=w_self[:, bass.ds(t, 1), 0:1].rearrange("p a c -> p (a c)")).then_inc(n2("own"), 1)
            norm_sqrt(act, n2)
            act.wait_ge(*n2.at("rstd", 1))
            for k in range(2):
                norm_row(n2, k, k, False)

            def n2_tile(t, k, first_pair, last_pair):
                act.wait_ge(*n2.at("tr", 2 * t + 2))
                nc.scalar.activation(HT[:, bass.ds(t, 1), :, :].rearrange("p a b c -> p (a b c)"), banks[2 + k][:, 0:D],
                                     ACT.Copy).then_inc(n2("ht"), 1)
                if not last_pair:
                    norm_row(n2, t + 2, k, True, "xrow")
            tile_rounds(act, n2_tile)

            act.wait_ge(prep("rest_in"), REST)

            def cols(j, q):
                act.wait_ge(gate("rbf_T"), 4 * j + 4)
                nc.scalar.activation(rbf_cols[q % 2], banks[0][0:RBF, :], ACT.Copy).then_inc(gate("cols"), 1)

            def silus(j, q):
                for h in range(2):
                    act.wait_ge(gate("hid_mm"), 2 * j + h + 1)
                    nc.scalar.activation(hidden[q % 2][:, h, :], banks[2 + h], ACT.Silu,
                                         bias=b_rbf[:, h:h + 1]).then_inc(gate("hid"), 1)

            def tanhs(j, q, reused):
                for k in range(4):
                    if reused and k == 0:
                        act.wait_ge(gate("gated"), 4 * j - 4)
                    act.wait_ge(gate("gate_mm"), 4 * j + k + 1)
                    nc.scalar.activation(gates[q % 2][:, k, :], banks[6 + k % 2][:, 0:D], ACT.Tanh,
                                         scale=0.5).then_inc(gate("gate"), 1)

            cols(0, 0)
            cols(1, 1)
            silus(0, 0)

            def gate_round(it, first_round, last_round):
                for q in range(4):
                    j = 4 * it + q
                    if not (last_round and q >= 2):
                        cols(j + 2, q)
                    if not (last_round and q == 3):
                        silus(j + 1, q + 1)
                    tanhs(j, q, not (first_round and q < 2))
            rounds(act, gate_round, ROUNDS)

            def n3_pair(it, first_pair, last_pair):
                act.wait_ge(*n3.at("tr", 4 * it + 4))
                if not first_pair:
                    act.wait_ge(*n3.at("hid", 8 * it))
                nc.scalar.activation(HTs.rearrange("p a b c -> p (a b c)"), banks[3], ACT.Copy).then_inc(n3("ht"), 1)
                if not first_pair:
                    act.wait_ge(*n3.at("mm", 4 * it))
                for h in range(2):
                    act.wait_ge(*n3.at("hid", 8 * it + 4 * h + 4))
                    nc.scalar.activation(upd_T[:, h, :], banks[1 + h][:, 0:2 * P], ACT.Silu,
                                         bias=b_u1[:, h:h + 1]).then_inc(n3("act"), 1)
            rounds(act, n3_pair, PAIRS)

            norm_sqrt(act, n3b)
            act.wait_ge(*n3b.at("rstd", 1))
            product_rows(n3b, ACT.Copy, D, True, "kept")

            def msg_evac(j, q):
                act.wait_ge(*g3.at("oh_tr", 4 * j + 4))
                nc.scalar.activation(onehotT_msg[:, (4 * q) % ROUND:(4 * q) % ROUND + 4, :],
                                     banks[2].rearrange("p (k n) -> p k n", k=4), ACT.Copy).then_inc(g3("oh_evac"), 1)
            act.wait_ge(*n3b.at("stored", 16 * PAIRS))
            msg_evac(0, 0)

            def msg_round(it, first_round, last_round):
                for q in range(4):
                    j = 4 * it + q
                    if not (last_round and q == 3):
                        msg_evac(j + 1, q + 1)
                    act.wait_ge(*g3.at("sum", 2 * j + 2))
                    nc.scalar.activation(G[:, 4 * q:4 * q + 4, 0:D], G[:, 4 * q:4 * q + 4, 0:D], ACT.Relu).then_inc(g3("relu"), 1)
            rounds(act, msg_round, ROUNDS)

            def n4_evac(t, k, reused):
                act.wait_ge(*n4.at("tr", 2 * t + 2))
                if reused:
                    act.wait_ge(*n4.at("mm", 5 * t - 5))
                nc.scalar.activation(HTs[:, k, :, :].rearrange("p b c -> p (b c)"), banks[2 + k][:, 0:D],
                                     ACT.Copy).then_inc(n4("ht"), 1)
                nc.scalar.activation(rows[:, k, :], HT[:, bass.ds(t, 1), :, :].rearrange("p a b c -> p (a b c)"),
                                     ACT.Copy).then_inc(n4("ht"), 1)
            n4_evac(0, 0, False)

            def n4_tile(t, k, first_pair, last_pair):
                if not (last_pair and k == 1):
                    n4_evac(t + 1, 1 - k, not (first_pair and k == 0))
                act.wait_ge(*n4.at("mm", 5 * t + 5))
                nc.scalar.activation(H[:, bass.ds(t, 1), 0:D], banks[4 + k][:, 0:D].unsqueeze(1),
                                     ACT.Relu).then_inc(n4("row"), 1)
            tile_rounds(act, n4_tile)

            def normalise(ph, t_in, width):
                act.wait_ge(*ph.at("rstd", 1))
                with act.Fori(0, NT) as t:
                    nc.scalar.activation(t_in[:, bass.ds(t, 1), 0:width], t_in[:, bass.ds(t, 1), 0:width], ACT.Identity,
                                         bias=nmr[:, bass.ds(t, 1)], scale=rstd[:, bass.ds(t, 1)]).then_inc(ph("normed"), 1)
            norm_sqrt(act, n4)
            normalise(n4, H, D)

            norm_sqrt(act, n4b)
            act.wait_ge(*n4b.at("rstd", 1))
            product_rows(n4b, ACT.Copy, TW, True)
            attention_phase(g4, HEADS, n4b.at("nd", NT))
            norm_sqrt(act, n5)
            normalise(n5, acc, D)

        @block.tensor
        def _(pe):
            pe.wait_ge(consts, 8)
            pe.wait_ge(codes, 1)
            for q in range(QS):
                nc.tensor.transpose(banks[0][:, q * P:q * P + EQR], code_rows[:, q, :], ident[0:EQR, 0:EQR]).then_inc(codes_T, 1)

            def hist(it, first_round):
                for b in range(2):
                    if not first_round:
                        pe.wait_ge(hist_add, 2 * it + b - 1)
                    pe.wait_ge(hist_oh, (2 * it + b + 1) * (HB + 1))
                    for c in range(HB):
                        nc.tensor.matmul(banks[1 - b][:, 0:NT], oh_lo[:, b, c, :], oh_hi[:, b, c, :],
                                         start=c == 0, stop=c == HB - 1).then_inc(hist_mm, 1)
            pe.wait_ge(weights_in, 16)

            def transposes(ph, t, k, ready, source, reused):
                pe.wait_ge(*ph.at(ready, t + 1))
                if reused:
                    pe.wait_ge(*ph.at("ht", t - 1))
                for c in range(2):
                    nc.tensor.transpose(banks[2 + k][:, c * P:(c + 1) * P], source[:, k, c * P:(c + 1) * P],
                                        ident[:, :]).then_inc(ph("tr"), 1)

            def node_products(ph, w, width, ready, readers, meanwhile=None):
                transposes(ph, 0, 0, ready, rows, False)

                def tile(t, k, first_pair, last_pair):
                    if meanwhile is not None:
                        meanwhile(t)
                    if not (last_pair and k == 1):
                        transposes(ph, t + 1, 1 - k, ready, rows, not (first_pair and k == 0))
                    pe.wait_ge(*ph.at("ht", t + 1))
                    if not first_pair:
                        for what in readers:
                            pe.wait_ge(*ph.at(what, t - 1))
                    for c in range(2):
                        nc.tensor.matmul(banks[4 + k][:, 0:width], HTs[:, k, c, :], w[:, c, 0:width],
                                         start=c == 0, stop=c == 1).then_inc(ph("mm"), 1)
                tile_rounds(pe, tile)
            ahead = HROUNDS - NT
            for it in range(ahead):
                hist(it, it == 0)
            node_products(n0, w_b, D, "h", ("row",), lambda t: hist(t + ahead, False))
            pe.wait_ge(counts, 1)
            nc.tensor.matmul(banks[0][:, 0:NT], ones[:, :], tb[:, 0, :], start=True, stop=True).then_inc(totals, 1)

            pe.wait_ge(tiles_known, 1)

            def shift_pair(it, first_pair, last_pair):
                q = nc.values_load_multi_w_load_instructions(
                    tile_i[0:1, 0, bass.ds(2 * it, 2)], engines=[mybir.EngineType.PE], min_val=0, max_val=ECOLS,
                    skip_runtime_bounds_check_because="a tile's first edge is one of the edges, or their end")[1]
                for k in range(2):
                    t = 2 * it + k
                    if not first_pair:
                        pe.wait_ge(slots_copied, t - 1)
                    pe.wait_ge(shift_ready, 2 * t + 2)
                    for a in range(2):
                        nc.tensor.matmul(banks[6 + k][:, 0:ECOLS], shift[:, k, a, :], E_col[:, bass.ds(q[k] + a, ECOLS)],
                                         start=a == 0, stop=a == 1).then_inc(shifted, 1)
            rounds(pe, shift_pair, PAIRS)

            pe.wait_ge(seg_ready, 1)
            for q in range(QS):
                nc.tensor.transpose(banks[0][0:ROWS, q * P:(q + 1) * P], tmp_a[:, q * ROWS:(q + 1) * ROWS], ident[:, :]).then_inc(seg_T, 1)
            pe.wait_ge(reset_ready, 1)
            for q in range(QS):
                nc.tensor.transpose(banks[1][:, q * ROWS:(q + 1) * ROWS], seg_rows[:, q, :], ident[0:ROWS, 0:ROWS]).then_inc(first_T, 1)

            def scatter(it, k, ph, first_round):
                if not (first_round and k < 2):
                    pe.wait_ge(*ph.at("added", ROUND * it + k - 1))
                nc.tensor.matmul(banks[4 + k % 2][:, 0:D], onehot[:, k, :], G[:, k, 0:D],
                                 start=True, stop=True).then_inc(ph("mm"), 1)

            def gcn_round(it, first_round, last_round):
                for k in range(ROUND):
                    if k % 4 == 0:
                        pe.wait_ge(*g0.at(f"rows{k // 4}", 64 * it + 64))
                        pe.wait_ge(*g0.at("onehot", ROUND * it + k + 4))
                    scatter(it, k, g0, first_round)
            rounds(pe, gcn_round, ROUNDS)

            def attention_phase(ph, heads, scores):
                w = 2 * heads

                def targets(g, b, reused, sums_before, midway=None):
                    if heads == 1:
                        pe.wait_ge(*ph.at("onehot", GROUP * (g + 1)))
                    else:
                        pe.wait_ge(*ph.at("act_onehot", g + 1))
                    for k in range(GROUP):
                        if reused and k % 4 == 0:
                            pe.wait_ge(*ph.at("oh_evac", 2 * g - 1 + k // 4))
                            if sums_before:
                                pe.wait_ge(*ph.at("added", GROUP * (g - 2) + 5 + k // 4))
                        nc.tensor.transpose(banks[k // 4][:, (k % 4) * P:(k % 4 + 1) * P], onehot_b[b][:, k, :],
                                            ident[:, :]).then_inc(ph("oh_tr"), 1)
                    tile_of = step_values(mybir.EngineType.PE, 0, GROUP * g, GROUP, NT - 1)
                    if reused:
                        pe.wait_ge(*ph.at("ad_copy", g))
                    for k in range(GROUP):
                        if k == GROUP // 2 and midway is not None:
                            midway()
                        if k % 4 == 0:
                            pe.wait_ge(*ph.at("oh_evac", 2 * g + 1 + k // 4))
                        nc.tensor.matmul(banks[6][:, 16 * k:16 * k + w], onehotT_b[b % 2][:, k, :],
                                         nd[:, bass.ds(tile_of[k], 1), 0:w].rearrange("p a c -> p (a c)"),
                                         start=True, stop=True).then_inc(ph("ad_mm"), 1)

                def sources(turn_of, g, b, reused):
                    pe.wait_ge(*ph.at(f"rows{b}", GROUP * 16 * (turn_of + 1)))
                    if reused:
                        pe.wait_ge(*ph.at("scan", 2 * g))
                    for k in range(GROUP):
                        nc.tensor.transpose(PS[0:heads, 2 + k // 4, (k % 4) * P:(k % 4 + 1) * P], G_b[b][:, k, D:D + heads],
                                            ident[:, :]).then_inc(ph("as_tr"), 1)

                def sums(g, b, first_group):
                    if heads == 1:
                        pe.wait_ge(*ph.at("own_col", g + 1))
                    for k in range(GROUP):
                        pe.wait_ge(*ph.at("act_scaled" if heads == 1 else "scaled", GROUP * g + k + 1))
                        if not (first_group and k < 4):
                            pe.wait_ge(*ph.at("added", GROUP * g + k - 3))
                        nc.tensor.matmul(banks[SUM_BANKS[k % 4]][:, 0:D + w], onehot_b[b][:, k, :],
                                         G_b[b][:, k, 0:D + w], start=True, stop=True).then_inc(ph("mm"), 1)

                def maxima(g, b, reused):
                    pe.wait_ge(*ph.at("scan", 2 * (g + 1)))
                    if reused:
                        pe.wait_ge(*ph.at("rho_in", g))
                    pe.sem_inc(pe_go, 1)
                    for k in range(GROUP):
                        nc.tensor.transpose(banks[7][:, 16 * k:16 * k + heads], both[0:heads, k * P:(k + 1) * P],
                                            ident[0:heads, 0:heads]).then_inc(ph("max_tr"), 1)
                    nc.tensor.transpose(banks[7][0:1, 128:128 + heads], fwd_b[1 - b % 2][0:heads, SG - 1:SG],
                                        ident[0:heads, 0:heads]).then_inc(ph("max_tr"), 1)

                def rescale(g, b):
                    pe.wait_ge(*ph.at("rho", g + 1))
                    nc.tensor.matmul(banks[7][:, 160:160 + heads], onehot_b[b][0:1, 0, :], att[0:1, 608:608 + heads],
                                     start=True, stop=True).then_inc(ph("rho_mm"), 1)

                pe.wait_ge(*scores)
                sources(0, 0, 0, False)
                targets(0, 0, False, False)
                maxima(0, 0, False)
                sources(0, 1, 1, True)

                def turn(it, first_turn, last_turn):
                    for b in range(LIVE):
                        g = LIVE * it + b
                        last_group = last_turn and b == LIVE - 1
                        if not last_group:
                            targets(g + 1, (b + 1) % LIVE, True, not (first_turn and b == 0),
                                    lambda: rescale(g, b))
                        else:
                            rescale(g, b)
                        sums(g, b, first_turn and b == 0)
                        if not last_group:
                            pe.wait_ge(*ph.at("rescale", g + 1))
                            maxima(g + 1, (b + 1) % LIVE, True)
                        if not (last_turn and b >= LIVE - 2):
                            sources(it + (b + 2) // LIVE, g + 2, (b + 2) % LIVE, True)
                rounds(pe, turn, TURNS)

            pe.wait_ge(prep("w_ready"), 2)
            node_products(n1, w_c, D + 2, "agg", ("row", "nd"))
            attention_phase(g1, 1, n1.at("nd", NT))

            tile_rounds(pe, lambda t, k, first_pair, last_pair: transposes(n2, t, k, "h", rows, not first_pair))

            pe.wait_ge(prep("rest_in"), REST)
            pe.wait_ge(gate("w_in"), 16)

            def rbf_T(it, q, j, reused):
                pe.wait_ge(gate(f"rbf{q}"), 64 * (it + 1))
                if reused:
                    pe.wait_ge(gate("cols"), j)
                pe.sem_inc(pe_go, 1)
                for k in range(4):
                    nc.tensor.transpose(banks[0][0:RBF, k * P:(k + 1) * P], rbf_rows[:, 4 * q + k, :],
                                        ident[:, :]).then_inc(gate("rbf_T"), 1)

            def hid_mm(j, q, reused):
                pe.wait_ge(gate("cols"), j + 1)
                for h in range(2):
                    if reused:
                        pe.wait_ge(gate("hid"), 2 * j - 1 + h)
                    nc.tensor.matmul(banks[2 + h], w_rbf[:, h * P:(h + 1) * P], rbf_cols[q % 2],
                                     start=True, stop=True).then_inc(gate("hid_mm"), 1)

            def gate_mm(j, q, k, reused):
                if reused or k >= 2:
                    pe.wait_ge(gate("gate"), 4 * j + k - 1)
                for h in range(2):
                    nc.tensor.matmul(banks[6 + k % 2][:, 0:D], hidden[q % 2][:, h, k * P:(k + 1) * P],
                                     w_c[:, h, 0:D], start=h == 0, stop=False)
                nc.tensor.matmul(banks[6 + k % 2][:, 0:D], ones_bf[:, :], parts_gate[:, :],
                                 start=False, stop=True).then_inc(gate("gate_mm"), 1)

            rbf_T(0, 0, 0, False)
            rbf_T(0, 1, 1, True)
            hid_mm(0, 0, False)

            def gate_round(it, first_round, last_round):
                for q in range(4):
                    j = 4 * it + q
                    if not (last_round and q >= 2):
                        rbf_T(it + (q + 2) // 4, (q + 2) % 4, j + 2, True)
                    if not (last_round and q == 3):
                        hid_mm(j + 1, q + 1, True)
                    pe.wait_ge(gate("hid"), 2 * j + 2)
                    for k in range(4):
                        gate_mm(j, q, k, not (first_round and q == 0))
                        if not (first_round and q == 0):
                            back = (q - 1) % 4
                            if k == 0:
                                pe.wait_ge(gate("gated"), 4 * j)
                            scatter(it if q else it - 1, 4 * back + k, g2, first_round and q == 1)
            rounds(pe, gate_round, ROUNDS)
            pe.wait_ge(gate("gated"), STEPS)
            for k in range(4):
                scatter(ROUNDS - 1, 12 + k, g2, False)

            def n3_turned(it, reused):
                pe.wait_ge(*n3.at("agg", it + 1))
                if reused:
                    pe.wait_ge(*n3.at("ht", it))
                for k in range(2):
                    for c in range(2):
                        nc.tensor.transpose(banks[3][:, (2 * k + c) * P:(2 * k + c + 1) * P],
                                            rows[:, k, c * P:(c + 1) * P], ident[:, :]).then_inc(n3("tr"), 1)

            def n3_hidden(it, reused):
                pe.wait_ge(*n3.at("ht", it + 1))
                for h in range(2):
                    if reused:
                        pe.wait_ge(*n3.at("act", 2 * it - 1 + h))
                    for c in range(4):
                        moving = (HT[:, bass.ds(2 * it, 2), c, :] if c < 2 else HTs[:, :, c - 2, :])
                        nc.tensor.matmul(banks[1 + h][:, 0:2 * P], w_a[:, c, h * P:(h + 1) * P], moving,
                                         start=c == 0, stop=c == 3).then_inc(n3("hid"), 1)
            n3_turned(0, False)
            n3_hidden(0, False)

            def n3_pair(it, first_pair, last_pair):
                if not last_pair:
                    n3_turned(it + 1, True)
                pe.wait_ge(*n3.at("act", 2 * it + 2))
                for k in range(2):
                    if not first_pair:
                        pe.wait_ge(*n3.at("out", 2 * it - 1 + k))
                    for h in range(2):
                        nc.tensor.matmul(banks[4 + k][:, 0:D], upd_T[:, h, k * P:(k + 1) * P], w_b[:, h, :],
                                         start=h == 0, stop=h == 1).then_inc(n3("mm"), 1)
                if not last_pair:
                    n3_hidden(it + 1, True)
            rounds(pe, n3_pair, PAIRS)
            node_products(n3b, w_msg, 2 * D, "h", ("row", "out"))

            def msg_T(j, q, reused):
                pe.wait_ge(*g3.at("onehot", 4 * j + 4))
                if reused:
                    pe.wait_ge(*g3.at("oh_evac", j))
                for k in range(4):
                    nc.tensor.transpose(banks[2][:, k * P:(k + 1) * P], onehot[:, (4 * q + k) % ROUND, :],
                                        ident[:, :]).then_inc(g3("oh_tr"), 1)

            def msg_q(j, q, tile_of, reused):
                pe.wait_ge(*g3.at("oh_evac", j + 1))
                for k in range(4):
                    if reused and k % 2 == 0:
                        pe.wait_ge(*g3.at("sum", 2 * j - 1 + k // 2))
                    nc.tensor.matmul(banks[k // 2][:, (k % 2) * D:(k % 2 + 1) * D], onehotT_msg[:, 4 * q + k, :],
                                     Q[:, bass.ds(tile_of[4 * q + k] * D, D)], start=True, stop=True).then_inc(g3("qmm"), 1)
            msg_T(0, 0, False)

            def msg_round(it, first_round, last_round):
                tile_of = step_values(mybir.EngineType.PE, 0, ROUND * it, ROUND, NT - 1)
                for q in range(4):
                    j = 4 * it + q
                    if not (last_round and q == 3):
                        msg_T(j + 1, q + 1, True)
                    msg_q(j, q, tile_of, not (first_round and q == 0))
                    if not (first_round and q == 0):
                        back = (q - 1) % 4
                        pe.wait_ge(*g3.at("relu", j))
                        for k in range(4):
                            scatter(it if q else it - 1, 4 * back + k, g3, first_round and q == 1)
            rounds(pe, msg_round, ROUNDS)
            pe.wait_ge(*g3.at("relu", STEPS // 4))
            for k in range(4):
                scatter(ROUNDS - 1, 12 + k, g3, False)

            pe.wait_ge(*n3.at("w_in", 32))

            def n4_turned(t, k, reused):
                pe.wait_ge(*n4.at("agg", t + 1))
                if reused:
                    pe.wait_ge(*n4.at("ht", 2 * t - 2))
                for c in range(2):
                    nc.tensor.transpose(banks[2 + k][:, c * P:(c + 1) * P], G[:, k, c * P:(c + 1) * P],
                                        ident[:, :]).then_inc(n4("tr"), 1)
            n4_turned(0, 0, False)

            def n4_tile(t, k, first_pair, last_pair):
                if not (last_pair and k == 1):
                    n4_turned(t + 1, 1 - k, not (first_pair and k == 0))
                pe.wait_ge(*n4.at("ht", 2 * t + 2))
                if not first_pair:
                    pe.wait_ge(*n4.at("row", t - 1))
                nc.tensor.matmul(banks[4 + k][:, 0:D], ones[0:1, :], row_upd[:, :], start=True, stop=False).then_inc(n4("mm"), 1)
                for c in range(4):
                    still = rows[:, k, c * P:(c + 1) * P] if c < 2 else HTs[:, k, c - 2, :]
                    nc.tensor.matmul(banks[4 + k][:, 0:D], still, w_a[:, c, :], start=False, stop=c == 3).then_inc(n4("mm"), 1)
            tile_rounds(pe, n4_tile)
            node_products(n4b, w_heads, GW, "h", ("row", "nd"))
            attention_phase(g4, HEADS, n4b.at("nd", NT))

        @block.vector
        def _(dve):
            seq = Ordered(dve, dve_seq)
            CNT, DEG, REC, TOT, INC, BEG, NUM, SIN, STA, CCC, DLT, RMD = range(12)
            dve.wait_ge(edges_in, 16 * 6)
            seq.done(nc.vector.tensor_copy(dst_f, dst_i[:, :, :]))
            seq.done(nc.vector.tensor_copy(src_f, src_i[:, :, :]))
            nc.vector.scalar_tensor_tensor(out=code_rows, in0=dst_f, scalar=float(CODE), in1=src_f,
                                           op0=ALU.mult, op1=ALU.add).then_inc(codes, 1)
            dve.wait_ge(codes_T, QS)
            for q in range(QS):
                seq.done(nc.vector.tensor_copy(E_col[:, q * EQR:(q + 1) * EQR], banks[0][:, q * P:q * P + EQR]))
            seq.done(nc.vector.tensor_copy(col_i[:, :], E_col[:, 0:EC]))
            seq.done(nc.vector.tensor_scalar(col_j[:, :], col_i[:, :], 19, None, ALU.logical_shift_right))
            seq.done(nc.vector.tensor_copy(hi_f, col_j[:, :]))
            seq.done(nc.vector.tensor_scalar(col_j[:, :], col_i[:, :], 12, 127, ALU.logical_shift_right, ALU.bitwise_and))
            seq.done(nc.vector.tensor_copy(lo_f, col_j[:, :]))
            seq.done(nc.vector.memset(tb[:, CNT, :], 0.0))
            dve.wait_ge(consts, 8)

            dve.wait_ge(x_in, 32)
            norm_stats(seq, X, n0)

            def hist(it, first_round):
                for b in range(2):
                    c0 = (2 * it + b) * HB
                    if not first_round:
                        dve.wait_ge(hist_mm, HB * (2 * it + b - 1))
                    for c in range(HB):
                        nc.vector.tensor_scalar(oh_lo[:, b, c, :], iota_bf[:, :], lo_f[:, bass.ds(c0 + c, 1)], None,
                                                ALU.is_equal).then_inc(hist_oh, 1)
                    nc.vector.tensor_tensor(oh_hi[:, b, :, :], iota_row[:, 0:NT].unsqueeze(1).broadcast_to([P, HB, NT]),
                                            hi_f[:, bass.ds(c0, HB)].unsqueeze(2).broadcast_to([P, HB, NT]),
                                            ALU.is_equal).then_inc(hist_oh, 1)
                    if not (first_round and b == 0):
                        dve.wait_ge(hist_mm, HB * (2 * it + b))
                        if not (first_round and b < 2):
                            dve.wait_ge(hist_add, 2 * it + b - 1)
                        nc.vector.tensor_tensor(tb[:, CNT, :], tb[:, CNT, :], banks[b][:, 0:NT], ALU.add).then_inc(hist_add, 1)
            hist(0, True)
            with dve.Fori(1, HROUNDS) as it:
                hist(it, False)
            dve.wait_ge(hist_mm, HB * 2 * HROUNDS)
            dve.wait_ge(hist_add, 2 * HROUNDS - 1)
            seq.done(nc.vector.tensor_tensor(tb[:, CNT, :], tb[:, CNT, :], banks[0][:, 0:NT], ALU.add))
            nc.vector.tensor_scalar(lonely[:, :], tb[:, CNT, :], 0.0, None, ALU.is_equal).then_inc(counts, 1)
            seq.done(nc.vector.tensor_scalar(tb[:, DEG, :], tb[:, CNT, :], 1.0, None, ALU.add))
            nc.vector.reciprocal(tb[:, REC, :], tb[:, DEG, :]).then_inc(deg_ready, 1)

            dve.wait_ge(totals, 1)
            seq.done(nc.vector.tensor_copy(tb[:, TOT, :], banks[0][:, 0:NT]))
            seq.done(nc.vector.tensor_tensor_scan(tb[:, INC, :], ones[:, 0:NT], tb[:, TOT, :], 0.0, ALU.mult, ALU.add))
            seq.done(nc.vector.tensor_tensor(tb[:, BEG, :], tb[:, INC, :], tb[:, TOT, :], ALU.subtract))
            seq.done(nc.vector.tensor_scalar(tile_i[:, 3, :], tb[:, TOT, :], float(P - 1), None, ALU.add))
            seq.done(nc.vector.tensor_scalar(tile_i[:, 2, :], tile_i[:, 3, :], 7, None, ALU.logical_shift_right))
            seq.done(nc.vector.tensor_copy(tb[:, NUM, :], tile_i[:, 2, :]))
            seq.done(nc.vector.tensor_tensor_scan(tb[:, SIN, :], ones[:, 0:NT], tb[:, NUM, :], 0.0, ALU.mult, ALU.add))
            seq.done(nc.vector.tensor_tensor(tb[:, STA, :], tb[:, SIN, :], tb[:, NUM, :], ALU.subtract))
            seq.done(nc.vector.scalar_tensor_tensor(out=tb[:, CCC, :], in0=tb[:, STA, :], scalar=-float(P),
                                                    in1=tb[:, BEG, :], op0=ALU.mult, op1=ALU.add))
            seq.done(nc.vector.tensor_copy(tb[:, DLT, 0:1], tb[:, CCC, 0:1]))
            seq.done(nc.vector.tensor_tensor(tb[:, DLT, 1:NT], tb[:, CCC, 1:NT], tb[:, CCC, 0:NT - 1], ALU.subtract))
            seq.done(nc.vector.tensor_copy(tile_i[:, 1, :], tb[:, STA, :]))
            seq.done(nc.vector.tensor_copy(tile_i[:, 2, :], tb[:, BEG, :]))
            seq.done(nc.vector.tensor_scalar(tile_i[:, 3, :], tile_i[:, 2, :], P - 1, None, ALU.bitwise_and))
            seq.done(nc.vector.tensor_copy(tb[:, RMD, :], tile_i[:, 3, :]))
            nc.vector.tensor_scalar(tile_i[:, 0, :], tile_i[:, 2, :], 7, None, ALU.logical_shift_right).then_inc(tiles_known, 1)

            seq.done(nc.vector.tensor_copy(step_f[:, 0, :], step_i[:, :]))
            seq.done(nc.vector.tensor_tensor(indic[:, 0, :, :], step_f[:, 0, :].unsqueeze(2).broadcast_to([ROWS, QS, NT]),
                                             tb[0:ROWS, STA, :].unsqueeze(1).broadcast_to([ROWS, QS, NT]), ALU.is_ge))
            seq.done(nc.vector.tensor_tensor(indic[:, 1, :, :], indic[:, 0, :, :],
                                             tb[0:ROWS, DLT, :].unsqueeze(1).broadcast_to([ROWS, QS, NT]), ALU.mult))
            seq.done(nc.vector.reduce_sum(step_f[:, 1, :], indic[:, 0, :, :], X_AXIS))
            seq.done(nc.vector.reduce_sum(step_f[:, 2, :], indic[:, 1, :, :], X_AXIS))
            seq.done(nc.vector.tensor_scalar(step_out[:, 0, :], step_f[:, 1, :], -1.0, None, ALU.add))
            seq.done(nc.vector.scalar_tensor_tensor(out=step_f[:, 3, :], in0=step_f[:, 0, :], scalar=float(P),
                                                    in1=step_f[:, 2, :], op0=ALU.mult, op1=ALU.add))
            nc.vector.tensor_scalar(step_out[:, 1, :], step_f[:, 3, :], float(E), None, ALU.min).then_inc(steps_known, 1)

            def shift_build(it, k):
                for a in range(2):
                    nc.vector.tensor_scalar(shift[:, k, a, :], diff[:, :], tb[:, RMD, bass.ds(2 * it + k, 1)], float(a * P),
                                            ALU.add, ALU.is_equal).then_inc(shift_ready, 1)

            dve.wait_ge(dinv_ready, 1)
            dve.wait_ge(*n0.at("row", NT))
            with dve.Fori(0, PAIRS) as it:
                for k in range(2):
                    t = 2 * it + k
                    nc.vector.tensor_scalar(acc[:, bass.ds(t, 1), 0:D], acc[:, bass.ds(t, 1), 0:D], dinv[:, bass.ds(t, 1)],
                                            None, ALU.mult).then_inc(n0("out"), 1)
            for k in range(2):
                shift_build(0, k)

            def shift_pair(it, first_pair, last_pair):
                s = nc.values_load_multi_w_load_instructions(
                    tile_i[0:1, 1, bass.ds(2 * it, 2)], engines=[mybir.EngineType.DVE], min_val=0, max_val=STEPS,
                    skip_runtime_bounds_check_because="a tile's first step is one of the steps, or their end")[1]
                for k in range(2):
                    t = 2 * it + k
                    dve.wait_ge(shifted, 2 * t + 2)
                    if not (first_pair and k == 0):
                        dve.wait_ge(slots_copied, t)
                    nc.vector.tensor_copy(slots[:, bass.ds(s[k], ECOLS)], banks[6 + k][:, 0:ECOLS]).then_inc(slots_copied, 1)
                    if not last_pair:
                        shift_build(it + 1, k)
            rounds(dve, shift_pair, PAIRS)
            dve.wait_ge(slots_copied, NT)

            dve.wait_ge(steps_in, 32)
            seq.done(nc.vector.tensor_copy(slot_i[:, :], slots[:, 0:STEPS]))
            seq.done(nc.vector.tensor_scalar(srcI[:, :], slot_i[:, :], CODE - 1, None, ALU.bitwise_and))
            seq.done(nc.vector.tensor_scalar(slot_i[:, :], slot_i[:, :], 12, None, ALU.logical_shift_right))
            seq.done(nc.vector.tensor_copy(tmp_a, slot_i[:, :]))
            seq.done(nc.vector.tensor_copy(tmp_b, jB[:, :]))
            seq.done(nc.vector.scalar_tensor_tensor(out=dloc[:, :], in0=tmp_b, scalar=-float(P), in1=tmp_a,
                                                    op0=ALU.mult, op1=ALU.add))
            seq.done(nc.vector.scalar_tensor_tensor(out=tmp_a, in0=tmp_b, scalar=float(CODE), in1=tmp_a,
                                                    op0=ALU.mult, op1=ALU.add))
            seq.done(nc.vector.memset(first[:, 0:1], 0.0))
            dve.sem_inc(slots_ready, 1)
            dve.sem_inc(seg_ready, 1)

            dve.wait_ge(prep("w_in"), 16 * 7)
            for w, heads, v in ((w_c, 1, 0), (w_heads, HEADS, 2)):
                for i in range(2):
                    for c in range(2):
                        seq.done(nc.vector.tensor_tensor(att_tmp, w[:, c, 0:D], att_vec[:, v + i, :], ALU.mult))
                        last = nc.vector.reduce_sum(w[:, c, D + i * heads:D + (i + 1) * heads],
                                                    att_tmp.rearrange("p (h c) -> p h c", h=heads), X_AXIS)
                        seq.done(last)
                dve.sem_inc(prep("w_ready"), 1)
            for i in range(3):
                seq.done(nc.vector.tensor_copy(part_gate[:, i, :], row_gate[:, i, :]))
                if i < 2:
                    seq.done(nc.vector.tensor_tensor(row_gate[:, i + 1, :], row_gate[:, i, :], part_gate[:, i, :], ALU.subtract))
            dve.sem_inc(prep("gate_parts"), 1)

            dve.wait_ge(seg_T, QS)
            nc.vector.tensor_copy(seg_rows, banks[0][0:ROWS, :].rearrange("p (q e) -> p q e", q=QS)).then_inc(seg_rows_ready, 1)
            dve.wait_ge(seg_rows_ready, 1)
            dve.wait_ge(seg_back, 16)
            seq.done(nc.vector.tensor_tensor(prev_rows, prev_rows, seg_rows, ALU.is_equal))
            seq.done(nc.vector.tensor_scalar(seg_rows, prev_rows, -1.0, 1.0, ALU.mult, ALU.add))
            nc.vector.tensor_scalar(prev_rows, seg_rows, -BIG, None, ALU.mult).then_inc(reset_ready, 1)
            dve.wait_ge(first_T, QS)
            nc.vector.tensor_copy(first[:, :], banks[1][:, 0:STEPS]).then_inc(first_ready, 1)

            def make_onehot(it, k, ph):
                nc.vector.tensor_scalar(onehot[:, k, :], iota_row[:, :], dloc[:, bass.ds(ROUND * it + k, 1)], None,
                                        ALU.is_equal).then_inc(ph("onehot"), 1)

            def tiles_of(step0, count):
                return step_values(mybir.EngineType.DVE, 0, step0, count, NT - 1)

            def add_step(ph, step, k, reg, width, very_first, sums_in=(4, 5)):
                dve.wait_ge(*ph.at("mm", step + 1))
                if not very_first:
                    dve.wait_ge(*ph.at("added", step))
                nc.vector.tensor_tensor(acc[:, bass.ds(reg, 1), 0:width], acc[:, bass.ds(reg, 1), 0:width],
                                        banks[sums_in[k % len(sums_in)]][:, 0:width].unsqueeze(1),
                                        ALU.add).then_inc(ph("added"), 1)

            for k in range(ROUND):
                make_onehot(0, k, g0)

            def gcn_round(it, first_round, last_round):
                regs = tiles_of(ROUND * it, ROUND)
                for k in range(ROUND):
                    add_step(g0, ROUND * it + k, k, regs[k], D, first_round and k == 0)
                    if not last_round:
                        make_onehot(it + 1, k, g0)
            rounds(dve, gcn_round, ROUNDS)
            dve.wait_ge(*g0.at("added", STEPS))

            def score_columns(ph, heads, t, k):
                dve.wait_ge(*ph.at("row", t + 1))
                nc.vector.tensor_copy(nd[:, bass.ds(t, 1), 0:2 * heads],
                                      banks[4 + k][:, D:D + 2 * heads].unsqueeze(1)).then_inc(ph("nd"), 1)

            dve.wait_ge(prep("rest_in"), REST)

            def n1_row(t, k, reused):
                if reused:
                    dve.wait_ge(*n1.at("tr", 2 * t - 2))
                nc.vector.scalar_tensor_tensor(out=rows[:, k:k + 1, :], in0=acc[:, bass.ds(t, 1), 0:D],
                                               scalar=dinv[:, bass.ds(t, 1)], in1=b_gcn[:, :].unsqueeze(1),
                                               op0=ALU.mult, op1=ALU.add).then_inc(n1("agg"), 1)
            for k in range(2):
                n1_row(k, k, False)

            def n1_tile(t, k, first_pair, last_pair):
                if not last_pair:
                    n1_row(t + 2, k, True)
                score_columns(n1, 1, t, k)
            tile_rounds(dve, n1_tile)
            dve.wait_ge(*n1.at("agg", NT))
            dve.wait_ge(*n1.at("nd", NT))
            dve.wait_ge(acc_cleared, 1)

            def attention_phase(ph, heads):
                w = 2 * heads
                n = heads * GROUP
                ade = att[:, 0:16 * GROUP].rearrange("p (k c) -> p k c", k=GROUP)
                asd, add_ = ade[:, :, 0:heads], ade[:, :, heads:w]
                top = att[:, 128:128 + n].rearrange("p (k h) -> p k h", k=GROUP)
                z = att[:, 192:192 + 3 * n].rearrange("p (a k h) -> p a k h", a=3, k=GROUP)
                zf = att[:, 192:192 + 3 * n]
                expo = att[:, 384:384 + 2 * n].rearrange("p (a k h) -> p a k h", a=2, k=GROUP)
                ex1 = att[:, 512:512 + n].rearrange("p (k h) -> p k h", k=GROUP)
                rr = att[:, 616:616 + heads]
                ps_max = banks[7][:, 0:16 * GROUP].rearrange("p (k c) -> p k c", k=GROUP)[:, :, 0:heads]

                def onehot_of(g, b, k):
                    nc.vector.tensor_scalar(onehot_b[b][:, k, :], iota_row[:, :],
                                            dloc[:, bass.ds(GROUP * g + k, 1)], None, ALU.is_equal).then_inc(ph("onehot"), 1)

                def scans(turn_of, g, b, reused, between=None):
                    b = b % 2
                    dve.wait_ge(*ph.at(f"reset{b}", 16 * (turn_of + 1)))
                    dve.wait_ge(*ph.at("as_tr", GROUP * (g + 1)))
                    if reused:
                        dve.wait_ge(*ph.at("max_tr", (GROUP + 1) * g))
                        dve.wait_ge(*ph.at("scan", 2 * g))
                    nc.vector.tensor_tensor_scan(fwd_b[b][0:heads, :], reset_b[b][0:heads, 0:SG],
                                                 PS[0:heads, 2:4, :].rearrange("p a e -> p (a e)"),
                                                 fwd_b[1 - b][0:heads, SG - 1:SG], ALU.add, ALU.max).then_inc(ph("scan"), 1)
                    if between is not None:
                        between()
                    dve.wait_ge(*ph.at("scan", 2 * g + 1))
                    nc.vector.tensor_tensor_scan(both[0:heads, ::-1], reset_b[b][0:heads, SG:0:-1],
                                                 fwd_b[b][0:heads, ::-1], LOW, ALU.add, ALU.max).then_inc(ph("scan"), 1)

                def adds(g, b, regs, first_group, last_groups):
                    for k in range(GROUP):
                        add_step(ph, GROUP * g + k, k, regs[k], D + w, first_group and k == 0, SUM_BANKS)
                        if heads == 1 and not last_groups:
                            onehot_of(g + 2, (b + 2) % LIVE, k)
                        if heads > 1 and k + 4 < GROUP:
                            scale(b, k + 4)

                def exponents(g, b):
                    dve.wait_ge(*ph.at("max_tr", (GROUP + 1) * (g + 1)))
                    dve.wait_ge(*ph.at("ad_copy", g + 1))
                    a0 = att[0:1, 576:576 + heads]
                    a1 = att[0:1, 584:584 + heads]
                    a2 = att[0:1, 592:592 + heads]
                    seq.start(nc.vector.tensor_tensor(z[:, 0, :, :], G_b[b][:, :, D:D + heads], add_, ALU.add))
                    seq.start(nc.vector.tensor_tensor(z[:, 1, :, :], asd, add_, ALU.add))
                    seq.start(nc.vector.tensor_tensor(top, ps_max, asd, ALU.max))
                    seq.done(nc.vector.tensor_tensor(a0, banks[7][0:1, 128:128 + heads], asd[0:1, 0, :], ALU.max))
                    seq.start(nc.vector.tensor_tensor(z[:, 2, :, :], top, add_, ALU.add))
                    seq.done(nc.vector.tensor_tensor(a0, a0, add_[0:1, 0, :], ALU.add))
                    seq.start(nc.vector.scalar_tensor_tensor(out=zf, in0=zf, scalar=SLOPE, in1=zf, op0=ALU.mult, op1=ALU.max))
                    seq.done(nc.vector.scalar_tensor_tensor(out=a1, in0=a0, scalar=SLOPE, in1=a0, op0=ALU.mult, op1=ALU.max))
                    nc.vector.tensor_tensor(expo, z[:, 0:2, :, :], z[:, 2:3, :, :].broadcast_to([P, 2, GROUP, heads]),
                                            ALU.subtract).then_inc(ph("small"), 1)
                    seq.done(nc.vector.tensor_tensor(a1, a1, z[0:1, 2, 0, :], ALU.subtract))
                    nc.vector.tensor_scalar(a2, a1, 0.0, None, ALU.min).then_inc(ph("rho_in"), 1)

                def scale(b, k):
                    rh = G_b[b][:, k, 0:D].rearrange("p (h c) -> p h c", h=heads)
                    nc.vector.tensor_tensor(rh, rh, G_b[b][:, k, D:D + heads].unsqueeze(2)
                                            .broadcast_to([P, heads, D // heads]), ALU.mult).then_inc(ph("scaled"), 1)

                def scales(g, b):
                    dve.wait_ge(*ph.at("ex", 2 * (g + 1)))
                    own = nc.vector.tensor_tensor(G_b[b][:, :, D + heads:D + w], ex1,
                                                  first[:, bass.ds(GROUP * g, GROUP)].unsqueeze(2)
                                                  .broadcast_to([P, GROUP, heads]), ALU.mult)
                    if heads == 1:
                        own.then_inc(ph("own_col"), 1)
                        return
                    for k in range(4):
                        scale(b, k)

                def rho(g):
                    dve.wait_ge(*ph.at("rho_ex", g + 1))
                    nc.vector.tensor_scalar(att[0:1, 608:608 + heads], att[0:1, 600:600 + heads], -1.0, None,
                                            ALU.add).then_inc(ph("rho"), 1)

                def rescale(g, reg, first_group):
                    if not first_group:
                        dve.wait_ge(*ph.at("added", GROUP * g))
                    dve.wait_ge(*ph.at("rho_mm", g + 1))
                    nc.vector.tensor_scalar(rr, banks[7][:, 160:160 + heads], 1.0, None, ALU.add).then_inc(ph("rescale"), 1)
                    dve.wait_ge(*ph.at("rescale", g + 1))
                    av = acc[:, bass.ds(reg, 1), 0:D].rearrange("p a (h c) -> p (a h) c", h=heads)
                    seq.start(nc.vector.tensor_tensor(av, av, rr.unsqueeze(2).broadcast_to([P, heads, D // heads]), ALU.mult))
                    aw = acc[:, bass.ds(reg, 1), D:D + w].rearrange("p a (v h) -> p (a v) h", v=2)
                    seq.done(nc.vector.tensor_tensor(aw, aw, rr.unsqueeze(1).broadcast_to([P, 2, heads]), ALU.mult))

                seq.done(nc.vector.memset(fwd_b[1][0:heads, SG - 1:SG], LOW))
                scans(0, 0, 0, False)
                for g in range(2 if heads == 1 else 0):
                    for k in range(GROUP):
                        onehot_of(g, g, k)

                def turn(it, first_turn, last_turn):
                    for b in range(LIVE):
                        g = LIVE * it + b
                        first_group = first_turn and b == 0
                        exponents(g, b)
                        if not (last_turn and b == LIVE - 1):
                            scans(2 * it + (b + 1) // 2, g + 1, b + 1, True, lambda: rho(g))
                        else:
                            rho(g)
                        regs = tiles_of(GROUP * g, GROUP)
                        if heads == 1:
                            scales(g, b)
                        rescale(g, regs[0], first_group)
                        if heads > 1:
                            scales(g, b)
                        adds(g, b, regs, first_group, last_turn and b >= LIVE - 2)
                turn(0, True, False)
                with seq.loop(1, TURNS - 1, LIVE * (9 + 2)) as it:
                    turn(it, False, False)
                turn(TURNS - 1, False, True)
                dve.wait_ge(*ph.at("added", STEPS))

            def attention_shares(heads):
                ws, dn = w_self[:, :, 0:heads], den[:, :, 0:heads]
                seq.done(nc.vector.tensor_tensor(ws, acc[:, :, D + heads:D + 2 * heads],
                                                 lonely[:, :].unsqueeze(2).broadcast_to([P, NT, heads]), ALU.add))
                seq.done(nc.vector.scalar_tensor_tensor(out=dn, in0=acc[:, :, D:D + heads], scalar=1e-16, in1=ws,
                                                        op0=ALU.add, op1=ALU.add))
                seq.done(nc.vector.reciprocal(dn, dn))
                seq.done(nc.vector.tensor_tensor(ws, ws, dn, ALU.mult))

            def attention_end(heads):
                attention_shares(heads)
                num = acc[:, :, 0:D].rearrange("p t (h c) -> p t h c", h=heads)
                own = H[:, :, 0:D].rearrange("p t (h c) -> p t h c", h=heads)
                wide = [P, NT, heads, D // heads]
                seq.start(nc.vector.tensor_tensor(num, num, den[:, :, 0:heads].unsqueeze(3).broadcast_to(wide), ALU.mult))
                seq.done(nc.vector.tensor_tensor(own, own, w_self[:, :, 0:heads].unsqueeze(3).broadcast_to(wide), ALU.mult))
                seq.done(nc.vector.tensor_tensor(num, num, own, ALU.add))

            def on_tiles(row):
                return row[:, :].unsqueeze(1).broadcast_to([P, NT, D])

            attention_phase(g1, 1)

            attention_shares(1)
            dve.sem_inc(n2("shares"), 1)

            def received(t):
                dve.wait_ge(*n2.at("own_biased", t + 1))
                nc.vector.scalar_tensor_tensor(out=acc[:, bass.ds(t, 1), 0:D], in0=acc[:, bass.ds(t, 1), 0:D],
                                               scalar=den[:, bass.ds(t, 1), 0:1].rearrange("p a c -> p (a c)"),
                                               in1=H[:, bass.ds(t, 1), 0:D],
                                               op0=ALU.mult, op1=ALU.add).then_inc(n2("received"), 1)

            def into_x(t):
                dve.wait_ge(*n2.at("received", t + 1))
                nc.vector.scalar_tensor_tensor(out=X[:, bass.ds(t, 1), :], in0=acc[:, bass.ds(t, 1), 0:D], scalar=0.0,
                                               in1=X[:, bass.ds(t, 1), :], op0=ALU.max, op1=ALU.add).then_inc(n2("x"), 1)

            def stats_of_x(t):
                dve.wait_ge(*n2.at("x", t + 1))
                nc.vector.bn_stats(stats[:, bass.ds(t, 1), :].rearrange("p a c -> p (a c)"),
                                   X[:, bass.ds(t, 1), :].rearrange("p a c -> p (a c)")).then_inc(n2("x_stats"), 1)

            def n2_tile(t, k, first_pair, last_pair):
                received(t)
                if not (first_pair and k == 0):
                    into_x(t - 1)
                if not first_pair:
                    stats_of_x(t - 2)
            tile_rounds(dve, n2_tile)
            into_x(NT - 1)
            for t in (NT - 2, NT - 1):
                stats_of_x(t)
            dve.wait_ge(*n2.at("x_stats", NT))
            norm_scales(seq, n2)

            def n2_pair(it, first_pair, last_pair):
                for k in range(2):
                    t = 2 * it + k
                    dve.wait_ge(*n2.at("h", t + 1))
                    nc.vector.tensor_scalar(H[:, bass.ds(t, 1), 0:D], rows[:, k:k + 1, :], 0.5, None, ALU.mult).then_inc(n2("half"), 1)
                    nc.vector.tensor_tensor(X[:, bass.ds(t, 1), :], X[:, bass.ds(t, 1), :], rows[:, k:k + 1, :],
                                            ALU.add).then_inc(n2("xrow"), 1)
            rounds(dve, n2_pair, PAIRS)
            dve.wait_ge(*n2.at("xrow", NT))
            dve.wait_ge(acc_cleared, 2)

            def four_onehots(ph, j, q):
                for k in range(4):
                    kk = (4 * q + k) % ROUND
                    nc.vector.tensor_scalar(onehot[:, kk, :], iota_row[:, :], dloc[:, bass.ds(4 * j + k, 1)], None,
                                            ALU.is_equal).then_inc(ph("onehot"), 1)

            def four_adds(ph, j, back, regs, very_first):
                for k in range(4):
                    add_step(ph, 4 * j + k, k, regs[k], D, very_first and k == 0)

            four_onehots(g2, 0, 0)
            four_onehots(g2, 1, 1)

            def gate_round(it, first_round, last_round):
                for q in range(4):
                    j = 4 * it + q
                    if not (last_round and q >= 2):
                        four_onehots(g2, j + 2, q + 2)
                    dve.wait_ge(*g2.at(f"rows{q}", 64 * (it + 1)))
                    if not (first_round and q == 0):
                        regs = tiles_of(4 * j - 4, 4)
                    for k in range(4):
                        dve.wait_ge(gate("gate"), 4 * j + k + 1)
                        r = G[:, 4 * q + k, 0:D]
                        nc.vector.scalar_tensor_tensor(out=r, in0=gates[q % 2][:, k, :], scalar=1.0, in1=r,
                                                       op0=ALU.add, op1=ALU.mult).then_inc(gate("gated"), 1)
                        if not (first_round and q == 0):
                            add_step(g2, 4 * j - 4 + k, k, regs[k], D, first_round and q == 1 and k == 0)
            rounds(dve, gate_round, ROUNDS)
            four_adds(g2, STEPS // 4 - 1, 0, tiles_of(STEPS - 4, 4), False)
            dve.wait_ge(*g2.at("added", STEPS))

            def n3_copy(it, first_pair):
                if not first_pair:
                    dve.wait_ge(*n3.at("tr", 4 * it))
                nc.vector.tensor_copy(rows[:, :, :], acc[:, bass.ds(2 * it, 2), 0:D]).then_inc(n3("agg"), 1)
            dve.wait_ge(bias_added, NT)
            n3_copy(0, True)

            def n3_pair(it, first_pair, last_pair):
                if not last_pair:
                    n3_copy(it + 1, False)
                for k in range(2):
                    t = 2 * it + k
                    dve.wait_ge(*n3.at("mm", 4 * it + 2 * k + 2))
                    nc.vector.tensor_tensor(X[:, bass.ds(t, 1), :], X[:, bass.ds(t, 1), :],
                                            banks[4 + k][:, 0:D].unsqueeze(1), ALU.add).then_inc(n3("out"), 1)
            rounds(dve, n3_pair, PAIRS)
            dve.wait_ge(*n3.at("out", NT))
            norm_stats(seq, X, n3b)

            def n3b_tile(t, k, first_pair, last_pair):
                dve.wait_ge(*n3b.at("ht", t + 1))
                nc.vector.tensor_copy(HT[:, bass.ds(t, 1), :, :].rearrange("p a b c -> p (a b c)"),
                                      HTs[:, k, :, :].rearrange("p b c -> p (b c)")).then_inc(n3b("kept"), 1)
                dve.wait_ge(*n3b.at("row", t + 1))
                nc.vector.tensor_tensor(Q[:, bass.ds(t * D, D)], banks[4 + k][:, D:2 * D], b_msg[:, :],
                                        ALU.add).then_inc(n3b("out"), 1)
            tile_rounds(dve, n3b_tile)
            dve.wait_ge(*n3b.at("out", NT))
            dve.wait_ge(*n3b.at("kept", NT))
            dve.wait_ge(acc_cleared, 3)

            four_onehots(g3, 0, 0)
            four_onehots(g3, 1, 1)

            def msg_round(it, first_round, last_round):
                for q in range(4):
                    j = 4 * it + q
                    if not (last_round and q >= 2):
                        four_onehots(g3, j + 2, q + 2)
                    dve.wait_ge(*g3.at(f"rows{q}", 64 * (it + 1)))
                    for k in (0, 2):
                        dve.wait_ge(*g3.at("qmm", 4 * j + k + 2))
                        r = G[:, 4 * q + k:4 * q + k + 2, 0:D]
                        nc.vector.tensor_tensor(r, r, banks[k // 2].rearrange("p (k d) -> p k d", k=2),
                                                ALU.add).then_inc(g3("sum"), 1)
                    if not (first_round and q == 0):
                        regs = tiles_of(4 * j - 4, 4)
                        four_adds(g3, j - 1, 0, regs, first_round and q == 1)
            rounds(dve, msg_round, ROUNDS)
            four_adds(g3, STEPS // 4 - 1, 0, tiles_of(STEPS - 4, 4), False)
            dve.wait_ge(*g3.at("added", STEPS))

            dve.wait_ge(bias_added, 2 * NT)
            dve.wait_ge(*g3.at("mm", STEPS))

            def n4_copy(t, k, reused):
                if reused:
                    dve.wait_ge(*n4.at("tr", 2 * t - 2))
                nc.vector.tensor_copy(G[:, k:k + 1, 0:D], acc[:, bass.ds(t, 1), 0:D]).then_inc(n4("agg"), 1)
            for k in range(2):
                n4_copy(k, k, False)

            def n4_tile(t, k, first_pair, last_pair):
                if not last_pair:
                    n4_copy(t + 2, k, True)
                dve.wait_ge(*n4.at("row", t + 1))
                nc.vector.bn_stats(stats[:, bass.ds(t, 1), :].rearrange("p a c -> p (a c)"),
                                   H[:, bass.ds(t, 1), 0:D].rearrange("p a c -> p (a c)")).then_inc(n4("stats"), 1)
            tile_rounds(dve, n4_tile)
            dve.wait_ge(*n4.at("stats", NT))
            norm_scales(seq, n4)

            def scaled_add(ph, t_in, stats_too):
                def stats_of(t):
                    dve.wait_ge(*ph.at("xrow", t + 1))
                    nc.vector.bn_stats(stats[:, bass.ds(t, 1), :].rearrange("p a c -> p (a c)"),
                                       X[:, bass.ds(t, 1), :].rearrange("p a c -> p (a c)")).then_inc(ph("xstats"), 1)

                def tile(t, k, first_pair, last_pair):
                    dve.wait_ge(*ph.at("gamma", t + 1))
                    nc.vector.tensor_tensor(X[:, bass.ds(t, 1), :], X[:, bass.ds(t, 1), :],
                                            t_in[:, bass.ds(t, 1), 0:D], ALU.add).then_inc(ph("xrow"), 1)
                    if stats_too and not (first_pair and k == 0):
                        stats_of(t - 1)
                tile_rounds(dve, tile)
                if stats_too:
                    stats_of(NT - 1)
                    dve.wait_ge(*ph.at("xstats", NT))
            scaled_add(n4, H, True)
            norm_scales(seq, n4b)

            tile_rounds(dve, lambda t, k, first_pair, last_pair: score_columns(n4b, HEADS, t, k))
            dve.wait_ge(*n4b.at("nd", NT))
            dve.wait_ge(acc_cleared, 4)
            attention_phase(g4, HEADS)
            attention_end(HEADS)
            seq.done(nc.vector.tensor_tensor(acc[:, :, 0:D], acc[:, :, 0:D], on_tiles(b_heads), ALU.add))
            norm_stats(seq, acc, n5)
            dve.wait_ge(bias_added, 3 * NT)
            scaled_add(n5, acc, False)


_INS = ['x', 'src', 'dst', 'edge_attr_64', 'L0_gnn_W1', 'L0_gnn_b1', 'L0_gnn_W2', 'L0_gnn_att_src', 'L0_gnn_att_dst',
        'L0_gnn_b2', 'L1_gnn_W1', 'L1_gnn_b1', 'L1_gnn_W2', 'L1_gnn_b2', 'L1_gnn_U1', 'L1_gnn_c1', 'L1_gnn_U2',
        'L1_gnn_c2', 'L2_gnn_W_msg', 'L2_gnn_b_msg', 'L2_gnn_W_upd', 'L2_gnn_b_upd', 'L2_gnn_gamma', 'L2_gnn_beta',
        'L3_gnn_W', 'L3_gnn_att_src', 'L3_gnn_att_dst', 'L3_gnn_bias', 'L3_gnn_ln_gamma', 'L3_gnn_ln_beta']


def kernel(**inputs):
    import numpy as _np
    import concourse.bacc as _bacc
    from concourse import mybir as _mybir
    from concourse.bass_utils import run_bass_kernel_spmd as _run

    nc = _bacc.Bacc("TRN2", target_bir_lowering=False, num_devices=1)
    arrays, args = {}, []
    for name in _INS:
        a = _np.ascontiguousarray(inputs[name])
        arrays[f"in_{name}"] = a
        args.append(nc.dram_tensor(f"in_{name}", a.shape, _mybir.dt.from_np(a.dtype), kind="ExternalInput").ap())
    args.append(nc.dram_tensor("out_x", (N, D), _mybir.dt.float32, kind="ExternalOutput").ap())
    gnn_four_layers(nc, *args)
    r = _run(nc, [arrays], core_ids=[0])
    return r.results[0]["out_x"]
```
